# Optimizing a Trainium2 kernel written in Bass

```python
import numpy as np
import jax
import jax.numpy as jnp

def _softmax(x, axis=-1):
    return jax.nn.softmax(x, axis=axis)

def _gelu(x):
    return jax.nn.gelu(x, approximate=True)

def _silu(x):
    return jax.nn.silu(x)

def _sigmoid(x):
    return jax.nn.sigmoid(x)

def _layernorm(x, axis=-1, eps=1e-05):
    m = jnp.mean(x, axis=axis, keepdims=True)
    v = jnp.var(x, axis=axis, keepdims=True)
    return (x - m) / jnp.sqrt(v + eps)

def _scatter_add(tgt, idx, src, axis=0):
    return tgt.at[idx].add(src)

def _segment_sum(src, seg, n):
    return jax.ops.segment_sum(src, seg, n)
kernel_name = 'mk_seq_preln_d1_jaxref_r4_f5af25'

def setup_inputs(seed: int=0):
    np.random.seed(seed)
    _w = jnp.asarray

    def _L0_attn_setup():
        import jax, jax.numpy as jnp
        import numpy as np
        H = 16
        DH = 64
        M = 64
        ITERS = 6
        K = 13

        def moore_penrose_inverse(a, iters=ITERS):
            a_abs = jnp.abs(a)
            col = a_abs.sum(axis=-1)
            row = a_abs.sum(axis=-2)
            z = jnp.swapaxes(a, -1, -2) / (jnp.max(col) * jnp.max(row))
            I = jnp.eye(a.shape[-1], dtype=a.dtype)
            for _ in range(iters):
                az = a @ z
                z = 0.25 * z @ (13 * I - az @ (15 * I - az @ (7 * I - az)))
            return z
        key = jax.random.key(seed)
        k1, k2, k3, k4 = jax.random.split(key, 4)
        b, n, dim = (4, 1024, 256)
        inner = H * DH
        x = jax.random.normal(k1, (b, n, dim), dtype=jnp.float32)
        w_qkv = jax.random.normal(k2, (dim, 3 * inner), dtype=jnp.float32) * 0.02
        w_conv = jax.random.normal(k3, (H, 1, K, 1), dtype=jnp.float32) * 0.1
        w_fc = jax.random.normal(k4, (inner, dim), dtype=jnp.float32) * 0.02
        b_fc = jnp.zeros((dim,), dtype=jnp.float32)
        return {'x': x, 'w_qkv': w_qkv, 'w_conv': w_conv, 'w_fc': w_fc, 'b_fc': b_fc}
    _L0_attn_in = _L0_attn_setup()

    def _L0_ffn_setup():
        import jax, jax.numpy as jnp
        import numpy as np
        JITTER_EPS = 0.01
        NEG_INF = -jnp.inf

        def sparsemixer_eval(scores, jitter_eps):
            m1 = jnp.max(scores, axis=-1, keepdims=True)
            ind1 = jnp.argmax(scores, axis=-1)
            factor1 = jnp.maximum(jnp.abs(scores), m1)
            mask1 = jax.lax.stop_gradient((m1 - scores) / factor1 > 2.0 * jitter_eps)
            gates1 = jax.nn.softmax(jnp.where(mask1, NEG_INF, scores), axis=-1)
            mult1 = jnp.take_along_axis(gates1, ind1[:, None], axis=-1)[:, 0]
            E = scores.shape[-1]
            onehot1 = ind1[:, None] == jnp.arange(E)[None, :]
            masked_scores = jnp.where(onehot1, NEG_INF, scores)
            m2 = jnp.max(masked_scores, axis=-1, keepdims=True)
            ind2 = jnp.argmax(masked_scores, axis=-1)
            factor2 = jnp.maximum(jnp.abs(scores), m2)
            mask2 = jax.lax.stop_gradient((m2 - scores) / factor2 > 2.0 * jitter_eps)
            gates2 = jax.nn.softmax(jnp.where(mask2, NEG_INF, masked_scores), axis=-1)
            mult2 = jnp.take_along_axis(gates2, ind2[:, None], axis=-1)[:, 0]
            multiplier = jnp.stack([mult1, mult2], axis=-1)
            selected = jnp.stack([ind1, ind2], axis=-1)
            return (multiplier, selected)
        key = jax.random.key(seed)
        k0, k1, k2, k3, k4 = jax.random.split(key, 5)
        B, S, H, F, E = (2, 256, 256, 512, 8)
        scale = 0.02
        return {'hidden_states': jax.random.normal(k0, (B, S, H), dtype=jnp.float32), 'router_w': jax.random.normal(k1, (E, H), dtype=jnp.float32) * scale, 'w_gate': jax.random.normal(k2, (E, F, H), dtype=jnp.float32) * scale, 'w_up': jax.random.normal(k3, (E, F, H), dtype=jnp.float32) * scale, 'w_down': jax.random.normal(k4, (E, H, F), dtype=jnp.float32) * scale}
    _L0_ffn_in = _L0_ffn_setup()
    _d = {'L0_attn_x': _L0_attn_in['x'], 'L0_attn_w_qkv': _L0_attn_in['w_qkv'], 'L0_attn_w_conv': _L0_attn_in['w_conv'], 'L0_attn_w_fc': _L0_attn_in['w_fc'], 'L0_attn_b_fc': _L0_attn_in['b_fc'], 'L0_ffn_router_w': _L0_ffn_in['router_w'], 'L0_ffn_w_gate': _L0_ffn_in['w_gate'], 'L0_ffn_w_up': _L0_ffn_in['w_up'], 'L0_ffn_w_down': _L0_ffn_in['w_down']}
    _x0 = _d['L0_attn_x']
    _d['L0_attn_x'] = jax.random.normal(jax.random.fold_in(jax.random.key(seed), 1), (4, 1024, 256), dtype=_x0.dtype)
    del _x0
    return _d

def reference(L0_attn_x, L0_attn_w_qkv, L0_attn_w_conv, L0_attn_w_fc, L0_attn_b_fc, L0_ffn_router_w, L0_ffn_w_gate, L0_ffn_w_up, L0_ffn_w_down):

    def _L0_attn_ref(x, w_qkv, w_conv, w_fc, b_fc):
        import jax, jax.numpy as jnp
        import numpy as np
        H = 16
        DH = 64
        M = 64
        ITERS = 6
        K = 13

        def moore_penrose_inverse(a, iters=ITERS):
            a_abs = jnp.abs(a)
            col = a_abs.sum(axis=-1)
            row = a_abs.sum(axis=-2)
            z = jnp.swapaxes(a, -1, -2) / (jnp.max(col) * jnp.max(row))
            I = jnp.eye(a.shape[-1], dtype=a.dtype)
            for _ in range(iters):
                az = a @ z
                z = 0.25 * z @ (13 * I - az @ (15 * I - az @ (7 * I - az)))
            return z
        b, n, dim = x.shape
        scale = DH ** (-0.5)
        qkv = x @ w_qkv
        q, k, v = jnp.split(qkv, 3, axis=-1)
        split_heads = lambda t: t.reshape(b, n, H, DH).transpose(0, 2, 1, 3)
        q, k, v = (split_heads(q) * scale, split_heads(k), split_heads(v))
        l = n // M
        q_l = q.reshape(b, H, M, l, DH).sum(axis=3) / l
        k_l = k.reshape(b, H, M, l, DH).sum(axis=3) / l
        sim1 = jnp.einsum('bhid,bhjd->bhij', q, k_l)
        sim2 = jnp.einsum('bhid,bhjd->bhij', q_l, k_l)
        sim3 = jnp.einsum('bhid,bhjd->bhij', q_l, k)
        attn1 = jax.nn.softmax(sim1, axis=-1)
        attn2 = jax.nn.softmax(sim2, axis=-1)
        attn3 = jax.nn.softmax(sim3, axis=-1)
        attn2_inv = moore_penrose_inverse(attn2)
        out = attn1 @ attn2_inv @ (attn3 @ v)
        res = jax.lax.conv_general_dilated(out, w_conv, window_strides=(1, 1), padding=((K // 2, K // 2), (0, 0)), feature_group_count=H, dimension_numbers=('NCHW', 'OIHW', 'NCHW'))
        out = out + res
        out = out.transpose(0, 2, 1, 3).reshape(b, n, H * DH)
        out = out @ w_fc + b_fc
        return out

    def _L0_ffn_ref(hidden_states, router_w, w_gate, w_up, w_down):
        import jax, jax.numpy as jnp
        import numpy as np
        JITTER_EPS = 0.01
        NEG_INF = -jnp.inf

        def sparsemixer_eval(scores, jitter_eps):
            m1 = jnp.max(scores, axis=-1, keepdims=True)
            ind1 = jnp.argmax(scores, axis=-1)
            factor1 = jnp.maximum(jnp.abs(scores), m1)
            mask1 = jax.lax.stop_gradient((m1 - scores) / factor1 > 2.0 * jitter_eps)
            gates1 = jax.nn.softmax(jnp.where(mask1, NEG_INF, scores), axis=-1)
            mult1 = jnp.take_along_axis(gates1, ind1[:, None], axis=-1)[:, 0]
            E = scores.shape[-1]
            onehot1 = ind1[:, None] == jnp.arange(E)[None, :]
            masked_scores = jnp.where(onehot1, NEG_INF, scores)
            m2 = jnp.max(masked_scores, axis=-1, keepdims=True)
            ind2 = jnp.argmax(masked_scores, axis=-1)
            factor2 = jnp.maximum(jnp.abs(scores), m2)
            mask2 = jax.lax.stop_gradient((m2 - scores) / factor2 > 2.0 * jitter_eps)
            gates2 = jax.nn.softmax(jnp.where(mask2, NEG_INF, masked_scores), axis=-1)
            mult2 = jnp.take_along_axis(gates2, ind2[:, None], axis=-1)[:, 0]
            multiplier = jnp.stack([mult1, mult2], axis=-1)
            selected = jnp.stack([ind1, ind2], axis=-1)
            return (multiplier, selected)
        B, S, H = hidden_states.shape
        E = router_w.shape[0]
        x = hidden_states.reshape(-1, H)
        T = x.shape[0]
        logits = x @ router_w.T
        routing_weights, selected = sparsemixer_eval(logits, JITTER_EPS)
        tok = jnp.arange(T)
        dense_w = jnp.zeros((T, E), dtype=x.dtype)
        dense_w = dense_w.at[tok, selected[:, 0]].add(routing_weights[:, 0])
        dense_w = dense_w.at[tok, selected[:, 1]].add(routing_weights[:, 1])
        out = jnp.zeros_like(x)
        for e in range(E):
            h = jax.nn.silu(x @ w_gate[e].T) * (x @ w_up[e].T)
            out = out + dense_w[:, e:e + 1] * (h @ w_down[e].T)
        return out.reshape(B, S, H)
    x = L0_attn_x
    x = x + _L0_attn_ref(_layernorm(x, axis=-1), L0_attn_w_qkv, L0_attn_w_conv, L0_attn_w_fc, L0_attn_b_fc)
    x = x + _L0_ffn_ref(_layernorm(x, axis=-1), L0_ffn_router_w, L0_ffn_w_gate, L0_ffn_w_up, L0_ffn_w_down)
    return x

_drawn_inputs = setup_inputs


def setup_inputs(seed=0):
    import zlib

    import numpy as np

    out = dict(_drawn_inputs(seed))
    spreads = {'L0_attn_b_fc': (0.0, 0.8)}
    factors = {'L0_attn_w_qkv': 7.147,
     'L0_attn_w_conv': 8.0,
     'L0_attn_w_fc': 7.642,
     'L0_ffn_router_w': 8.0,
     'L0_ffn_w_gate': 8.0,
     'L0_ffn_w_up': 8.0,
     'L0_ffn_w_down': 8.0}
    for name, (base, spread) in spreads.items():
        noise = np.random.default_rng([zlib.crc32(name.encode()), seed]).standard_normal(out[name].shape)
        drawn = base * np.exp(spread * noise) if base else spread * noise
        out[name] = jnp.asarray(drawn.astype(out[name].dtype))
    for name, factor in factors.items():
        out[name] = (out[name] * factor).astype(out[name].dtype)
    return out
```

```python
from contextlib import ExitStack

import concourse.bass as bass
from concourse import mybir

F32 = mybir.dt.float32
I32 = mybir.dt.int32
U32 = mybir.dt.uint32
ALU = mybir.AluOpType
ACT = mybir.ActivationFunctionType
AX = mybir.AxisListType.X

P = 128
B, N, D = 4, 1024, 256
H, DH, M = 16, 64, 64
INNER = H * DH
J = H // 2
KD = D // P
RT = N // P
ITERS = 6
TAPS = 13
HALO = TAPS // 2
TO = P - 2 * HALO
CT = -(-N // TO)
LAST = N - (CT - 1) * TO
PADN = (CT - 1) * TO + P
NQ = B * J
EPS = 1e-5
E, F = 8, 512
JITTER2 = 0.02
TOK = B * N
REGION = TOK + P
ZROW = E * REGION
NTILE = (2 * TOK + E * (P - 1)) // P + 1
NTILE += NTILE % 2
ROW = D + 4
QT = B * CT
RSQRT_MAGIC = float(0x5F3759DF)
BIG = 3.0e38
CH = 8
STARTED = (
    "a_x_used", "c1_sim", "c1_ut", "c2_sim", "c2_x1_0", "c2_x1_1", "c2_conv", "x1n_out0",
    "x1n_out1", "c2_x1tp", "a_xnt_out", "a_lm", "c1_tp", "c1_v3mm", "c2_y", "c2_lgmm",
    "m_up0", "m_up1", "m_hid0", "m_hid1", "m_down0", "m_down1", "a_xn_out", "a_tp",
    "c1_exp", "c2_a1", "c2_x1n", "x1_out0", "x1_out1", "m_htp0", "m_htp1", "a_xnt",
    "c1_e3b", "c1_e3a", "c1_utb", "c1_v3", "i_zt", "c2_sub", "c2_cvt", "c2_lg",
    "m_y0", "m_y1",
)


class Chain:

    def __init__(self, eng, sem):
        self.eng, self.sem, self.base, self.n = eng, sem, 0, 0

    def step(self, ins):
        ins.then_inc(self.sem, 1)
        self.n += 1

    def sync(self):
        self.eng.wait_ge(self.sem, self.base + self.n)

    def link(self, ins):
        self.step(ins)
        self.sync()

    def enter(self, i, per_turn):
        self.start, self.per_turn, self.n0 = self.base + self.n, per_turn, self.n
        self.base, self.n = self.start + i * per_turn, 0

    def leave(self, turns):
        assert self.n == self.per_turn, (self.n, self.per_turn)
        self.base, self.n = self.start + turns * self.per_turn, 0


def layer(nc, x, w_qkv, wq_t, wk_t, conv_band, w_fc, b_fc, router_t, w_gu, w_down, out):
    with ExitStack() as ctx:
        def sb(name, words):
            return ctx.enter_context(nc.sbuf_tensor(name, [P, words], F32))

        def sem(name):
            return ctx.enter_context(nc.semaphore(name))

        def dram(name, shape):
            return nc.dram_tensor(name, shape, F32, kind="Internal").ap()

        xn_d = dram("xn_d", (B, P, RT * D))
        xnt_d = dram("xnt_d", (B, P, KD * PADN))
        x1_d = dram("x1_d", (B, N, D))
        x1n_d = dram("x1n_d", (B, N, D))
        xs_d = dram("xs_d", (ZROW + P, ROW))
        yo_d = dram("yo_d", (2 * TOK, D))

        mem = sb("mem", 50500)

        def at(start, words):
            return mem[:, start:start + words]

        SQ = NQ * P
        zt = at(0, SQ).rearrange("p (q c) -> p q c", q=NQ)
        z = at(SQ, SQ).rearrange("p (q c) -> p q c", q=NQ)
        azt = at(2 * SQ, SQ).rearrange("p (q c) -> p q c", q=NQ)
        tt = at(3 * SQ, SQ).rearrange("p (q c) -> p q c", q=NQ)
        att = at(4 * SQ, SQ).rearrange("p (q c) -> p q c", q=NQ)
        xnb = at(5 * SQ, RT * D).rearrange("p (t c) -> p t c", t=RT)
        g3 = at(5 * SQ + RT * D, KD * INNER).rearrange("p (k c) -> p k c", k=KD)
        q_bd = at(6 * SQ, SQ).rearrange("p (j b c) -> p j b c", j=J, b=B)
        k_bd = at(7 * SQ, SQ).rearrange("p (j b c) -> p j b c", j=J, b=B)
        v3 = at(8 * SQ, SQ).rearrange("p (b j c) -> p b j c", b=B, j=J)
        o = 9 * SQ
        xnt = at(o, KD * PADN).rearrange("p (k n) -> p k n", k=KD); o += KD * PADN
        wqt = at(o, J * D).rearrange("p (j c) -> p j c", j=J); o += J * D
        wkt = at(o, J * D).rearrange("p (j c) -> p j c", j=J)
        xr = at(o, 2 * D).rearrange("p (u c) -> p u c", u=2)
        x1 = at(o + 2 * D, 2 * D).rearrange("p (u c) -> p u c", u=2)
        x1n = at(o + 4 * D, 2 * D).rearrange("p (u c) -> p u c", u=2)
        bfc = at(o + 6 * D, D)
        o += J * D
        wv = at(o, KD * INNER).rearrange("p (k c) -> p k c", k=KD)
        x1t = at(o, KD * P).rearrange("p (k c) -> p k c", k=KD)
        logits = at(o + KD * P, QT * E).rearrange("p (q e) -> p q e", q=QT)
        o += KD * INNER
        wfc = at(o, J * D).rearrange("p (j c) -> p j c", j=J); o += J * D
        ex = at(o, 2 * INNER).rearrange("p (u c) -> p u c", u=2); o += 2 * INNER
        e3t = at(o, RT * P).rearrange("p (t c) -> p t c", t=RT)
        wts = at(o, 4 * P).rearrange("p (s c) -> p s c", s=4)
        utb = at(o + RT * P, KD * P).rearrange("p (k c) -> p k c", k=KD)
        xm = at(5 * SQ + RT * D, KD * B * M).rearrange("p (k c) -> p k c", k=KD)
        o += RT * P + KD * P
        assert o <= 50500
        xb = at(0, RT * D).rearrange("p (t c) -> p t c", t=RT)
        wqk = at(2 * SQ, KD * 2 * INNER).rearrange("p (k c) -> p k c", k=KD)
        k_st = at(3 * SQ, J * B * M).rearrange("p (j b c) -> p j b c", j=J, b=B)
        sm2 = at(3 * SQ + 2048, NQ * M).rearrange("p (q c) -> p q c", q=NQ)
        w_gu_s = at(0, E * KD * 2 * F).rearrange("p (e k g f) -> p e k g f", e=E, k=KD, g=2)
        pm = at(4 * SQ, NQ * D).rearrange("p (b j c) -> p b j c", b=B, j=J)
        a1 = at(6 * SQ, 2 * INNER).rearrange("p (u h c) -> p u h c", u=2, h=H)
        cvt = at(6 * SQ + 2 * INNER, 2 * J * TO).rearrange("p (u j c) -> p u j c", u=2, j=J)
        g1 = at(8 * SQ, KD * INNER).rearrange("p (k c) -> p k c", k=KD)
        band = at(8 * SQ + KD * INNER, H * TO).rearrange("p (h c) -> p h c", h=H)
        w_d_s = at(6 * SQ, E * 4 * D).rearrange("p (e f c) -> p e f c", e=E, f=4)
        o = 8 * SQ
        def take(words):
            nonlocal o
            o += words
            return at(o - words, words)
        r_a = [take(QT * E).rearrange("p (q e) -> p q e", q=QT) for _ in range(11)]
        assert o < 9 * SQ + KD * PADN
        o = 8 * SQ
        xd = take(3 * 2 * ROW).rearrange("p (u c w) -> p u c w", u=3, c=2)
        o = 8 * SQ
        xs = take(2 * ROW).rearrange("p (u c) -> p u c", u=2)
        xst = take(2 * D).rearrange("p (u k c) -> p u k c", u=2, k=KD)
        sil = take(2 * F).rearrange("p (u c) -> p u c", u=2)
        hid = take(2 * F).rearrange("p (u c) -> p u c", u=2)
        hidt = take(2 * F).rearrange("p (u f c) -> p u f c", u=2, f=4)
        ys = take(2 * D).rearrange("p (u c) -> p u c", u=2)
        o = 0
        CW = TOK * D // P // CH
        fin = take(2 * 3 * CW).rearrange("p (u s c) -> p u s c", u=2, s=3)

        ident = sb("ident", P)
        eyes = sb("eyes", 3 * P)
        eye7, eye15, eye13 = (eyes[:, i * P:(i + 1) * P] for i in range(3))
        tri = sb("tri", P)
        ones = sb("ones", P)
        shift = sb("shift", TO)
        validf = sb("validf", 4)
        rw = sb("rw", KD * E)
        small = sb("small", 512)
        stats = small[:, 0:6 * RT].rearrange("p (t c) -> p t c", t=RT)
        mv = small[:, 48:48 + 2 * RT].rearrange("p (t c) -> p t c", t=RT)
        ve, rs, tmp = (small[:, 64 + 8 * i:72 + 8 * i] for i in range(3))
        mx = small[:, 96:128]
        sm = small[:, 128:160]
        ri = small[:, 160:192]
        zz = small[:, 192:200]
        mv2 = small[:, 200:204].rearrange("p (u c) -> p u c", u=2)
        st2 = small[:, 204:216].rearrange("p (u c) -> p u c", u=2)
        rs2 = small[:, 216:218]
        tm2 = small[:, 218:220]
        nmx = small[:, 220:222]
        s3 = small[:, 222:224]
        r3 = small[:, 224:226]
        idx = small[:, 226:232]
        ecol = small[:, 232:240]
        ebase = small[:, 240:248]
        n_e, nt, te, tb, tc = (small[:, 248 + 8 * i:256 + 8 * i] for i in range(5))
        mx2, sm2s, ri2 = (small[:, 288 + 32 * i:320 + 32 * i] for i in range(3))
        t_eid, t_row, t_a, t_tau = (sb(f"tab{i}", NTILE) for i in range(4))
        n_pad = sb("n_pad", E)
        route = sb("route", 8 * QT)
        m1, m2, i1, w1, w2, sl1, sl2, tokid = (route[:, i * QT:(i + 1) * QT] for i in range(8))
        pad = sb("pad", ROW)

        ps = ctx.enter_context(nc.psum_tensor("ps", [P, 8 * 512], F32))

        def bank(i, n=1):
            return ps[:, i * 512:(i + n) * 512]

        S = {}

        def s(name):
            if name not in S:
                S[name] = sem(name)
            return S[name]

        def use2(b, t):
            return ((CT + 1 - t % 2) // 2) * b + t // 2 + 1

        def use3(b, t):
            return (CT // 3) * b + t // 3 + 1

        def wait_alone(eng, name, count):
            eng.wait_ge(s(name), count)
            eng.sem_inc(s("passed"), 1)

        block = ctx.enter_context(nc.Block())
        x_t = x.rearrange("b (t p) c -> b p t c", p=P)

        @block.sync
        def _(sp):
            for name in STARTED:
                sp.sem_inc(s(name), 1)
            with sp.Fori(0, B) as b:
                sp.wait_ge(s("a_x_used"), 1 + b)
                sp.dma_start(xb, x_t[b]).then_inc(s("a_x_in"), 16)
                sp.wait_ge(s("a_xn"), RT * b + RT)
                sp.dma_start(xn_d[b].rearrange("p (t c) -> p t c", t=RT), xnb).then_inc(s("a_xn_out"), 16)
                sp.wait_ge(s("a_xnt"), 1 + 4 * b + 4)
                sp.dma_start(xnt_d[b].rearrange("p (k n) -> p k n", k=KD), xnt).then_inc(s("a_xnt_out"), 16)
            sp.dma_start(wqk, w_qkv[:, 0:2 * INNER].rearrange("(k p) c -> p k c", p=P)).then_inc(s("w_qk_in"), 16)
            sp.dma_start(wqt, wq_t.rearrange("(j p) c -> p j c", p=P)).then_inc(s("w_in"), 16)
            sp.dma_start(wkt, wk_t.rearrange("(j p) c -> p j c", p=P)).then_inc(s("w_in"), 16)
            sp.dma_start(wv, w_qkv[:, 2 * INNER:].rearrange("(k p) c -> p k c", p=P)).then_inc(s("w_in"), 16)
            sp.dma_start(wfc, w_fc.rearrange("(j p) c -> p j c", p=P)).then_inc(s("w_in"), 16)
            sp.dma_start(rw[:, :].rearrange("p (k e) -> p k e", k=KD),
                         router_t.rearrange("(k p) e -> p k e", p=P)).then_inc(s("w_in"), 16)
            sp.wait_ge(s("a_xn_out"), 1 + 16 * B)
            sp.wait_ge(s("a_xnt_out"), 1 + 16 * B)
            sp.wait_ge(s("a_lm"), 1 + KD * B)
            with sp.Fori(0, B) as b:
                sp.wait_ge(s("c1_sim"), 1 + J * b)
                sp.dma_start(xnt, xnt_d[b].rearrange("p (k n) -> p k n", k=KD)).then_inc(s("c1_xnt_in"), 16)
                sp.wait_ge(s("c1_ut"), 1 + J * b)
                sp.dma_start(xnb, xn_d[b].rearrange("p (t c) -> p t c", t=RT)).then_inc(s("c1_xn_in"), 16)
            sp.wait_ge(s("p_wt_mm"), NQ // 4)
            sp.dma_start(band, conv_band.rearrange("h p c -> p h c")).then_inc(s("band_in"), 16)
            sp.dma_start(bfc, b_fc.rearrange("(o c) -> o c", o=1).to_broadcast([P, D])).then_inc(s("bfc_in"), 16)
            for k in range(KD):
                sp.dma_start(w_gu_s[:, :, k], w_gu[:, k].rearrange("e p g f -> p e g f")).then_inc(s("wgu_in"), 16)
            sp.wait_ge(s("c1_sim"), 1 + J * B)
            with sp.Fori(0, B) as b:
                sp.wait_ge(s("c2_sim"), 1 + CT * b)
                sp.dma_start(xnt, xnt_d[b].rearrange("p (k n) -> p k n", k=KD)).then_inc(s("c2_xnt_in"), 16)
                for t in range(CT):
                    rows = TO if t < CT - 1 else LAST
                    u = t % 2
                    sp.wait_ge(s(f"c2_x1_{u}"), 1 + use2(b, t) - 1)
                    sp.dma_start(xr[0:rows, u], x[b, TO * t:TO * t + rows, :]).then_inc(s(f"c2_xr_in{u}"), 16)
            sp.wait_ge(s("c2_y"), 1 + QT)
            for e2 in range(2):
                sp.dma_start(w_d_s[:, 4 * e2:4 * e2 + 4], w_down[4 * e2:4 * e2 + 4].rearrange("e p f c -> p e f c"))\
                  .then_inc(s("wd_in"), 16)
            sp.wait_ge(s("d_tab"), 1)
            for e in range(E):
                n = sp.value_load(n_pad[0:1, e:e + 1].bitcast(I32), min_val=0, max_val=TOK)
                sp.dma_start(xs_d[bass.ds(n + e * REGION, P), :], pad[:, :]).then_inc(s("d_pad_out"), 16)
            sp.dma_start(xs_d[ZROW:ZROW + P, :], pad[:, :]).then_inc(s("d_pad_out"), 16)
            for u in range(2):
                sp.wait_ge(s(f"x1n_out{u}"), 1 + 16 * use2(B - 1, CT - 2 + (CT - u) % 2))
            def dispatch_rows(b, first):
                for t in range(CT):
                    rows, v = (TO if t < CT - 1 else LAST), t % 3
                    if not (first and t < 3):
                        sp.wait_ge(s(f"d_sc{v}"), 32 * (use3(b, t) - 1))
                    for c in range(2):
                        sp.dma_start(xd[0:rows, v, c, 0:D], x1n_d[b, TO * t:TO * t + rows, :])\
                          .then_inc(s(f"d_x_in{v}"), 16)

            dispatch_rows(0, True)
            with sp.Fori(1, B) as b:
                dispatch_rows(b, False)
            sp.wait_ge(s("d_pad_out"), 16 * (E + 1))
            for v in range(3):
                sp.wait_ge(s(f"d_sc{v}"), 32 * use3(B - 1, CT - 3 + v))
            def expert_rows(i, first):
                for u in range(2):
                    if not first:
                        sp.wait_ge(s(f"m_sc{u}"), 16 * i)
                    r = sp.value_load(t_row[0:1, bass.ds(2 * i + u, 1)].bitcast(I32), min_val=0, max_val=ZROW)
                    sp.dma_start(xs[:, u], xs_d[bass.ds(r, P), :]).then_inc(s(f"m_xs_in{u}"), 16)

            expert_rows(0, True)
            with sp.Fori(1, NTILE // 2) as i:
                expert_rows(i, False)
            for u in range(2):
                sp.wait_ge(s(f"m_sc{u}"), 16 * (NTILE // 2))
            for u in range(2):
                sp.wait_ge(s(f"x1_out{u}"), 1 + 16 * use2(B - 1, CT - 2 + (CT - u) % 2))
            x1f = x1_d.rearrange("b n c -> (b n c)").rearrange("(p k c) -> k p c", p=P, k=CH)
            yf = yo_d[0:2 * TOK, :].rearrange("(h n) c -> h (n c)", h=2).rearrange("h (p k c) -> h k p c", p=P, k=CH)
            of = out.rearrange("b n c -> (b n c)").rearrange("(p k c) -> k p c", p=P, k=CH)
            for k in range(CH):
                if k >= 2:
                    sp.wait_ge(s(f"f_out{k % 2}"), 16 * (k // 2))
                for c, src in enumerate((x1f[k], yf[0, k], yf[1, k])):
                    sp.dma_start(fin[:, k % 2, c], src).then_inc(s(f"f_in{k % 2}"), 16)
            for u in range(2):
                sp.wait_ge(s(f"f_out{u}"), 16 * CH // 2)

        @block.gpsimd
        def _(pool):
            ch = Chain(pool, s("pool_chain"))
            ch.link(pool.memset(ident[:, :], 0.0))
            ch.link(pool.affine_select(out=ident[:, :], in_=ident[:, :], compare_op=ALU.not_equal, fill=1.0,
                                       base=0, pattern=[[-1, P]], channel_multiplier=1))
            for eye, c in ((eye7, 7.0), (eye15, 15.0), (eye13, 13.0 / 4)):
                ch.link(pool.tensor_scalar(eye, ident[:, :], c, 0.0, ALU.mult, ALU.add))
            ch.link(pool.memset(ones[:, :], 1.0))
            ch.link(pool.memset(validf[:, :], 1.0))
            ch.link(pool.affine_select(out=tri[:, :], in_=ones[:, :], compare_op=ALU.is_gt, fill=0.0,
                                       base=0, pattern=[[1, P]], channel_multiplier=-1))
            ch.link(pool.affine_select(out=validf[:, 0:1], in_=validf[:, 0:1], compare_op=ALU.is_ge, fill=0.0,
                                       base=-HALO, pattern=[[0, 1]], channel_multiplier=1))
            ch.link(pool.affine_select(out=validf[:, 1:2], in_=validf[:, 1:2], compare_op=ALU.is_ge, fill=0.0,
                                       base=LAST + HALO - 1, pattern=[[0, 1]], channel_multiplier=-1))
            ch.link(pool.affine_select(out=validf[:, 2:3], in_=validf[:, 2:3], compare_op=ALU.is_ge, fill=0.0,
                                       base=TO - 1, pattern=[[0, 1]], channel_multiplier=-1))
            ch.link(pool.affine_select(out=validf[:, 3:4], in_=validf[:, 3:4], compare_op=ALU.is_ge, fill=0.0,
                                       base=LAST - 1, pattern=[[0, 1]], channel_multiplier=-1))
            ch.link(pool.memset(shift[:, :], 0.0))
            ch.link(pool.affine_select(out=shift[:, :], in_=shift[:, :], compare_op=ALU.not_equal, fill=1.0,
                                       base=-HALO, pattern=[[-1, TO]], channel_multiplier=1))
            ch.link(pool.iota(ecol.bitcast(I32), pattern=[[1, E]], base=-E, channel_multiplier=0))
            ch.link(pool.iota(ebase.bitcast(I32), pattern=[[REGION, E]], base=0, channel_multiplier=0))
            ch.link(pool.iota(t_tau[:, :].bitcast(I32), pattern=[[1, NTILE]], base=0, channel_multiplier=0))
            ch.link(pool.iota(tokid.bitcast(I32), pattern=[[N, B], [TO, CT]], base=0, channel_multiplier=1))
            ch.link(pool.memset(pad[:, :], 0.0))
            ch.link(pool.iota(pad[:, D + 1:D + 2].bitcast(I32), pattern=[[0, 1]], base=2 * TOK, channel_multiplier=1))
            ch.link(pool.memset(xnt[:, :, 0:HALO], 0.0))
            ch.link(pool.memset(xnt[:, :, HALO + N:PADN], 0.0))
            ch.link(pool.memset(q_bd[0:64, :, :, 64:128], 0.0))
            ch.link(pool.memset(q_bd[64:128, :, :, 0:64], 0.0))
            ch.link(pool.memset(k_bd[0:64, :, :, 64:128], 0.0))
            ch.link(pool.memset(k_bd[64:128, :, :, 0:64], 0.0))
            ch.link(pool.memset(v3[0:64, :, :, 64:128], 0.0))
            ch.sync()
            pool.memset(v3[64:128, :, :, 0:64], 0.0).then_inc(s("consts"), 1)
            pool.wait_ge(s("a_x_used"), 1 + B)
            ch.link(pool.memset(zt[0:64, :, 64:128], 0.0))
            ch.sync()
            pool.memset(zt[64:128, :, 0:64], 0.0).then_inc(s("zt_zero"), 1)
            pool.wait_ge(s("b_k_act"), J)
            pool.wait_ge(s("b_k_dve"), J)
            pool.tensor_copy(k_st[0:64], k_bd[0:64, :, :, 0:64]).then_inc(s("b_kst"), 1)
            pool.tensor_copy(k_st[64:128], k_bd[64:128, :, :, 64:128]).then_inc(s("b_kst"), 1)
            pool.wait_ge(s("b_sums"), 2)
            pool.partition_all_reduce(zz[:, 2:4], zz[:, 0:2], P, bass.bass_isa.ReduceOp.max).then_inc(s("b_gmax"), 1)
            pool.wait_ge(s("band_in"), 16)
            pool.tensor_tensor(band, band, shift[:, :].unsqueeze(1).to_broadcast([P, H, TO]), ALU.add)\
                .then_inc(s("band_ok"), 1)
            pool.wait_ge(s("bfc_in"), 16)

            def norm_rows(b, t):
                rows, u, q = (TO if t < CT - 1 else LAST), t % 2, CT * b + t
                pool.wait_ge(s("c2_guess"), q + 1)
                v, r, w = zz[:, 4 + u:5 + u], rs2[:, u:u + 1], tm2[:, u:u + 1]
                for n in range(3):
                    ch.link(pool.tensor_tensor(w, r, r, ALU.mult))
                    ch.step(pool.tensor_tensor(w, w, v, ALU.mult))
                    wait_alone(pool, "pool_chain", ch.base + ch.n)
                    ch.link(pool.tensor_scalar(w, w, -0.5, 1.5, ALU.mult, ALU.add))
                    ch.step(pool.tensor_tensor(r, r, w, ALU.mult))
                    ch.sync()
                pool.wait_ge(s(f"x1n_out{u}"), 1 + 16 * (use2(b, t) - 1))
                wait_alone(pool, "c2_x1tp", 1 + (q - 1 if t >= 1 else CT * b))
                pool.tensor_scalar(x1n[0:rows, u], x1[0:rows, u], mv2[0:rows, u, 0:1], rs2[0:rows, u:u + 1],
                                   ALU.subtract, ALU.mult).then_inc(s("c2_x1n"), 1)

            with pool.Fori(0, B) as b:
                ch.enter(b, 12 * CT)
                for t in range(CT + 1):
                    if t < CT:
                        rows, u, q = (TO if t < CT - 1 else LAST), t % 2, CT * b + t
                        pool.wait_ge(s(f"c2_xr_in{u}"), 16 * use2(b, t))
                        pool.tensor_tensor(xr[0:rows, u], xr[0:rows, u], bfc[0:rows], ALU.add).then_inc(s("c2_xrb"), 1)
                        pool.wait_ge(s("c2_rinv"), q + 1)
                        pool.wait_ge(s("c2_conv"), 1 + (q - 1 if t >= 1 else CT * b))
                        pool.tensor_tensor(a1[:, u], ex[:, u].rearrange("p (h c) -> p h c", h=H),
                                           ri[:, 16 * u:16 * u + 16].unsqueeze(2).to_broadcast([P, H, M]),
                                           ALU.mult).then_inc(s("c2_a1"), 1)
                    if t >= 1:
                        norm_rows(b, t - 1)
                ch.leave(B)
            with pool.Fori(0, B) as b:
                for t in range(CT):
                    rows = TO if t < CT - 1 else LAST
                    wait_alone(pool, "d_meta", CT * b + t + 1)
                    for c in range(2):
                        k = 2 * (t % 3) + c
                        pool.indirect_dma_start(
                            out=xs_d, out_offset=bass.IndirectOffsetOnAxis(ap=idx[0:rows, k:k + 1].bitcast(U32), axis=0),
                            in_=xd[0:rows, t % 3, c], in_offset=None).then_inc(s(f"d_sc{t % 3}"), 16)
            with pool.Fori(0, NTILE // 2) as i:
                for u in range(2):
                    wait_alone(pool, f"m_y{u}", 1 + i + 1)
                    pool.indirect_dma_start(
                        out=yo_d, out_offset=bass.IndirectOffsetOnAxis(ap=xs[:, u, D + 1:D + 2].bitcast(U32), axis=0),
                        in_=ys[:, u], in_offset=None, bounds_check=2 * TOK - 1, oob_is_err=False).then_inc(s(f"m_sc{u}"), 16)
            for k in range(CH):
                pool.wait_ge(s("f_sum1"), k + 1)
                pool.tensor_tensor(fin[:, k % 2, 0], fin[:, k % 2, 1], fin[:, k % 2, 2], ALU.add).then_inc(s("f_sum"), 1)

        @block.scalar
        def _(act):
            act.wait_ge(s("consts"), 1)
            with act.Fori(0, B) as b:
                act.wait_ge(s("a_xnt_out"), 1 + 16 * b)
                act.wait_ge(s("a_lm"), 1 + KD * b)
                for g in range(4):
                    half, k = g // 2, g % 2
                    act.wait_ge(s("a_tp"), 1 + 4 * b + g + 1)
                    act.activation(xnt[:, k, HALO + 512 * half:HALO + 512 * half + 512], bank(2 * k + half),
                                   ACT.Copy).then_inc(s("a_xnt"), 1)
            for j in range(J):
                act.wait_ge(s("b_lm"), 2 * j + 1)
                act.activation(q_bd[0:64, j, :, 0:64], bank(2 * j % 8)[0:64, 0:B * M].rearrange("p (b m) -> p b m", b=B),
                               ACT.Copy, scale=DH ** -0.5 / (N // M)).then_inc(s("b_q_act"), 1)
                act.wait_ge(s("b_lm"), 2 * j + 2)
                act.activation(k_bd[0:64, j, :, 0:64], bank((2 * j + 1) % 8)[0:64, 0:B * M].rearrange("p (b m) -> p b m", b=B),
                               ACT.Copy, scale=1.0 / (N // M)).then_inc(s("b_k_act"), 1)
            for g in range(B):
                act.wait_ge(s("b_sub"), g + 1)
                act.activation(sm2[:, J * g:J * g + J], sm2[:, J * g:J * g + J], ACT.Exp).then_inc(s("b_exp"), 1)
            for g in range(4):
                act.wait_ge(s("b_at_tp"), 2 * g + 1)
                act.activation(att[:, 8 * g:8 * g + 4], bank(2 * g).rearrange("p (q c) -> p q c", q=4),
                               ACT.Copy).then_inc(s("b_at_act"), 1)
            def c1_tail(b, j):
                q = J * b + j
                act.wait_ge(s("c1_ut"), 1 + q + 1)
                act.wait_ge(s("c1_v3mm"), 1 + q)
                act.activation(utb, bank(6)[:, 0:KD * P].rearrange("p (k c) -> p k c", k=KD), ACT.Copy)\
                   .then_inc(s("c1_utb"), 1)

            with act.Fori(0, B) as b:
                for k in range(KD):
                    act.wait_ge(s("c1_g3mm"), 2 * b + k + 1)
                    act.activation(g3[:, k], bank(2 * k, 2), ACT.Copy).then_inc(s("c1_g3"), 1)
                for j in range(J):
                    u, q = j % 2, J * b + j
                    act.wait_ge(s("c1_nmx"), q + 1)
                    act.wait_ge(s("c1_tp"), 1 + (q - 1 if j >= 1 else J * b))
                    act.activation(ex[:, u], bank(2 * u, 2), ACT.Exp, bias=nmx[:, u:u + 1],
                                   accum_out=s3[:, u:u + 1]).then_inc(s("c1_exp"), 1)
                    if j >= 1:
                        c1_tail(b, j - 1)
                    act.wait_ge(s("c1_tp"), 1 + q + 1)
                    act.wait_ge(s("c1_ut"), 1 + q)
                    act.activation(e3t[:, 0:4], bank(4).rearrange("p (t c) -> p t c", t=4), ACT.Copy)\
                       .then_inc(s("c1_e3a"), 1)
                c1_tail(b, J - 1)
            with act.Fori(0, ITERS) as it:
                for g in range(4):
                    act.wait_ge(s("i_zmm"), 4 * it + g + 1)
                    act.activation(z[:, 8 * g:8 * g + 8], bank(2 * g, 2).rearrange("p (q c) -> p q c", q=8),
                                   ACT.Copy).then_inc(s("i_z"), 1)
                for g in range(4):
                    act.wait_ge(s("i_ztp"), g + 1 + 4 * it)
                    act.activation(zt[:, 8 * g:8 * g + 8], bank(2 * g, 2).rearrange("p (q c) -> p q c", q=8),
                                   ACT.Copy).then_inc(s("i_zt"), 1)
            for g in range(NQ // 4):
                act.wait_ge(s("p_wt_mm"), g + 1)
                act.wait_ge(s("p_mm"), g)
                act.activation(wts, bank(g % 2).rearrange("p (s c) -> p s c", s=4), ACT.Copy).then_inc(s("p_wt"), 1)
                act.wait_ge(s("p_mm"), g + 1)
                act.activation(pm[:, g // 2, 4 * (g % 2):4 * (g % 2) + 4],
                               bank(2 + 2 * (g % 2), 2).rearrange("p (s c) -> p s c", s=4), ACT.Copy)\
                   .then_inc(s("p_pm"), 1)
            def store_rows(b, t):
                rows, u, q = (TO if t < CT - 1 else LAST), t % 2, CT * b + t
                act.wait_ge(s(f"c2_x1_{u}"), 1 + use2(b, t))
                act.dma_start(x1_d[b, TO * t:TO * t + rows, :], x1[0:rows, u]).then_inc(s(f"x1_out{u}"), 16)

            def store_norm(b, t):
                rows, u, q = (TO if t < CT - 1 else LAST), t % 2, CT * b + t
                act.wait_ge(s("c2_x1n"), 1 + q + 1)
                act.dma_start(x1n_d[b, TO * t:TO * t + rows, :], x1n[0:rows, u]).then_inc(s(f"x1n_out{u}"), 16)
                act.wait_ge(s("c2_x1tp"), 1 + q + 1)
                act.wait_ge(s("c2_lgmm"), 1 + q)
                act.activation(x1t[:, :, 0:rows], bank(7)[:, 0:KD * rows].rearrange("p (k c) -> p k c", k=KD),
                               ACT.Copy).then_inc(s("c2_x1t"), 1)

            with act.Fori(0, B) as b:
                for k in range(KD):
                    act.wait_ge(s("c2_g1mm"), 2 * b + k + 1)
                    act.activation(g1[:, k], bank(2 * k, 2), ACT.Copy, scale=DH ** -0.5).then_inc(s("c2_g1"), 1)
                for t in range(CT + 1):
                    if t < CT:
                        u, q = t % 2, CT * b + t
                        act.wait_ge(s("c2_sub"), 1 + q + 1)
                        act.activation(ex[:, u], ex[:, u], ACT.Exp).then_inc(s("c2_exp"), 1)
                    if t >= 1:
                        store_rows(b, t - 1)
                    if t >= 2:
                        store_norm(b, t - 2)
                    if t < CT:
                        act.wait_ge(s("c2_conv"), 1 + q + 1)
                        act.wait_ge(s("c2_y"), 1 + (q - 1 if t >= 1 else CT * b))
                        act.activation(cvt[:, u], bank(4, 2).rearrange("p (j c) -> p j c", j=J)[:, :, 0:TO],
                                       ACT.Copy).then_inc(s("c2_cvt"), 1)
                store_norm(b, CT - 1)
            for c in range(2):
                act.wait_ge(s("d_gap"), c + 1)
                act.activation(r_a[4 + c], r_a[4 + c], ACT.Exp, scale=-1.0).then_inc(s("d_exp"), 1)
            with act.Fori(0, NTILE // 2) as i:
                for u in range(2):
                    act.wait_ge(s(f"m_xtp{u}"), i + 1)
                    act.wait_ge(s(f"m_up{u}"), 1 + i)
                    act.activation(xst[:, u], bank(6)[:, 0:D].rearrange("p (k c) -> p k c", k=KD), ACT.Copy)\
                       .then_inc(s(f"m_xst{u}"), 1)
                    act.wait_ge(s(f"m_gate{u}"), i + 1)
                    act.wait_ge(s(f"m_hid{u}"), 1 + i)
                    act.activation(sil[:, u], bank(u), ACT.Silu).then_inc(s(f"m_sil{u}"), 1)
                    act.wait_ge(s(f"m_htp{u}"), 1 + i + 1)
                    act.wait_ge(s(f"m_down{u}"), 1 + i)
                    act.activation(hidt[:, u], bank(4).rearrange("p (f c) -> p f c", f=4), ACT.Copy)\
                       .then_inc(s(f"m_ht{u}"), 1)
            for k in range(CH):
                act.wait_ge(s("f_sum"), k + 1)
                act.dma_start(out.rearrange("b n c -> (b n c)").rearrange("(p k c) -> k p c", p=P, k=CH)[k],
                              fin[:, k % 2, 0]).then_inc(s(f"f_out{k % 2}"), 16)

        @block.vector
        def _(dve):
            ch = Chain(dve, s("dve_chain"))
            dve.wait_ge(s("consts"), 1)
            with dve.Fori(0, B) as b:
                ch.enter(b, 2 * RT + 11)
                dve.wait_ge(s("a_x_in"), 16 * (b + 1))
                for t in range(RT):
                    ch.step(dve.bn_stats(stats[:, t], xb[:, t]))
                wait_alone(dve, "dve_chain", ch.base + ch.n)
                for t in range(RT):
                    ch.step(dve.bn_aggr(mv[:, t], stats[:, t]))
                ch.sync()
                ch.link(dve.tensor_scalar(ve, mv[:, :, 1], EPS, None, ALU.add))
                ch.link(dve.tensor_scalar(rs.bitcast(I32), ve.bitcast(I32), -0.5, RSQRT_MAGIC, ALU.mult, ALU.add))
                for _ in range(3):
                    ch.link(dve.tensor_tensor(tmp, rs, rs, ALU.mult))
                    ch.link(dve.scalar_tensor_tensor(out=tmp, in0=tmp, scalar=-0.5, in1=ve, op0=ALU.mult, op1=ALU.mult))
                    ch.link(dve.scalar_tensor_tensor(out=rs, in0=tmp, scalar=1.5, in1=rs, op0=ALU.add, op1=ALU.mult))
                dve.wait_ge(s("a_xn_out"), 1 + 16 * b)
                dve.wait_ge(s("a_tp"), 1 + 4 * b)
                for t in range(RT):
                    dve.tensor_scalar(xnb[:, t], xb[:, t], mv[:, t, 0:1], rs[:, t:t + 1], ALU.subtract, ALU.mult)\
                       .then_inc(s("a_xn"), 1)
                dve.wait_ge(s("a_xn"), RT * b + RT)
                dve.memset(tmp[:, 0:1], 0.0).then_inc(s("a_x_used"), 1)
                for k in range(KD):
                    dve.wait_ge(s("a_xnt"), 1 + 4 * b + 4)
                    dve.tensor_reduce(xm[:, k, bass.ds(M * b, M)],
                                      xnt[:, k, HALO:HALO + N].rearrange("p (m l) -> p m l", m=M), AX, ALU.add)\
                       .then_inc(s("a_lm"), 1)
                ch.leave(B)
            for j in range(J):
                dve.wait_ge(s("b_lm"), 2 * j + 1)
                dve.tensor_scalar(q_bd[64:128, j, :, 64:128], bank(2 * j % 8)[64:128, 0:B * M].rearrange("p (b m) -> p b m", b=B),
                                  DH ** -0.5 / (N // M), None, ALU.mult).then_inc(s("b_q_dve"), 1)
                dve.wait_ge(s("b_lm"), 2 * j + 2)
                dve.tensor_scalar(k_bd[64:128, j, :, 64:128],
                                  bank((2 * j + 1) % 8)[64:128, 0:B * M].rearrange("p (b m) -> p b m", b=B),
                                  1.0 / (N // M), None, ALU.mult).then_inc(s("b_k_dve"), 1)
            for g in range(B):
                sl = slice(J * g, J * g + J)
                dve.wait_ge(s("b_sim2"), g + 1)
                pg = bank(g).rearrange("p (q c) -> p q c", q=J)
                ch.link(dve.tensor_reduce(mx2[:, sl], pg, AX, ALU.max))
                dve.tensor_tensor(sm2[:, sl], pg, mx2[:, sl].unsqueeze(2).to_broadcast([P, J, M]), ALU.subtract)\
                   .then_inc(s("b_sub"), 1)
            dve.wait_ge(s("zt_zero"), 1)
            for g in range(B):
                sl = slice(J * g, J * g + J)
                dve.wait_ge(s("b_exp"), g + 1)
                ch.link(dve.tensor_reduce(sm2s[:, sl], sm2[:, sl], AX, ALU.add))
                ch.link(dve.reciprocal(ri2[:, sl], sm2s[:, sl]))
                for hf in range(2):
                    r = slice(64 * hf, 64 * hf + 64)
                    dve.tensor_tensor(zt[r, sl, 64 * hf:64 * hf + 64], sm2[r, sl],
                                      ri2[r, sl].unsqueeze(2).to_broadcast([64, J, M]), ALU.mult).then_inc(s("b_a"), 1)
            dve.wait_ge(s("b_a"), 2 * B)
            ch.link(dve.tensor_reduce(mx2, zt, AX, ALU.add))
            dve.tensor_reduce(zz[:, 0:1], mx2, AX, ALU.max).then_inc(s("b_sums"), 1)
            for g in range(4):
                dve.wait_ge(s("b_at_tp"), 2 * g + 2)
                ch.step(dve.tensor_copy(att[:, 8 * g + 4:8 * g + 8], bank(2 * g + 1).rearrange("p (q c) -> p q c", q=4)))
            ch.sync()
            dve.wait_ge(s("b_at_act"), 4)
            ch.link(dve.tensor_reduce(sm2s, att, AX, ALU.add))
            dve.tensor_reduce(zz[:, 1:2], sm2s, AX, ALU.max).then_inc(s("b_sums"), 1)
            dve.wait_ge(s("b_gmax"), 1)
            ch.link(dve.tensor_tensor(zz[:, 0:1], zz[:, 2:3], zz[:, 3:4], ALU.mult))
            ch.link(dve.reciprocal(zz[:, 1:2], zz[:, 0:1]))
            dve.tensor_scalar(z, att, zz[:, 1:2], None, ALU.mult).then_inc(s("i_z0"), 1)
            dve.tensor_scalar(zt, zt, zz[:, 1:2], None, ALU.mult).then_inc(s("i_z0"), 1)

            def c1_tail(b, j):
                q, u = J * b + j, j % 2
                dve.wait_ge(s("c1_v3mm"), 1 + q + 1)
                for hf in range(2):
                    r = slice(64 * hf, 64 * hf + 64)
                    dve.tensor_scalar(v3[r, b, j, 64 * hf:64 * hf + 64], bank(7)[r, 64 * hf:64 * hf + 64],
                                      r3[r, u:u + 1], None, ALU.mult).then_inc(s("c1_v3"), 1)

            with dve.Fori(0, B) as b:
                ch.enter(b, 2 * J)
                for j in range(J):
                    u, q = j % 2, J * b + j
                    dve.wait_ge(s("c1_sim"), 1 + q + 1)
                    ch.link(dve.tensor_reduce(mx[:, u:u + 1], bank(2 * u, 2), AX, ALU.max))
                    dve.wait_ge(s("c1_exp"), 1 + (q - 1 if j >= 1 else J * b))
                    dve.tensor_scalar(nmx[:, u:u + 1], mx[:, u:u + 1], -1.0, None, ALU.mult).then_inc(s("c1_nmx"), 1)
                    dve.wait_ge(s("c1_tp"), 1 + q + 1)
                    dve.wait_ge(s("c1_ut"), 1 + q)
                    dve.tensor_copy(e3t[:, 4:8], bank(5).rearrange("p (t c) -> p t c", t=4)).then_inc(s("c1_e3b"), 1)
                    if j >= 1:
                        c1_tail(b, j - 1)
                    dve.wait_ge(s("c1_exp"), 1 + q + 1)
                    ch.link(dve.reciprocal(r3[:, u:u + 1], s3[:, u:u + 1]))
                c1_tail(b, J - 1)
                ch.leave(B)
            def bracket(name_in, count, g, c, eye, dst, name_out):
                dve.wait_ge(s(name_in), count)
                dve.scalar_tensor_tensor(out=dst[:, 8 * g:8 * g + 8], in0=bank(2 * g, 2).rearrange("p (q c) -> p q c", q=8),
                                         scalar=c, in1=eye.unsqueeze(1).to_broadcast([P, 8, P]),
                                         op0=ALU.mult, op1=ALU.add).then_inc(s(name_out), 1)

            with dve.Fori(0, ITERS) as it:
                for g in range(4):
                    bracket("i_azmm", 4 * it + g + 1, g, -1.0, eye7, tt, "i_t1")
                for g in range(4):
                    bracket("i_t1tp", 4 * it + g + 1, g, -1.0, eye7, azt, "i_azt")
                for g in range(4):
                    bracket("i_t1mm", 4 * it + g + 1, g, -1.0, eye15, tt, "i_t2")
                for g in range(4):
                    bracket("i_t2mm", 4 * it + g + 1, g, -0.25, eye13, tt, "i_t3")

            def rows_out(b, t):
                rows, u, q = (TO if t < CT - 1 else LAST), t % 2, CT * b + t
                dve.wait_ge(s("c2_y"), 1 + q + 1)
                dve.wait_ge(s("c2_xrb"), q + 1)
                dve.wait_ge(s(f"x1_out{u}"), 1 + 16 * (use2(b, t) - 1))
                dve.wait_ge(s("c2_x1n"), 1 + (q - 1 if t >= 1 else CT * b))
                dve.tensor_tensor(x1[0:rows, u], bank(6)[0:rows, 0:D], xr[0:rows, u], ALU.add).then_inc(s(f"c2_x1_{u}"), 1)
                dve.wait_ge(s(f"c2_x1_{u}"), 1 + use2(b, t))
                ch.step(dve.bn_stats(st2[0:rows, u], x1[0:rows, u]))
                wait_alone(dve, "dve_chain", ch.base + ch.n)
                ch.link(dve.bn_aggr(mv2[0:rows, u], st2[0:rows, u]))
                ch.link(dve.tensor_scalar(zz[:, 4 + u:5 + u], mv2[:, u, 1:2], EPS, None, ALU.add))
                dve.tensor_scalar(rs2[:, u:u + 1].bitcast(I32), zz[:, 4 + u:5 + u].bitcast(I32), -0.5, RSQRT_MAGIC,
                                  ALU.mult, ALU.add).then_inc(s("c2_guess"), 1)

            def logits_out(b, t):
                rows, q = (TO if t < CT - 1 else LAST), CT * b + t
                dve.wait_ge(s("c2_lgmm"), 1 + q + 1)
                dve.tensor_copy(logits[0:rows, bass.ds(q, 1), :], bank(7)[0:rows, 256:256 + E].unsqueeze(1))\
                   .then_inc(s("c2_lg"), 1)

            dve.wait_ge(s("p_mm"), NQ // 4)
            ch.step(dve.memset(mv2, 1.0))
            ch.link(dve.memset(logits, 0.0))
            with dve.Fori(0, B) as b:
                ch.enter(b, CT * 5 + 2)
                for t in range(CT + 1):
                    if t < CT:
                        u, q = t % 2, CT * b + t
                        m, sums, inv = mx[:, 16 * u:16 * u + 16], sm[:, 16 * u:16 * u + 16], ri[:, 16 * u:16 * u + 16]
                        sc = bank(2 * u, 2).rearrange("p (h c) -> p h c", h=H)
                        exu = ex[:, u].rearrange("p (h c) -> p h c", h=H)
                        dve.wait_ge(s("c2_sim"), 1 + q + 1)
                        ch.link(dve.tensor_reduce(m, sc, AX, ALU.max))
                        dve.wait_ge(s("c2_a1"), 1 + (q - 1 if t >= 1 else CT * b))
                        dve.tensor_tensor(exu, sc, m.unsqueeze(2).to_broadcast([P, H, M]), ALU.subtract)\
                           .then_inc(s("c2_sub"), 1)
                    if t >= 1:
                        rows_out(b, t - 1)
                    if t < CT:
                        dve.wait_ge(s("c2_exp"), q + 1)
                        ch.link(dve.tensor_reduce(sums, exu, AX, ALU.add))
                        if t in (0, CT - 1):
                            ch.link(dve.reciprocal(inv, sums))
                            dve.tensor_scalar(inv, inv, validf[:, t // (CT - 1):t // (CT - 1) + 1], None, ALU.mult)\
                               .then_inc(s("c2_rinv"), 1)
                        else:
                            dve.reciprocal(inv, sums).then_inc(s("c2_rinv"), 1)
                    if t >= 3:
                        logits_out(b, t - 3)
                for t in (CT - 2, CT - 1):
                    logits_out(b, t)
                ch.leave(B)
            dve.wait_ge(s("c2_lg"), 1 + QT)
            dve.wait_ge(s("c2_conv"), 1 + QT)
            dve.wait_ge(s("c2_sim"), 1 + QT)
            d1, oh1, d2, oh2, e1v, e2v, ab, sa, sc_, t1, t2 = r_a
            bc = lambda a: a.unsqueeze(2).to_broadcast([P, QT, E])
            ec = lambda a: a.unsqueeze(1).to_broadcast([P, QT, E])
            for v in (ecol, ebase, t_tau[:, :]):
                ch.step(dve.tensor_copy(v, v.bitcast(I32)))
            ch.sync()
            ch.link(dve.scalar_tensor_tensor(out=ab, in0=logits, scalar=-1.0, in1=logits, op0=ALU.mult, op1=ALU.max))
            lg = logits
            for c, (m, d, oh, ev, w) in enumerate(((m1, d1, oh1, e1v, w1), (m2, d2, oh2, e2v, w2))):
                if c == 1:
                    ch.link(dve.scalar_tensor_tensor(out=t2, in0=oh1, scalar=-BIG, in1=logits, op0=ALU.mult, op1=ALU.add))
                    lg = t2
                ch.link(dve.tensor_reduce(m, lg, AX, ALU.max))
                ch.link(dve.tensor_tensor(d, bc(m), lg, ALU.subtract))
                ch.link(dve.scalar_tensor_tensor(out=t1, in0=d, scalar=0.0, in1=ec(ecol), op0=ALU.is_equal, op1=ALU.mult))
                ch.link(dve.tensor_reduce(i1, t1, AX, ALU.min))
                ch.link(dve.tensor_tensor(oh, bc(i1), ec(ecol), ALU.is_equal))
                dve.tensor_copy(ev, d).then_inc(s("d_gap"), 1)
                ch.link(dve.tensor_tensor(t1, ab, bc(m), ALU.max))
                ch.link(dve.scalar_tensor_tensor(out=t1, in0=t1, scalar=JITTER2, in1=d, op0=ALU.mult, op1=ALU.is_ge))
                dve.wait_ge(s("d_exp"), c + 1)
                ch.link(dve.tensor_tensor(t1, t1, ev, ALU.mult))
                ch.link(dve.tensor_reduce(w, t1, AX, ALU.add))
                ch.link(dve.reciprocal(w, w))
            ch.link(dve.tensor_tensor(t1, oh1, oh2, ALU.add))
            ch.link(dve.tensor_scalar(t2, t1, validf[:, 2:3], None, ALU.mult))
            last = lambda a: a.rearrange("p (b t) e -> p b t e", b=B)[:, :, CT - 1]
            dve.tensor_scalar(last(t2), last(t1), validf[:, 3:4], None, ALU.mult).then_inc(s("d_hot"), 1)
            dve.wait_ge(s("d_cnt"), 1)
            cnt = bank(1)[:, 0:QT * E].rearrange("p (q e) -> p q e", q=QT)
            ch.link(dve.tensor_copy(sa, cnt))
            src, dst, sh = sa, sc_, 1
            while sh < QT:
                ch.step(dve.tensor_copy(dst[:, 0:sh], src[:, 0:sh]))
                ch.link(dve.tensor_tensor(dst[:, sh:], src[:, sh:], src[:, 0:QT - sh], ALU.add))
                src, dst, sh = dst, src, 2 * sh
            ch.step(dve.tensor_copy(n_e, src[:, QT - 1]))
            ch.link(dve.tensor_tensor(dst, src, cnt, ALU.subtract))
            ch.link(dve.tensor_tensor(dst, dst, bank(0)[:, 0:QT * E].rearrange("p (q e) -> p q e", q=QT), ALU.add))
            ch.link(dve.tensor_tensor(dst, dst, ec(ebase), ALU.add))
            for oh, sl in ((oh1, sl1), (oh2, sl2)):
                ch.link(dve.tensor_tensor(t1, oh, dst, ALU.mult))
                ch.link(dve.tensor_reduce(sl, t1, AX, ALU.add))
                ch.link(dve.tensor_copy(sl.bitcast(I32), sl))
            ch.link(dve.tensor_copy(n_pad[:, :].bitcast(I32), n_e))
            ch.link(dve.tensor_scalar(te.bitcast(I32), n_e, float(P - 1), None, ALU.add))
            ch.link(dve.tensor_scalar(te.bitcast(I32), te.bitcast(I32), 7, None, ALU.logical_shift_right))
            ch.link(dve.tensor_copy(nt, te.bitcast(I32)))
            ch.link(dve.tensor_copy(te, nt))
            src, dst, sh = te, tb, 1
            while sh < E:
                ch.step(dve.tensor_copy(dst[:, 0:sh], src[:, 0:sh]))
                ch.link(dve.tensor_tensor(dst[:, sh:], src[:, sh:], src[:, 0:E - sh], ALU.add))
                src, dst, sh = dst, src, 2 * sh
            ends = src
            ch.link(dve.tensor_tensor(tc, ends, nt, ALU.subtract))
            ch.link(dve.scalar_tensor_tensor(out=tc, in0=tc, scalar=-float(P), in1=ebase, op0=ALU.mult, op1=ALU.add))
            big = ex[:, 0, 0:NTILE * E].rearrange("p (t e) -> p t e", t=NTILE)
            tbc = lambda a: a.unsqueeze(2).to_broadcast([P, NTILE, E])
            tec = lambda a: a.unsqueeze(1).to_broadcast([P, NTILE, E])
            ch.link(dve.tensor_tensor(big, tbc(t_tau[:, :]), tec(ends), ALU.is_ge))
            ch.link(dve.tensor_reduce(t_eid[:, :], big, AX, ALU.add))
            ch.link(dve.tensor_scalar(t_a[:, :], t_eid[:, :], -float(E), None, ALU.add))
            ch.link(dve.tensor_tensor(big, tbc(t_a[:, :]), tec(ecol), ALU.is_equal))
            ch.link(dve.tensor_tensor(big, big, tec(tc), ALU.mult))
            ch.link(dve.tensor_reduce(t_row[:, :], big, AX, ALU.add))
            ch.link(dve.scalar_tensor_tensor(out=t_row[:, :], in0=t_tau[:, :], scalar=float(P), in1=t_row[:, :],
                                             op0=ALU.mult, op1=ALU.add))
            ch.link(dve.tensor_scalar(t_a[:, :], t_a[:, :], 0.0, None, ALU.is_equal))
            ch.link(dve.tensor_scalar(t_tau[:, :], t_row[:, :], -1.0, float(ZROW), ALU.mult, ALU.add))
            ch.link(dve.tensor_tensor(t_tau[:, :], t_tau[:, :], t_a[:, :], ALU.mult))
            ch.link(dve.tensor_tensor(t_row[:, :].bitcast(I32), t_row[:, :], t_tau[:, :], ALU.add))
            ch.link(dve.tensor_scalar(t_eid[:, :].bitcast(I32), t_eid[:, :], float(E - 1), None, ALU.min))
            dve.memset(t_a[:, 0:1], 0.0).then_inc(s("d_tab"), 1)
            with dve.Fori(0, B) as b:
                ch.enter(b, CT * 5)
                for t in range(CT):
                    rows = TO if t < CT - 1 else LAST
                    q, v = CT * b + t, t % 3
                    dve.wait_ge(s(f"d_x_in{v}"), 32 * use3(b, t))
                    for c, (w, slt) in enumerate(((w1, sl1), (w2, sl2))):
                        ch.step(dve.tensor_copy(xd[0:rows, v, c, D:D + 1], w[0:rows, bass.ds(q, 1)]))
                        ch.step(dve.tensor_scalar(xd[0:rows, v, c, D + 1:D + 2].bitcast(I32),
                                                  tokid[0:rows, bass.ds(q, 1)].bitcast(I32), float(TOK * c), None, ALU.add))
                        ins = dve.tensor_copy(idx[0:rows, 2 * v + c:2 * v + c + 1].bitcast(I32),
                                              slt[0:rows, bass.ds(q, 1)].bitcast(I32))
                        if c == 0:
                            ch.link(ins)
                        else:
                            ch.sync()
                            ins.then_inc(s("d_meta"), 1)
                ch.leave(B)
            def expert_tiles(i, first):
                for u in range(2):
                    dve.wait_ge(s(f"m_sil{u}"), i + 1)
                    dve.wait_ge(s(f"m_up{u}"), 1 + i + 1)
                    dve.wait_ge(s(f"m_htp{u}"), 1 + i)
                    dve.tensor_tensor(hid[:, u], sil[:, u], bank(2 + u), ALU.mult).then_inc(s(f"m_hid{u}"), 1)
                    dve.wait_ge(s(f"m_down{u}"), 1 + i + 1)
                    if not first:
                        dve.wait_ge(s(f"m_sc{u}"), 16 * i)
                    dve.tensor_scalar(ys[:, u], bank(5)[:, 0:D], xs[:, u, D:D + 1], None, ALU.mult)\
                       .then_inc(s(f"m_y{u}"), 1)

            expert_tiles(0, True)
            with dve.Fori(1, NTILE // 2) as i:
                expert_tiles(i, False)
            for k in range(CH):
                dve.wait_ge(s(f"f_in{k % 2}"), 48 * (k // 2 + 1))
                dve.tensor_tensor(fin[:, k % 2, 1], fin[:, k % 2, 0], fin[:, k % 2, 1], ALU.add).then_inc(s("f_sum1"), 1)

        @block.tensor
        def _(pe):
            pe.wait_ge(s("consts"), 1)
            idt = ident[:, :]
            with pe.Fori(0, B) as b:
                pe.wait_ge(s("a_xnt"), 1 + 4 * b)
                for half in range(2):
                    for k in range(KD):
                        for t in range(4):
                            if k == 0:
                                pe.wait_ge(s("a_xn"), RT * b + 4 * half + t + 1)
                            mm = pe.transpose(bank(2 * k + half)[:, t * P:(t + 1) * P],
                                              xnb[:, 4 * half + t, k * P:(k + 1) * P], idt)
                        mm.then_inc(s("a_tp"), 1)
            pe.wait_ge(s("a_lm"), 1 + KD * B)
            pe.wait_ge(s("a_xnt"), 1 + 4 * B)
            pe.wait_ge(s("w_qk_in"), 16)
            for j in range(J):
                for c in range(2):
                    n = 2 * j + c
                    if n >= 8:
                        for e_ in ("act", "dve"):
                            pe.wait_ge(s(f"b_{'qk'[c]}_{e_}"), j - 3)
                    for k in range(KD):
                        mm = pe.matmul(bank(n % 8)[:, 0:B * M], wqk[:, k, c * INNER + j * P:c * INNER + (j + 1) * P],
                                       xm[:, k], start=(k == 0), stop=(k == KD - 1))
                    mm.then_inc(s("b_lm"), 1)
            for e_ in ("act", "dve"):
                pe.wait_ge(s(f"b_q_{e_}"), J)
            pe.wait_ge(s("b_kst"), 2)
            for g in range(B):
                for j in range(J):
                    mm = pe.matmul(bank(g)[:, j * M:(j + 1) * M], q_bd[:, j, g], k_st[:, j, g], start=True, stop=True)
                mm.then_inc(s("b_sim2"), 1)
            pe.wait_ge(s("b_a"), 2 * B)
            pe.wait_ge(s("b_sub"), B)
            for n in range(8):
                for q in range(4):
                    mm = pe.transpose(bank(n)[:, q * P:(q + 1) * P], zt[:, 4 * n + q], idt)
                mm.then_inc(s("b_at_tp"), 1)
            pe.wait_ge(s("w_in"), 16 * 5)
            pe.wait_ge(s("i_z0"), 2)

            def c1_sim(b, j):
                q, u = J * b + j, j % 2
                pe.wait_ge(s("c1_exp"), 1 + (q - 1 if j >= 1 else J * b))
                for half in range(2):
                    for k in range(KD):
                        mm = pe.matmul(bank(2 * u + half), g3[:, k, j * P:(j + 1) * P],
                                       xnt[:, k, HALO + 512 * half:HALO + 512 * half + 512],
                                       start=(k == 0), stop=(k == KD - 1))
                mm.then_inc(s("c1_sim"), 1)

            def c1_v3(b, j):
                q = J * b + j
                pe.wait_ge(s("c1_utb"), 1 + q + 1)
                pe.wait_ge(s("c1_v3"), 1 + 2 * q)
                for k in range(KD):
                    mm = pe.matmul(bank(7)[:, 0:P], utb[:, k], wv[:, k, j * P:(j + 1) * P],
                                   start=(k == 0), stop=(k == KD - 1))
                mm.then_inc(s("c1_v3mm"), 1)

            with pe.Fori(0, B) as b:
                pe.wait_ge(s("c1_exp"), 1 + J * b)
                for k in range(KD):
                    for j in range(J):
                        mm = pe.matmul(bank(2 * k, 2)[:, j * P:(j + 1) * P], wkt[:, j, k * P:(k + 1) * P],
                                       q_bd[:, j, b], start=True, stop=True)
                    mm.then_inc(s("c1_g3mm"), 1)
                pe.wait_ge(s("c1_g3"), KD * b + KD)
                pe.wait_ge(s("c1_xnt_in"), 16 * (b + 1))
                c1_sim(b, 0)
                for j in range(J):
                    u, q = j % 2, J * b + j
                    if j < J - 1:
                        c1_sim(b, j + 1)
                    pe.wait_ge(s("c1_exp"), 1 + q + 1)
                    pe.wait_ge(s("c1_e3a"), 1 + q)
                    pe.wait_ge(s("c1_e3b"), 1 + q)
                    for t in range(RT):
                        mm = pe.transpose(bank(4 + t // 4)[:, (t % 4) * P:(t % 4 + 1) * P],
                                          ex[:, u, t * P:(t + 1) * P], idt)
                    mm.then_inc(s("c1_tp"), 1)
                    if j >= 1:
                        c1_v3(b, j - 1)
                    else:
                        pe.wait_ge(s("c1_xn_in"), 16 * (b + 1))
                        pe.wait_ge(s("c1_utb"), 1 + q)
                    pe.wait_ge(s("c1_e3a"), 1 + q + 1)
                    pe.wait_ge(s("c1_e3b"), 1 + q + 1)
                    for k in range(KD):
                        for t in range(RT):
                            mm = pe.matmul(bank(6)[:, k * P:(k + 1) * P], xnb[:, t, k * P:(k + 1) * P], e3t[:, t],
                                           start=(t == 0), stop=(t == RT - 1))
                    mm.then_inc(s("c1_ut"), 1)
                c1_v3(b, J - 1)
            pe.wait_ge(s("c1_v3"), 1 + 2 * NQ)

            def products(lhs, rhs, waits, name):
                for g in range(4):
                    for w, n in waits:
                        pe.wait_ge(s(w), n + g)
                    for q in range(8 * g, 8 * g + 8):
                        o_ = ps[:, q * P:(q + 1) * P]
                        mm = pe.transpose(o_, lhs[:, q], idt) if rhs is None else \
                            pe.matmul(o_, lhs[:, q], rhs[:, q], start=True, stop=True)
                    mm.then_inc(s(name), 1)

            with pe.Fori(0, ITERS) as it:
                pe.wait_ge(s("i_zt"), 1 + 4 * it)
                products(att, z, (), "i_azmm")
                products(tt, None, (("i_t1", 4 * it + 1),), "i_t1tp")
                products(azt, tt, (("i_azt", 4 * it + 1),), "i_t1mm")
                products(azt, tt, (("i_t2", 4 * it + 1),), "i_t2mm")
                products(zt, tt, (("i_t3", 4 * it + 1),), "i_zmm")
                products(z, None, (("i_z", 4 * it + 1),), "i_ztp")
            pe.wait_ge(s("i_zt"), 1 + 4 * ITERS)
            for g in range(NQ // 4):
                if g >= 2:
                    pe.wait_ge(s("p_wt"), g - 1)
                for i in range(4):
                    q = 4 * g + i
                    mm = pe.matmul(bank(g % 2)[:, i * P:(i + 1) * P], v3[:, q // J, q % J], zt[:, q], start=True, stop=True)
                mm.then_inc(s("p_wt_mm"), 1)
                pe.wait_ge(s("p_wt"), g + 1)
                if g >= 2:
                    pe.wait_ge(s("p_pm"), g - 1)
                for i in range(4):
                    q = 4 * g + i
                    mm = pe.matmul(bank(2 + 2 * (g % 2), 2)[:, i * D:(i + 1) * D], wts[:, i], wfc[:, q % J],
                                   start=True, stop=True)
                mm.then_inc(s("p_mm"), 1)
            pe.wait_ge(s("p_pm"), NQ // 4)

            def c2_sim(b, t):
                q, u = CT * b + t, t % 2
                pe.wait_ge(s("c2_sub"), 1 + (q - 1 if t >= 1 else CT * b))
                for half in range(2):
                    for k in range(KD):
                        mm = pe.matmul(bank(2 * u + half), xnt[:, k, TO * t:TO * t + P], g1[:, k, 512 * half:512 * half + 512],
                                       start=(k == 0), stop=(k == KD - 1))
                mm.then_inc(s("c2_sim"), 1)

            def c2_tp(b, t):
                rows, u, q = (TO if t < CT - 1 else LAST), t % 2, CT * b + t
                pe.wait_ge(s("c2_x1n"), 1 + q + 1)
                pe.wait_ge(s("c2_lg"), 1 + q)
                for k in range(KD):
                    mm = pe.transpose(bank(7)[:, k * rows:(k + 1) * rows], x1n[0:rows, u, k * P:(k + 1) * P],
                                      ident[0:rows, 0:rows])
                mm.then_inc(s("c2_x1tp"), 1)

            def c2_lg(b, t):
                rows, q = (TO if t < CT - 1 else LAST), CT * b + t
                pe.wait_ge(s("c2_x1t"), q + 1)
                for k in range(KD):
                    mm = pe.matmul(bank(7)[0:rows, 256:256 + E], x1t[:, k, 0:rows], rw[:, k * E:(k + 1) * E],
                                   start=(k == 0), stop=(k == KD - 1))
                mm.then_inc(s("c2_lgmm"), 1)

            def c2_g1(b):
                for k in range(KD):
                    for j in range(J):
                        mm = pe.matmul(bank(2 * k, 2)[:, j * P:(j + 1) * P], wqt[:, j, k * P:(k + 1) * P],
                                       k_bd[:, j, b], start=True, stop=True)
                    mm.then_inc(s("c2_g1mm"), 1)

            pe.wait_ge(s("band_ok"), 1)
            with pe.Fori(0, B) as b:
                pe.wait_ge(s("c2_sub"), 1 + CT * b)
                c2_g1(b)
                pe.wait_ge(s("c2_g1"), KD * b + KD)
                pe.wait_ge(s("c2_xnt_in"), 16 * (b + 1))
                c2_sim(b, 0)
                for t in range(CT):
                    rows, u, q = (TO if t < CT - 1 else LAST), t % 2, CT * b + t
                    if t < CT - 1:
                        c2_sim(b, t + 1)
                    pe.wait_ge(s("c2_a1"), 1 + q + 1)
                    pe.wait_ge(s("c2_cvt"), 1 + q)
                    for h in range(H):
                        c = 64 * (h % 2)
                        mm = pe.matmul(bank(4, 2)[c:c + 64, (h // 2) * P:(h // 2) * P + TO], a1[:, u, h], band[:, h],
                                       start=True, stop=True)
                    mm.then_inc(s("c2_conv"), 1)
                    if t >= 2:
                        c2_tp(b, t - 2)
                    pe.wait_ge(s("c2_cvt"), 1 + q + 1)
                    if t >= 1:
                        pe.wait_ge(s(f"c2_x1_{1 - u}"), 1 + use2(b, t - 1))
                    else:
                        pe.wait_ge(s("c2_x1_0"), 1 + use2(b, 0) - 1)
                    for j in range(J):
                        mm = pe.matmul(bank(6)[0:rows, 0:D], cvt[:, u, j, 0:rows], pm[:, b, j],
                                       start=(j == 0), stop=(j == J - 1))
                    mm.then_inc(s("c2_y"), 1)
                    if t >= 2:
                        c2_lg(b, t - 2)
                for t in (CT - 2, CT - 1):
                    c2_tp(b, t)
                    c2_lg(b, t)
            pe.wait_ge(s("d_hot"), 1)
            hot = r_a[10].rearrange("p q e -> p (q e)")
            pe.matmul(bank(0)[:, 0:QT * E], tri[:, :], hot, start=True, stop=True)
            pe.matmul(bank(1)[:, 0:QT * E], ones[:, :], hot, start=True, stop=True).then_inc(s("d_cnt"), 1)
            pe.wait_ge(s("wgu_in"), 16 * KD)
            pe.wait_ge(s("wd_in"), 32)
            pe.wait_ge(s("d_tab"), 1)

            def xtp(i, u):
                pe.wait_ge(s(f"m_xs_in{u}"), 16 * (i + 1))
                for k in range(KD):
                    mm = pe.transpose(bank(6)[:, k * P:(k + 1) * P], xs[:, u, k * P:(k + 1) * P], idt)
                mm.then_inc(s(f"m_xtp{u}"), 1)

            with pe.Fori(0, NTILE // 2) as i:
                for u in range(2):
                    e = pe.value_load(t_eid[0:1, bass.ds(2 * i + u, 1)].bitcast(I32), min_val=0, max_val=E - 1)
                    xtp(i, u)
                    pe.wait_ge(s(f"m_xst{u}"), i + 1)
                    for k in range(KD):
                        mm = pe.matmul(bank(u), xst[:, u, k], w_gu_s[:, e, k, 0], start=(k == 0), stop=(k == KD - 1))
                    mm.then_inc(s(f"m_gate{u}"), 1)
                    for k in range(KD):
                        mm = pe.matmul(bank(2 + u), xst[:, u, k], w_gu_s[:, e, k, 1], start=(k == 0), stop=(k == KD - 1))
                    mm.then_inc(s(f"m_up{u}"), 1)
                    pe.wait_ge(s(f"m_hid{u}"), 1 + i + 1)
                    for f in range(4):
                        mm = pe.transpose(bank(4)[:, f * P:(f + 1) * P], hid[:, u, f * P:(f + 1) * P], idt)
                    mm.then_inc(s(f"m_htp{u}"), 1)
                    pe.wait_ge(s(f"m_ht{u}"), i + 1)
                    if u == 0:
                        pe.wait_ge(s("m_y1"), 1 + i)
                    else:
                        pe.wait_ge(s("m_y0"), 1 + i + 1)
                    for f in range(4):
                        mm = pe.matmul(bank(5)[:, 0:D], hidt[:, u, f], w_d_s[:, e, f], start=(f == 0), stop=(f == 3))
                    mm.then_inc(s(f"m_down{u}"), 1)


_OUT = (B, N, D)


def kernel(**inputs):
    import numpy as np
    import concourse.bacc as bacc
    from concourse.bass_utils import run_bass_kernel_spmd as run

    f = {k: np.asarray(v) for k, v in inputs.items()}
    wqkv = f["L0_attn_w_qkv"]
    taps = f["L0_attn_w_conv"].reshape(H, TAPS)
    band = np.zeros((H, P, TO), taps.dtype)
    for o in range(TO):
        band[:, o:o + TAPS, o] = taps
    gate_t = f["L0_ffn_w_gate"].transpose(0, 2, 1).reshape(E, KD, P, F)
    up_t = f["L0_ffn_w_up"].transpose(0, 2, 1).reshape(E, KD, P, F)
    arrays = {
        "x": f["L0_attn_x"],
        "w_qkv": wqkv,
        "wq_t": wqkv[:, 0:INNER].T,
        "wk_t": wqkv[:, INNER:2 * INNER].T,
        "conv_band": band,
        "w_fc": f["L0_attn_w_fc"],
        "b_fc": f["L0_attn_b_fc"],
        "router_t": f["L0_ffn_router_w"].T,
        "w_gu": np.stack([gate_t, up_t], axis=3),
        "w_down": f["L0_ffn_w_down"].transpose(0, 2, 1).reshape(E, 4, P, D).transpose(0, 2, 1, 3),
    }
    nc = bacc.Bacc("TRN2", target_bir_lowering=False, num_devices=1)
    args = []
    for name in list(arrays):
        arrays[name] = np.ascontiguousarray(arrays[name])
        args.append(nc.dram_tensor(name, arrays[name].shape, mybir.dt.from_np(arrays[name].dtype), kind="ExternalInput").ap())
    args.append(nc.dram_tensor("out", _OUT, F32, kind="ExternalOutput").ap())
    layer(nc, *args)
    r = run(nc, [arrays], core_ids=[0])
    return r.results[0]["out"]
```

```python
from contextlib import ExitStack

import concourse.bass as bass
from concourse import mybir

F32 = mybir.dt.float32
I32 = mybir.dt.int32
U32 = mybir.dt.uint32
ALU = mybir.AluOpType
ACT = mybir.ActivationFunctionType
AX = mybir.AxisListType.X

P = 128
B, N, D = 4, 1024, 256
H, DH, M = 16, 64, 64
INNER = H * DH
J = H // 2
KD = D // P
RT = N // P
ITERS = 6
TAPS = 13
HALO = TAPS // 2
TO = P - 2 * HALO
CT = -(-N // TO)
LAST = N - (CT - 1) * TO
PADN = (CT - 1) * TO + P
NQ = B * J
EPS = 1e-5
E, F = 8, 512
JITTER2 = 0.02
TOK = B * N
REGION = TOK + P
ZROW = E * REGION
NTILE = (2 * TOK + E * (P - 1)) // P + 1
NTILE += -NTILE % 4
ROW = D + 4
QT = B * CT
RSQRT_MAGIC = float(0x5F3759DF)
BIG = 3.0e38
CH = 8
STARTED = (
    "a_x_used", "c1_sim", "c1_ut", "c2_sim", "c2_x1_0", "c2_x1_1", "c2_conv", "x1n_out0",
    "x1n_out1", "c2_x1tp", "a_xnt_out", "a_lm", "c1_tp", "c1_v3mm", "c2_y", "c2_lgmm",
      "a_xn_out", "a_tp",
    "c1_exp", "c2_a1", "c2_x1n", "x1_out0", "x1_out1",  "a_xnt",
    "c1_e3b", "c1_e3a", "c1_utb", "c1_v3", "i_zt", "c2_sub", "c2_cvt", "c2_lg",
    
)


class Chain:

    def __init__(self, eng, sem):
        self.eng, self.sem, self.base, self.n = eng, sem, 0, 0

    def step(self, ins):
        ins.then_inc(self.sem, 1)
        self.n += 1

    def sync(self):
        self.eng.wait_ge(self.sem, self.base + self.n)

    def link(self, ins):
        self.step(ins)
        self.sync()

    def enter(self, i, per_turn):
        self.start, self.per_turn, self.n0 = self.base + self.n, per_turn, self.n
        self.base, self.n = self.start + i * per_turn, 0

    def leave(self, turns):
        assert self.n == self.per_turn, (self.n, self.per_turn)
        self.base, self.n = self.start + turns * self.per_turn, 0


def layer(nc, x, w_qkv, wq_t, wk_t, conv_band, w_fc, b_fc, router_t, w_gu, w_down, out):
    with ExitStack() as ctx:
        def sb(name, words):
            return ctx.enter_context(nc.sbuf_tensor(name, [P, words], F32))

        def sem(name):
            return ctx.enter_context(nc.semaphore(name))

        def dram(name, shape):
            return nc.dram_tensor(name, shape, F32, kind="Internal").ap()

        xn_d = dram("xn_d", (B, P, RT * D))
        xnt_d = dram("xnt_d", (B, P, KD * PADN))
        x1_d = dram("x1_d", (B, N, D))
        x1n_d = dram("x1n_d", (B, N, D))
        xs_d = dram("xs_d", (ZROW + P, ROW))
        yo_d = dram("yo_d", (2 * TOK, D))

        mem = sb("mem", 50500)

        def at(start, words):
            return mem[:, start:start + words]

        SQ = NQ * P
        zt = at(0, SQ).rearrange("p (q c) -> p q c", q=NQ)
        z = at(SQ, SQ).rearrange("p (q c) -> p q c", q=NQ)
        azt = at(2 * SQ, SQ).rearrange("p (q c) -> p q c", q=NQ)
        tt = at(3 * SQ, SQ).rearrange("p (q c) -> p q c", q=NQ)
        att = at(4 * SQ, SQ).rearrange("p (q c) -> p q c", q=NQ)
        xnb = at(5 * SQ, RT * D).rearrange("p (t c) -> p t c", t=RT)
        g3 = at(5 * SQ + RT * D, KD * INNER).rearrange("p (k c) -> p k c", k=KD)
        q_bd = at(6 * SQ, SQ).rearrange("p (j b c) -> p j b c", j=J, b=B)
        k_bd = at(7 * SQ, SQ).rearrange("p (j b c) -> p j b c", j=J, b=B)
        v3 = at(8 * SQ, SQ).rearrange("p (b j c) -> p b j c", b=B, j=J)
        o = 9 * SQ
        xnt = at(o, KD * PADN).rearrange("p (k n) -> p k n", k=KD); o += KD * PADN
        wqt = at(o, J * D).rearrange("p (j c) -> p j c", j=J); o += J * D
        wkt = at(o, J * D).rearrange("p (j c) -> p j c", j=J)
        xr = at(o, 2 * D).rearrange("p (u c) -> p u c", u=2)
        x1 = at(o + 2 * D, 2 * D).rearrange("p (u c) -> p u c", u=2)
        x1n = at(o + 4 * D, 2 * D).rearrange("p (u c) -> p u c", u=2)
        bfc = at(o + 6 * D, D)
        o += J * D
        wv = at(o, KD * INNER).rearrange("p (k c) -> p k c", k=KD)
        x1t = at(o, KD * P).rearrange("p (k c) -> p k c", k=KD)
        logits = at(o + KD * P, QT * E).rearrange("p (q e) -> p q e", q=QT)
        o += KD * INNER
        wfc = at(o, J * D).rearrange("p (j c) -> p j c", j=J); o += J * D
        ex = at(o, 2 * INNER).rearrange("p (u c) -> p u c", u=2); o += 2 * INNER
        e3t = at(o, RT * P).rearrange("p (t c) -> p t c", t=RT)
        wts = at(o, 4 * P).rearrange("p (s c) -> p s c", s=4)
        utb = at(o + RT * P, KD * P).rearrange("p (k c) -> p k c", k=KD)
        xm = at(5 * SQ + RT * D, KD * B * M).rearrange("p (k c) -> p k c", k=KD)
        o += RT * P + KD * P
        assert o <= 50500
        xb = at(0, RT * D).rearrange("p (t c) -> p t c", t=RT)
        wqk = at(2 * SQ, KD * 2 * INNER).rearrange("p (k c) -> p k c", k=KD)
        k_st = at(3 * SQ, J * B * M).rearrange("p (j b c) -> p j b c", j=J, b=B)
        sm2 = at(3 * SQ + 2048, NQ * M).rearrange("p (q c) -> p q c", q=NQ)
        w_gu_s = at(0, E * KD * 2 * F).rearrange("p (e k g f) -> p e k g f", e=E, k=KD, g=2)
        pm = at(4 * SQ, NQ * D).rearrange("p (b j c) -> p b j c", b=B, j=J)
        a1 = at(6 * SQ, 2 * INNER).rearrange("p (u h c) -> p u h c", u=2, h=H)
        cvt = at(6 * SQ + 2 * INNER, 2 * J * TO).rearrange("p (u j c) -> p u j c", u=2, j=J)
        g1 = at(8 * SQ, KD * INNER).rearrange("p (k c) -> p k c", k=KD)
        band = at(8 * SQ + KD * INNER, H * TO).rearrange("p (h c) -> p h c", h=H)
        w_d_s = at(6 * SQ, E * 4 * D).rearrange("p (e f c) -> p e f c", e=E, f=4)
        o = 8 * SQ
        def take(words):
            nonlocal o
            o += words
            return at(o - words, words)
        r_a = [take(QT * E).rearrange("p (q e) -> p q e", q=QT) for _ in range(11)]
        assert o < 9 * SQ + KD * PADN
        o = 8 * SQ
        xd = take(3 * 2 * ROW).rearrange("p (u c w) -> p u c w", u=3, c=2)
        o = 8 * SQ
        xs = take(4 * ROW).rearrange("p (u c) -> p u c", u=4)
        xst = take(2 * D).rearrange("p (u k c) -> p u k c", u=2, k=KD)
        sil = take(2 * F).rearrange("p (u c) -> p u c", u=2)
        hid = take(2 * F).rearrange("p (u c) -> p u c", u=2)
        hidt = take(2 * F).rearrange("p (u f c) -> p u f c", u=2, f=4)
        ys = take(4 * D).rearrange("p (u c) -> p u c", u=4)
        o = 0
        CW = TOK * D // P // CH
        fin = take(2 * 3 * CW).rearrange("p (u s c) -> p u s c", u=2, s=3)

        ident = sb("ident", P)
        eyes = sb("eyes", 3 * P)
        eye7, eye15, eye13 = (eyes[:, i * P:(i + 1) * P] for i in range(3))
        tri = sb("tri", P)
        ones = sb("ones", P)
        shift = sb("shift", TO)
        validf = sb("validf", 4)
        rw = sb("rw", KD * E)
        small = sb("small", 512)
        stats = small[:, 0:6 * RT].rearrange("p (t c) -> p t c", t=RT)
        mv = small[:, 48:48 + 2 * RT].rearrange("p (t c) -> p t c", t=RT)
        ve, rs, tmp = (small[:, 64 + 8 * i:72 + 8 * i] for i in range(3))
        mx = small[:, 96:128]
        sm = small[:, 128:160]
        ri = small[:, 160:192]
        zz = small[:, 192:200]
        mv2 = small[:, 200:204].rearrange("p (u c) -> p u c", u=2)
        st2 = small[:, 204:216].rearrange("p (u c) -> p u c", u=2)
        rs2 = small[:, 216:218]
        tm2 = small[:, 218:220]
        nmx = small[:, 220:222]
        s3 = small[:, 222:224]
        r3 = small[:, 224:226]
        idx = small[:, 226:232]
        ecol = small[:, 232:240]
        ebase = small[:, 240:248]
        n_e, nt, te, tb, tc = (small[:, 248 + 8 * i:256 + 8 * i] for i in range(5))
        mx2, sm2s, ri2 = (small[:, 288 + 32 * i:320 + 32 * i] for i in range(3))
        t_eid, t_row, t_a, t_tau = (sb(f"tab{i}", NTILE) for i in range(4))
        n_pad = sb("n_pad", E)
        route = sb("route", 8 * QT)
        m1, m2, i1, w1, w2, sl1, sl2, tokid = (route[:, i * QT:(i + 1) * QT] for i in range(8))
        pad = sb("pad", ROW)

        ps = ctx.enter_context(nc.psum_tensor("ps", [P, 8 * 512], F32))

        def bank(i, n=1):
            return ps[:, i * 512:(i + n) * 512]

        S = {}

        def s(name):
            if name not in S:
                S[name] = sem(name)
            return S[name]

        def use2(b, t):
            return ((CT + 1 - t % 2) // 2) * b + t // 2 + 1

        def use3(b, t):
            return (CT // 3) * b + t // 3 + 1

        def wait_alone(eng, name, count):
            eng.wait_ge(s(name), count)
            eng.sem_inc(s("passed"), 1)

        def c2_batches(eng, step, steps, ch=None, links=0):
            def body(b, first, last):
                def tile(op, k, t):
                    if t >= k:
                        if not last:
                            op(b, t - k)
                    elif not first:
                        op(b - 1, CT + t - k)
                for t in range(steps if last else CT):
                    step(b, t, lambda op, k: tile(op, k, t))

            body(0, True, False)
            with eng.Fori(1, B) as b:
                if ch:
                    ch.enter(b - 1, links)
                body(b, False, False)
                if ch:
                    ch.leave(B - 1)
            body(B, False, True)

        block = ctx.enter_context(nc.Block())
        x_t = x.rearrange("b (t p) c -> b p t c", p=P)

        @block.sync
        def _(sp):
            for name in STARTED:
                sp.sem_inc(s(name), 1)
            with sp.Fori(0, B) as b:
                sp.wait_ge(s("a_x_used"), 1 + b)
                sp.dma_start(xb, x_t[b]).then_inc(s("a_x_in"), 16)
                sp.wait_ge(s("a_xn"), RT * b + RT)
                sp.dma_start(xn_d[b].rearrange("p (t c) -> p t c", t=RT), xnb).then_inc(s("a_xn_out"), 16)
                sp.wait_ge(s("a_xnt"), 1 + 4 * b + 4)
                sp.dma_start(xnt_d[b].rearrange("p (k n) -> p k n", k=KD), xnt).then_inc(s("a_xnt_out"), 16)
            sp.dma_start(wqk, w_qkv[:, 0:2 * INNER].rearrange("(k p) c -> p k c", p=P)).then_inc(s("w_qk_in"), 16)
            sp.dma_start(wqt, wq_t.rearrange("(j p) c -> p j c", p=P)).then_inc(s("w_in"), 16)
            sp.dma_start(wkt, wk_t.rearrange("(j p) c -> p j c", p=P)).then_inc(s("w_in"), 16)
            sp.dma_start(wv, w_qkv[:, 2 * INNER:].rearrange("(k p) c -> p k c", p=P)).then_inc(s("w_in"), 16)
            sp.dma_start(wfc, w_fc.rearrange("(j p) c -> p j c", p=P)).then_inc(s("w_in"), 16)
            sp.dma_start(rw[:, :].rearrange("p (k e) -> p k e", k=KD),
                         router_t.rearrange("(k p) e -> p k e", p=P)).then_inc(s("w_in"), 16)
            sp.wait_ge(s("a_xn_out"), 1 + 16 * B)
            sp.wait_ge(s("a_xnt_out"), 1 + 16 * B)
            sp.wait_ge(s("a_lm"), 1 + KD * B)
            with sp.Fori(0, B) as b:
                sp.wait_ge(s("c1_sim"), 1 + J * b)
                sp.dma_start(xnt, xnt_d[b].rearrange("p (k n) -> p k n", k=KD)).then_inc(s("c1_xnt_in"), 16)
                sp.wait_ge(s("c1_ut"), 1 + J * b)
                sp.dma_start(xnb, xn_d[b].rearrange("p (t c) -> p t c", t=RT)).then_inc(s("c1_xn_in"), 16)
            sp.wait_ge(s("p_wt_mm"), NQ // 4)
            sp.dma_start(band, conv_band.rearrange("h p c -> p h c")).then_inc(s("band_in"), 16)
            sp.dma_start(bfc, b_fc.rearrange("(o c) -> o c", o=1).to_broadcast([P, D])).then_inc(s("bfc_in"), 16)
            for k in range(KD):
                sp.dma_start(w_gu_s[:, :, k], w_gu[:, k].rearrange("e p g f -> p e g f")).then_inc(s("wgu_in"), 16)
            sp.wait_ge(s("c1_sim"), 1 + J * B)

            def batch_columns(b, t):
                sp.wait_ge(s("c2_sim"), 1 + CT * b)
                sp.dma_start(xnt, xnt_d[b].rearrange("p (k n) -> p k n", k=KD)).then_inc(s("c2_xnt_in"), 16)

            def residual_rows(b, t):
                rows, u = (TO if t < CT - 1 else LAST), t % 2
                sp.wait_ge(s(f"c2_x1_{u}"), 1 + use2(b, t) - 1)
                sp.dma_start(xr[0:rows, u], x[b, TO * t:TO * t + rows, :]).then_inc(s(f"c2_xr_in{u}"), 16)

            def c2_loads(b, t, tile):
                if t == 0:
                    tile(batch_columns, 0)
                tile(residual_rows, 2)

            c2_batches(sp, c2_loads, 2)
            sp.wait_ge(s("c2_y"), 1 + QT)
            for e2 in range(2):
                sp.dma_start(w_d_s[:, 4 * e2:4 * e2 + 4], w_down[4 * e2:4 * e2 + 4].rearrange("e p f c -> p e f c"))\
                  .then_inc(s("wd_in"), 16)
            sp.wait_ge(s("d_tab"), 1)
            for e in range(E):
                n = sp.value_load(n_pad[0:1, e:e + 1].bitcast(I32), min_val=0, max_val=TOK)
                sp.dma_start(xs_d[bass.ds(n + e * REGION, P), :], pad[:, :]).then_inc(s("d_pad_out"), 16)
            sp.dma_start(xs_d[ZROW:ZROW + P, :], pad[:, :]).then_inc(s("d_pad_out"), 16)
            for u in range(2):
                sp.wait_ge(s(f"x1n_out{u}"), 1 + 16 * use2(B - 1, CT - 2 + (CT - u) % 2))
            def dispatch_rows(b, first):
                for t in range(CT):
                    rows, v = (TO if t < CT - 1 else LAST), t % 3
                    if not (first and t < 3):
                        sp.wait_ge(s(f"d_sc{v}"), 32 * (use3(b, t) - 1))
                    for c in range(2):
                        sp.dma_start(xd[0:rows, v, c, 0:D], x1n_d[b, TO * t:TO * t + rows, :])\
                          .then_inc(s(f"d_x_in{v}"), 16)

            dispatch_rows(0, True)
            with sp.Fori(1, B) as b:
                dispatch_rows(b, False)
            sp.wait_ge(s("d_pad_out"), 16 * (E + 1))
            for v in range(3):
                sp.wait_ge(s(f"d_sc{v}"), 32 * use3(B - 1, CT - 3 + v))
            def expert_rows(i, first):
                for v in range(4):
                    if not first:
                        sp.wait_ge(s(f"m_sc{v}"), 16 * i)
                    r = sp.value_load(t_row[0:1, bass.ds(4 * i + v, 1)].bitcast(I32), min_val=0, max_val=ZROW)
                    sp.dma_start(xs[:, v], xs_d[bass.ds(r, P), :]).then_inc(s(f"m_xs_in{v}"), 16)

            expert_rows(0, True)
            with sp.Fori(1, NTILE // 4) as i:
                expert_rows(i, False)
            for v in range(4):
                sp.wait_ge(s(f"m_sc{v}"), 16 * (NTILE // 4))
            for u in range(2):
                sp.wait_ge(s(f"x1_out{u}"), 1 + 16 * use2(B - 1, CT - 2 + (CT - u) % 2))
            x1f = x1_d.rearrange("b n c -> (b n c)").rearrange("(p k c) -> k p c", p=P, k=CH)
            yf = yo_d[0:2 * TOK, :].rearrange("(h n) c -> h (n c)", h=2).rearrange("h (p k c) -> h k p c", p=P, k=CH)
            of = out.rearrange("b n c -> (b n c)").rearrange("(p k c) -> k p c", p=P, k=CH)
            for k in range(CH):
                if k >= 2:
                    sp.wait_ge(s(f"f_out{k % 2}"), 16 * (k // 2))
                for c, src in enumerate((x1f[k], yf[0, k], yf[1, k])):
                    sp.dma_start(fin[:, k % 2, c], src).then_inc(s(f"f_in{k % 2}"), 16)
            for u in range(2):
                sp.wait_ge(s(f"f_out{u}"), 16 * CH // 2)

        @block.gpsimd
        def _(pool):
            ch = Chain(pool, s("pool_chain"))
            ch.link(pool.memset(ident[:, :], 0.0))
            ch.link(pool.affine_select(out=ident[:, :], in_=ident[:, :], compare_op=ALU.not_equal, fill=1.0,
                                       base=0, pattern=[[-1, P]], channel_multiplier=1))
            for eye, c in ((eye7, 7.0), (eye15, 15.0), (eye13, 13.0 / 4)):
                ch.link(pool.tensor_scalar(eye, ident[:, :], c, 0.0, ALU.mult, ALU.add))
            ch.link(pool.memset(ones[:, :], 1.0))
            ch.link(pool.memset(validf[:, :], 1.0))
            ch.link(pool.affine_select(out=tri[:, :], in_=ones[:, :], compare_op=ALU.is_gt, fill=0.0,
                                       base=0, pattern=[[1, P]], channel_multiplier=-1))
            ch.link(pool.affine_select(out=validf[:, 0:1], in_=validf[:, 0:1], compare_op=ALU.is_ge, fill=0.0,
                                       base=-HALO, pattern=[[0, 1]], channel_multiplier=1))
            ch.link(pool.affine_select(out=validf[:, 1:2], in_=validf[:, 1:2], compare_op=ALU.is_ge, fill=0.0,
                                       base=LAST + HALO - 1, pattern=[[0, 1]], channel_multiplier=-1))
            ch.link(pool.affine_select(out=validf[:, 2:3], in_=validf[:, 2:3], compare_op=ALU.is_ge, fill=0.0,
                                       base=TO - 1, pattern=[[0, 1]], channel_multiplier=-1))
            ch.link(pool.affine_select(out=validf[:, 3:4], in_=validf[:, 3:4], compare_op=ALU.is_ge, fill=0.0,
                                       base=LAST - 1, pattern=[[0, 1]], channel_multiplier=-1))
            ch.link(pool.memset(shift[:, :], 0.0))
            ch.link(pool.affine_select(out=shift[:, :], in_=shift[:, :], compare_op=ALU.not_equal, fill=1.0,
                                       base=-HALO, pattern=[[-1, TO]], channel_multiplier=1))
            ch.link(pool.iota(ecol.bitcast(I32), pattern=[[1, E]], base=-E, channel_multiplier=0))
            ch.link(pool.iota(ebase.bitcast(I32), pattern=[[REGION, E]], base=0, channel_multiplier=0))
            ch.link(pool.iota(t_tau[:, :].bitcast(I32), pattern=[[1, NTILE]], base=0, channel_multiplier=0))
            ch.link(pool.iota(tokid.bitcast(I32), pattern=[[N, B], [TO, CT]], base=0, channel_multiplier=1))
            ch.link(pool.memset(pad[:, :], 0.0))
            ch.link(pool.iota(pad[:, D + 1:D + 2].bitcast(I32), pattern=[[0, 1]], base=2 * TOK, channel_multiplier=1))
            ch.link(pool.memset(xnt[:, :, 0:HALO], 0.0))
            ch.link(pool.memset(xnt[:, :, HALO + N:PADN], 0.0))
            ch.link(pool.memset(q_bd[0:64, :, :, 64:128], 0.0))
            ch.link(pool.memset(q_bd[64:128, :, :, 0:64], 0.0))
            ch.link(pool.memset(k_bd[0:64, :, :, 64:128], 0.0))
            ch.link(pool.memset(k_bd[64:128, :, :, 0:64], 0.0))
            ch.link(pool.memset(v3[0:64, :, :, 64:128], 0.0))
            ch.sync()
            pool.memset(v3[64:128, :, :, 0:64], 0.0).then_inc(s("consts"), 1)
            pool.wait_ge(s("a_x_used"), 1 + B)
            ch.link(pool.memset(zt[0:64, :, 64:128], 0.0))
            ch.sync()
            pool.memset(zt[64:128, :, 0:64], 0.0).then_inc(s("zt_zero"), 1)
            pool.wait_ge(s("b_k_act"), J)
            pool.wait_ge(s("b_k_dve"), J)
            pool.tensor_copy(k_st[0:64], k_bd[0:64, :, :, 0:64]).then_inc(s("b_kst"), 1)
            pool.tensor_copy(k_st[64:128], k_bd[64:128, :, :, 64:128]).then_inc(s("b_kst"), 1)
            pool.wait_ge(s("b_sums"), 2)
            pool.partition_all_reduce(zz[:, 2:4], zz[:, 0:2], P, bass.bass_isa.ReduceOp.max).then_inc(s("b_gmax"), 1)
            pool.wait_ge(s("band_in"), 16)
            pool.tensor_tensor(band, band, shift[:, :].unsqueeze(1).to_broadcast([P, H, TO]), ALU.add)\
                .then_inc(s("band_ok"), 1)
            pool.wait_ge(s("bfc_in"), 16)

            def norm_rows(b, t):
                rows, u, q = (TO if t < CT - 1 else LAST), t % 2, CT * b + t
                pool.wait_ge(s("c2_guess"), q + 1)
                v, r, w = zz[:, 4 + u:5 + u], rs2[:, u:u + 1], tm2[:, u:u + 1]
                for n in range(3):
                    ch.link(pool.tensor_tensor(w, r, r, ALU.mult))
                    ch.step(pool.tensor_tensor(w, w, v, ALU.mult))
                    wait_alone(pool, "pool_chain", ch.base + ch.n)
                    ch.link(pool.tensor_scalar(w, w, -0.5, 1.5, ALU.mult, ALU.add))
                    ch.step(pool.tensor_tensor(r, r, w, ALU.mult))
                    ch.sync()
                pool.wait_ge(s(f"x1n_out{u}"), 1 + 16 * (use2(b, t) - 1))
                wait_alone(pool, "c2_x1tp", 1 + (q - 1 if t >= 1 else CT * b))
                pool.tensor_scalar(x1n[0:rows, u], x1[0:rows, u], mv2[0:rows, u, 0:1], rs2[0:rows, u:u + 1],
                                   ALU.subtract, ALU.mult).then_inc(s("c2_x1n"), 1)

            def add_bias(b, t):
                rows, u = (TO if t < CT - 1 else LAST), t % 2
                pool.wait_ge(s(f"c2_xr_in{u}"), 16 * use2(b, t))
                pool.tensor_tensor(xr[0:rows, u], xr[0:rows, u], bfc[0:rows], ALU.add).then_inc(s("c2_xrb"), 1)

            def weigh(b, t):
                u, q = t % 2, CT * b + t
                pool.wait_ge(s("c2_rinv"), q + 1)
                pool.wait_ge(s("c2_conv"), 1 + (q - 1 if t >= 1 else CT * b))
                pool.tensor_tensor(a1[:, u], ex[:, u].rearrange("p (h c) -> p h c", h=H),
                                   ri[:, 16 * u:16 * u + 16].unsqueeze(2).to_broadcast([P, H, M]),
                                   ALU.mult).then_inc(s("c2_a1"), 1)

            def c2_pool(b, t, tile):
                tile(weigh, 0)
                tile(add_bias, 2)
                tile(norm_rows, 3)

            c2_batches(pool, c2_pool, 3, ch, 12 * CT)
            with pool.Fori(0, B) as b:
                for t in range(CT):
                    rows = TO if t < CT - 1 else LAST
                    wait_alone(pool, "d_meta", CT * b + t + 1)
                    for c in range(2):
                        k = 2 * (t % 3) + c
                        pool.indirect_dma_start(
                            out=xs_d, out_offset=bass.IndirectOffsetOnAxis(ap=idx[0:rows, k:k + 1].bitcast(U32), axis=0),
                            in_=xd[0:rows, t % 3, c], in_offset=None).then_inc(s(f"d_sc{t % 3}"), 16)
            with pool.Fori(0, NTILE // 4) as i:
                for v in range(4):
                    wait_alone(pool, "m_y", 4 * i + v + 1)
                    pool.indirect_dma_start(
                        out=yo_d, out_offset=bass.IndirectOffsetOnAxis(ap=xs[:, v, D + 1:D + 2].bitcast(U32), axis=0),
                        in_=ys[:, v], in_offset=None, bounds_check=2 * TOK - 1, oob_is_err=False)\
                        .then_inc(s(f"m_sc{v}"), 16)
            for k in range(CH):
                pool.wait_ge(s("f_sum1"), k + 1)
                pool.tensor_tensor(fin[:, k % 2, 0], fin[:, k % 2, 1], fin[:, k % 2, 2], ALU.add).then_inc(s("f_sum"), 1)

        @block.scalar
        def _(act):
            act.wait_ge(s("consts"), 1)
            with act.Fori(0, B) as b:
                act.wait_ge(s("a_xnt_out"), 1 + 16 * b)
                act.wait_ge(s("a_lm"), 1 + KD * b)
                for g in range(4):
                    half, k = g // 2, g % 2
                    act.wait_ge(s("a_tp"), 1 + 4 * b + g + 1)
                    act.activation(xnt[:, k, HALO + 512 * half:HALO + 512 * half + 512], bank(2 * k + half),
                                   ACT.Copy).then_inc(s("a_xnt"), 1)
            for j in range(J):
                act.wait_ge(s("b_lm"), 2 * j + 1)
                act.activation(q_bd[0:64, j, :, 0:64], bank(2 * j % 8)[0:64, 0:B * M].rearrange("p (b m) -> p b m", b=B),
                               ACT.Copy, scale=DH ** -0.5 / (N // M)).then_inc(s("b_q_act"), 1)
                act.wait_ge(s("b_lm"), 2 * j + 2)
                act.activation(k_bd[0:64, j, :, 0:64], bank((2 * j + 1) % 8)[0:64, 0:B * M].rearrange("p (b m) -> p b m", b=B),
                               ACT.Copy, scale=1.0 / (N // M)).then_inc(s("b_k_act"), 1)
            for g in range(B):
                act.wait_ge(s("b_sub"), g + 1)
                act.activation(sm2[:, J * g:J * g + J], sm2[:, J * g:J * g + J], ACT.Exp).then_inc(s("b_exp"), 1)
            for g in range(4):
                act.wait_ge(s("b_at_tp"), 2 * g + 1)
                act.activation(att[:, 8 * g:8 * g + 4], bank(2 * g).rearrange("p (q c) -> p q c", q=4),
                               ACT.Copy).then_inc(s("b_at_act"), 1)
            def c1_tail(b, j):
                q = J * b + j
                act.wait_ge(s("c1_ut"), 1 + q + 1)
                act.wait_ge(s("c1_v3mm"), 1 + q)
                act.activation(utb, bank(6)[:, 0:KD * P].rearrange("p (k c) -> p k c", k=KD), ACT.Copy)\
                   .then_inc(s("c1_utb"), 1)

            with act.Fori(0, B) as b:
                for k in range(KD):
                    act.wait_ge(s("c1_g3mm"), 2 * b + k + 1)
                    act.activation(g3[:, k], bank(2 * k, 2), ACT.Copy).then_inc(s("c1_g3"), 1)
                for j in range(J):
                    u, q = j % 2, J * b + j
                    act.wait_ge(s("c1_nmx"), q + 1)
                    act.wait_ge(s("c1_tp"), 1 + (q - 1 if j >= 1 else J * b))
                    act.activation(ex[:, u], bank(2 * u, 2), ACT.Exp, bias=nmx[:, u:u + 1],
                                   accum_out=s3[:, u:u + 1]).then_inc(s("c1_exp"), 1)
                    if j >= 1:
                        c1_tail(b, j - 1)
                    act.wait_ge(s("c1_tp"), 1 + q + 1)
                    act.wait_ge(s("c1_ut"), 1 + q)
                    act.activation(e3t[:, 0:4], bank(4).rearrange("p (t c) -> p t c", t=4), ACT.Copy)\
                       .then_inc(s("c1_e3a"), 1)
                c1_tail(b, J - 1)
            with act.Fori(0, ITERS) as it:
                for g in range(4):
                    act.wait_ge(s("i_zmm"), 4 * it + g + 1)
                    act.activation(z[:, 8 * g:8 * g + 8], bank(2 * g, 2).rearrange("p (q c) -> p q c", q=8),
                                   ACT.Copy).then_inc(s("i_z"), 1)
                for g in range(4):
                    act.wait_ge(s("i_ztp"), g + 1 + 4 * it)
                    act.activation(zt[:, 8 * g:8 * g + 8], bank(2 * g, 2).rearrange("p (q c) -> p q c", q=8),
                                   ACT.Copy).then_inc(s("i_zt"), 1)
            for g in range(NQ // 4):
                act.wait_ge(s("p_wt_mm"), g + 1)
                act.wait_ge(s("p_mm"), g)
                act.activation(wts, bank(g % 2).rearrange("p (s c) -> p s c", s=4), ACT.Copy).then_inc(s("p_wt"), 1)
                act.wait_ge(s("p_mm"), g + 1)
                act.activation(pm[:, g // 2, 4 * (g % 2):4 * (g % 2) + 4],
                               bank(2 + 2 * (g % 2), 2).rearrange("p (s c) -> p s c", s=4), ACT.Copy)\
                   .then_inc(s("p_pm"), 1)
            def store_rows(b, t):
                rows, u, q = (TO if t < CT - 1 else LAST), t % 2, CT * b + t
                act.wait_ge(s(f"c2_x1_{u}"), 1 + use2(b, t))
                act.dma_start(x1_d[b, TO * t:TO * t + rows, :], x1[0:rows, u]).then_inc(s(f"x1_out{u}"), 16)

            def store_norm(b, t):
                rows, u, q = (TO if t < CT - 1 else LAST), t % 2, CT * b + t
                act.wait_ge(s("c2_x1n"), 1 + q + 1)
                act.dma_start(x1n_d[b, TO * t:TO * t + rows, :], x1n[0:rows, u]).then_inc(s(f"x1n_out{u}"), 16)

            def norm_columns(b, t):
                rows, q = (TO if t < CT - 1 else LAST), CT * b + t
                act.wait_ge(s("c2_x1tp"), 1 + q + 1)
                act.wait_ge(s("c2_lgmm"), 1 + q)
                act.activation(x1t[:, :, 0:rows], bank(7)[:, 0:KD * rows].rearrange("p (k c) -> p k c", k=KD),
                               ACT.Copy).then_inc(s("c2_x1t"), 1)

            def g1_out(b, t):
                for k in range(KD):
                    act.wait_ge(s("c2_g1mm"), 2 * b + k + 1)
                    act.activation(g1[:, k], bank(2 * k, 2), ACT.Copy, scale=DH ** -0.5).then_inc(s("c2_g1"), 1)

            def exponentials(b, t):
                act.wait_ge(s("c2_sub"), 1 + CT * b + t + 1)
                act.activation(ex[:, t % 2], ex[:, t % 2], ACT.Exp).then_inc(s("c2_exp"), 1)

            def conv_out(b, t):
                u, q = t % 2, CT * b + t
                act.wait_ge(s("c2_conv"), 1 + q + 1)
                act.wait_ge(s("c2_y"), 1 + (q - 1 if t >= 1 else CT * b))
                act.activation(cvt[:, u], bank(4, 2).rearrange("p (j c) -> p j c", j=J)[:, :, 0:TO],
                               ACT.Copy).then_inc(s("c2_cvt"), 1)

            def c2_act(b, t, tile):
                if t > 0:
                    tile(exponentials, 0)
                tile(norm_columns, 5)
                tile(conv_out, 1)
                if t == 0:
                    tile(g1_out, 0)
                    tile(exponentials, 0)
                tile(store_rows, 3)
                tile(store_norm, 4)

            c2_batches(act, c2_act, 5)
            for c in range(2):
                act.wait_ge(s("d_gap"), c + 1)
                act.activation(r_a[4 + c], r_a[4 + c], ACT.Exp, scale=-1.0).then_inc(s("d_exp"), 1)
            def xs_columns(n, v, free):
                act.wait_ge(s("m_xtp"), n + 1)
                if not free:
                    act.wait_ge(s("m_up"), n - 1)
                act.activation(xst[:, v % 2], bank(6)[:, 0:D].rearrange("p (k c) -> p k c", k=KD), ACT.Copy)\
                   .then_inc(s("m_xst"), 1)

            def hidden_columns(n, v, free):
                act.wait_ge(s("m_htp"), n + 1)
                if not free:
                    act.wait_ge(s("m_down"), n - 1)
                act.activation(hidt[:, v % 2], bank(4).rearrange("p (f c) -> p f c", f=4), ACT.Copy)\
                   .then_inc(s("m_ht"), 1)

            def expert_tiles(i, first, last):
                for v in range(4):
                    n = 4 * i + v
                    act.wait_ge(s("m_gate"), n + 1)
                    if not (first and v < 2):
                        act.wait_ge(s("m_hid"), n - 1)
                    act.activation(sil[:, v % 2], bank(v % 2), ACT.Silu).then_inc(s("m_sil"), 1)
                    if not (first and v == 0):
                        hidden_columns(n - 1, v + 3, first and v < 3)
                    if not (last and v == 3):
                        xs_columns(n + 1, v + 1, first and v == 0)

            xs_columns(0, 0, True)
            expert_tiles(0, True, False)
            with act.Fori(1, NTILE // 4 - 1) as i:
                expert_tiles(i, False, False)
            expert_tiles(NTILE // 4 - 1, False, True)
            hidden_columns(NTILE - 1, 3, False)
            for k in range(CH):
                act.wait_ge(s("f_sum"), k + 1)
                act.dma_start(out.rearrange("b n c -> (b n c)").rearrange("(p k c) -> k p c", p=P, k=CH)[k],
                              fin[:, k % 2, 0]).then_inc(s(f"f_out{k % 2}"), 16)

        @block.vector
        def _(dve):
            ch = Chain(dve, s("dve_chain"))
            dve.wait_ge(s("consts"), 1)
            with dve.Fori(0, B) as b:
                ch.enter(b, 2 * RT + 11)
                dve.wait_ge(s("a_x_in"), 16 * (b + 1))
                for t in range(RT):
                    ch.step(dve.bn_stats(stats[:, t], xb[:, t]))
                wait_alone(dve, "dve_chain", ch.base + ch.n)
                for t in range(RT):
                    ch.step(dve.bn_aggr(mv[:, t], stats[:, t]))
                ch.sync()
                ch.link(dve.tensor_scalar(ve, mv[:, :, 1], EPS, None, ALU.add))
                ch.link(dve.tensor_scalar(rs.bitcast(I32), ve.bitcast(I32), -0.5, RSQRT_MAGIC, ALU.mult, ALU.add))
                for _ in range(3):
                    ch.link(dve.tensor_tensor(tmp, rs, rs, ALU.mult))
                    ch.link(dve.scalar_tensor_tensor(out=tmp, in0=tmp, scalar=-0.5, in1=ve, op0=ALU.mult, op1=ALU.mult))
                    ch.link(dve.scalar_tensor_tensor(out=rs, in0=tmp, scalar=1.5, in1=rs, op0=ALU.add, op1=ALU.mult))
                dve.wait_ge(s("a_xn_out"), 1 + 16 * b)
                dve.wait_ge(s("a_tp"), 1 + 4 * b)
                for t in range(RT):
                    dve.tensor_scalar(xnb[:, t], xb[:, t], mv[:, t, 0:1], rs[:, t:t + 1], ALU.subtract, ALU.mult)\
                       .then_inc(s("a_xn"), 1)
                dve.wait_ge(s("a_xn"), RT * b + RT)
                dve.memset(tmp[:, 0:1], 0.0).then_inc(s("a_x_used"), 1)
                for k in range(KD):
                    dve.wait_ge(s("a_xnt"), 1 + 4 * b + 4)
                    dve.tensor_reduce(xm[:, k, bass.ds(M * b, M)],
                                      xnt[:, k, HALO:HALO + N].rearrange("p (m l) -> p m l", m=M), AX, ALU.add)\
                       .then_inc(s("a_lm"), 1)
                ch.leave(B)
            for j in range(J):
                dve.wait_ge(s("b_lm"), 2 * j + 1)
                dve.tensor_scalar(q_bd[64:128, j, :, 64:128], bank(2 * j % 8)[64:128, 0:B * M].rearrange("p (b m) -> p b m", b=B),
                                  DH ** -0.5 / (N // M), None, ALU.mult).then_inc(s("b_q_dve"), 1)
                dve.wait_ge(s("b_lm"), 2 * j + 2)
                dve.tensor_scalar(k_bd[64:128, j, :, 64:128],
                                  bank((2 * j + 1) % 8)[64:128, 0:B * M].rearrange("p (b m) -> p b m", b=B),
                                  1.0 / (N // M), None, ALU.mult).then_inc(s("b_k_dve"), 1)
            for g in range(B):
                sl = slice(J * g, J * g + J)
                dve.wait_ge(s("b_sim2"), g + 1)
                pg = bank(g).rearrange("p (q c) -> p q c", q=J)
                ch.link(dve.tensor_reduce(mx2[:, sl], pg, AX, ALU.max))
                dve.tensor_tensor(sm2[:, sl], pg, mx2[:, sl].unsqueeze(2).to_broadcast([P, J, M]), ALU.subtract)\
                   .then_inc(s("b_sub"), 1)
            dve.wait_ge(s("zt_zero"), 1)
            for g in range(B):
                sl = slice(J * g, J * g + J)
                dve.wait_ge(s("b_exp"), g + 1)
                ch.link(dve.tensor_reduce(sm2s[:, sl], sm2[:, sl], AX, ALU.add))
                ch.link(dve.reciprocal(ri2[:, sl], sm2s[:, sl]))
                for hf in range(2):
                    r = slice(64 * hf, 64 * hf + 64)
                    dve.tensor_tensor(zt[r, sl, 64 * hf:64 * hf + 64], sm2[r, sl],
                                      ri2[r, sl].unsqueeze(2).to_broadcast([64, J, M]), ALU.mult).then_inc(s("b_a"), 1)
            dve.wait_ge(s("b_a"), 2 * B)
            ch.link(dve.tensor_reduce(mx2, zt, AX, ALU.add))
            dve.tensor_reduce(zz[:, 0:1], mx2, AX, ALU.max).then_inc(s("b_sums"), 1)
            for g in range(4):
                dve.wait_ge(s("b_at_tp"), 2 * g + 2)
                ch.step(dve.tensor_copy(att[:, 8 * g + 4:8 * g + 8], bank(2 * g + 1).rearrange("p (q c) -> p q c", q=4)))
            ch.sync()
            dve.wait_ge(s("b_at_act"), 4)
            ch.link(dve.tensor_reduce(sm2s, att, AX, ALU.add))
            dve.tensor_reduce(zz[:, 1:2], sm2s, AX, ALU.max).then_inc(s("b_sums"), 1)
            dve.wait_ge(s("b_gmax"), 1)
            ch.link(dve.tensor_tensor(zz[:, 0:1], zz[:, 2:3], zz[:, 3:4], ALU.mult))
            ch.link(dve.reciprocal(zz[:, 1:2], zz[:, 0:1]))
            dve.tensor_scalar(z, att, zz[:, 1:2], None, ALU.mult).then_inc(s("i_z0"), 1)
            dve.tensor_scalar(zt, zt, zz[:, 1:2], None, ALU.mult).then_inc(s("i_z0"), 1)

            def c1_tail(b, j):
                q, u = J * b + j, j % 2
                dve.wait_ge(s("c1_v3mm"), 1 + q + 1)
                for hf in range(2):
                    r = slice(64 * hf, 64 * hf + 64)
                    dve.tensor_scalar(v3[r, b, j, 64 * hf:64 * hf + 64], bank(7)[r, 64 * hf:64 * hf + 64],
                                      r3[r, u:u + 1], None, ALU.mult).then_inc(s("c1_v3"), 1)

            with dve.Fori(0, B) as b:
                ch.enter(b, 2 * J)
                for j in range(J):
                    u, q = j % 2, J * b + j
                    dve.wait_ge(s("c1_sim"), 1 + q + 1)
                    ch.link(dve.tensor_reduce(mx[:, u:u + 1], bank(2 * u, 2), AX, ALU.max))
                    dve.wait_ge(s("c1_exp"), 1 + (q - 1 if j >= 1 else J * b))
                    dve.tensor_scalar(nmx[:, u:u + 1], mx[:, u:u + 1], -1.0, None, ALU.mult).then_inc(s("c1_nmx"), 1)
                    dve.wait_ge(s("c1_tp"), 1 + q + 1)
                    dve.wait_ge(s("c1_ut"), 1 + q)
                    dve.tensor_copy(e3t[:, 4:8], bank(5).rearrange("p (t c) -> p t c", t=4)).then_inc(s("c1_e3b"), 1)
                    if j >= 1:
                        c1_tail(b, j - 1)
                    dve.wait_ge(s("c1_exp"), 1 + q + 1)
                    ch.link(dve.reciprocal(r3[:, u:u + 1], s3[:, u:u + 1]))
                c1_tail(b, J - 1)
                ch.leave(B)
            def bracket(name_in, count, g, c, eye, dst, name_out):
                dve.wait_ge(s(name_in), count)
                dve.scalar_tensor_tensor(out=dst[:, 8 * g:8 * g + 8], in0=bank(2 * g, 2).rearrange("p (q c) -> p q c", q=8),
                                         scalar=c, in1=eye.unsqueeze(1).to_broadcast([P, 8, P]),
                                         op0=ALU.mult, op1=ALU.add).then_inc(s(name_out), 1)

            with dve.Fori(0, ITERS) as it:
                for g in range(4):
                    bracket("i_azmm", 4 * it + g + 1, g, -1.0, eye7, tt, "i_t1")
                for g in range(4):
                    bracket("i_t1tp", 4 * it + g + 1, g, -1.0, eye7, azt, "i_azt")
                for g in range(4):
                    bracket("i_t1mm", 4 * it + g + 1, g, -1.0, eye15, tt, "i_t2")
                for g in range(4):
                    bracket("i_t2mm", 4 * it + g + 1, g, -0.25, eye13, tt, "i_t3")

            def rows_out(b, t):
                rows, u, q = (TO if t < CT - 1 else LAST), t % 2, CT * b + t
                dve.wait_ge(s("c2_y"), 1 + q + 1)
                dve.wait_ge(s("c2_xrb"), q + 1)
                dve.wait_ge(s(f"x1_out{u}"), 1 + 16 * (use2(b, t) - 1))
                dve.wait_ge(s("c2_x1n"), 1 + (q - 1 if t >= 1 else CT * b))
                dve.tensor_tensor(x1[0:rows, u], bank(6)[0:rows, 0:D], xr[0:rows, u], ALU.add)\
                   .then_inc(s(f"c2_x1_{u}"), 1)
                dve.wait_ge(s(f"c2_x1_{u}"), 1 + use2(b, t))
                ch.step(dve.bn_stats(st2[0:rows, u], x1[0:rows, u]))
                wait_alone(dve, "dve_chain", ch.base + ch.n)
                ch.link(dve.bn_aggr(mv2[0:rows, u], st2[0:rows, u]))
                ch.link(dve.tensor_scalar(zz[:, 4 + u:5 + u], mv2[:, u, 1:2], EPS, None, ALU.add))
                dve.tensor_scalar(rs2[:, u:u + 1].bitcast(I32), zz[:, 4 + u:5 + u].bitcast(I32), -0.5, RSQRT_MAGIC,
                                  ALU.mult, ALU.add).then_inc(s("c2_guess"), 1)

            def logits_out(b, t):
                rows, q = (TO if t < CT - 1 else LAST), CT * b + t
                dve.wait_ge(s("c2_lgmm"), 1 + q + 1)
                dve.tensor_copy(logits[0:rows, bass.ds(q, 1), :], bank(7)[0:rows, 256:256 + E].unsqueeze(1))\
                   .then_inc(s("c2_lg"), 1)

            dve.wait_ge(s("p_mm"), NQ // 4)
            ch.step(dve.memset(mv2, 1.0))
            ch.link(dve.memset(logits, 0.0))

            def less_max(b, t):
                u, q = t % 2, CT * b + t
                m, sc = mx[:, 16 * u:16 * u + 16], bank(2 * u, 2).rearrange("p (h c) -> p h c", h=H)
                dve.wait_ge(s("c2_sim"), 1 + q + 1)
                ch.link(dve.tensor_reduce(m, sc, AX, ALU.max))
                dve.wait_ge(s("c2_a1"), 1 + (q - 1 if t >= 1 else CT * b))
                dve.tensor_tensor(ex[:, u].rearrange("p (h c) -> p h c", h=H), sc,
                                  m.unsqueeze(2).to_broadcast([P, H, M]), ALU.subtract).then_inc(s("c2_sub"), 1)

            def inverse_sums(b, t):
                u, q = t % 2, CT * b + t
                sums, inv = sm[:, 16 * u:16 * u + 16], ri[:, 16 * u:16 * u + 16]
                dve.wait_ge(s("c2_exp"), q + 1)
                ch.link(dve.tensor_reduce(sums, ex[:, u].rearrange("p (h c) -> p h c", h=H), AX, ALU.add))
                if t in (0, CT - 1):
                    ch.link(dve.reciprocal(inv, sums))
                    dve.tensor_scalar(inv, inv, validf[:, t // (CT - 1):t // (CT - 1) + 1], None, ALU.mult)\
                       .then_inc(s("c2_rinv"), 1)
                else:
                    dve.reciprocal(inv, sums).then_inc(s("c2_rinv"), 1)

            def c2_dve(b, t, tile):
                if t > 0:
                    tile(less_max, 0)
                tile(logits_out, 6)
                tile(rows_out, 3)
                if t == 0:
                    tile(less_max, 0)
                tile(inverse_sums, 0)

            c2_batches(dve, c2_dve, 6, ch, CT * 5 + 2)
            dve.wait_ge(s("c2_lg"), 1 + QT)
            dve.wait_ge(s("c2_conv"), 1 + QT)
            dve.wait_ge(s("c2_sim"), 1 + QT)
            d1, oh1, d2, oh2, e1v, e2v, ab, sa, sc_, t1, t2 = r_a
            bc = lambda a: a.unsqueeze(2).to_broadcast([P, QT, E])
            ec = lambda a: a.unsqueeze(1).to_broadcast([P, QT, E])
            for v in (ecol, ebase, t_tau[:, :]):
                ch.step(dve.tensor_copy(v, v.bitcast(I32)))
            ch.sync()
            ch.link(dve.scalar_tensor_tensor(out=ab, in0=logits, scalar=-1.0, in1=logits, op0=ALU.mult, op1=ALU.max))
            lg = logits
            for c, (m, d, oh, ev, w) in enumerate(((m1, d1, oh1, e1v, w1), (m2, d2, oh2, e2v, w2))):
                if c == 1:
                    ch.link(dve.scalar_tensor_tensor(out=t2, in0=oh1, scalar=-BIG, in1=logits, op0=ALU.mult, op1=ALU.add))
                    lg = t2
                ch.link(dve.tensor_reduce(m, lg, AX, ALU.max))
                ch.link(dve.tensor_tensor(d, bc(m), lg, ALU.subtract))
                ch.link(dve.scalar_tensor_tensor(out=t1, in0=d, scalar=0.0, in1=ec(ecol), op0=ALU.is_equal, op1=ALU.mult))
                ch.link(dve.tensor_reduce(i1, t1, AX, ALU.min))
                ch.link(dve.tensor_tensor(oh, bc(i1), ec(ecol), ALU.is_equal))
                dve.tensor_copy(ev, d).then_inc(s("d_gap"), 1)
                ch.link(dve.tensor_tensor(t1, ab, bc(m), ALU.max))
                ch.link(dve.scalar_tensor_tensor(out=t1, in0=t1, scalar=JITTER2, in1=d, op0=ALU.mult, op1=ALU.is_ge))
                dve.wait_ge(s("d_exp"), c + 1)
                ch.link(dve.tensor_tensor(t1, t1, ev, ALU.mult))
                ch.link(dve.tensor_reduce(w, t1, AX, ALU.add))
                ch.link(dve.reciprocal(w, w))
            ch.link(dve.tensor_tensor(t1, oh1, oh2, ALU.add))
            ch.link(dve.tensor_scalar(t2, t1, validf[:, 2:3], None, ALU.mult))
            last = lambda a: a.rearrange("p (b t) e -> p b t e", b=B)[:, :, CT - 1]
            dve.tensor_scalar(last(t2), last(t1), validf[:, 3:4], None, ALU.mult).then_inc(s("d_hot"), 1)
            dve.wait_ge(s("d_cnt"), 1)
            cnt = bank(1)[:, 0:QT * E].rearrange("p (q e) -> p q e", q=QT)
            ch.link(dve.tensor_copy(sa, cnt))
            src, dst, sh = sa, sc_, 1
            while sh < QT:
                ch.step(dve.tensor_copy(dst[:, 0:sh], src[:, 0:sh]))
                ch.link(dve.tensor_tensor(dst[:, sh:], src[:, sh:], src[:, 0:QT - sh], ALU.add))
                src, dst, sh = dst, src, 2 * sh
            ch.step(dve.tensor_copy(n_e, src[:, QT - 1]))
            ch.link(dve.tensor_tensor(dst, src, cnt, ALU.subtract))
            ch.link(dve.tensor_tensor(dst, dst, bank(0)[:, 0:QT * E].rearrange("p (q e) -> p q e", q=QT), ALU.add))
            ch.link(dve.tensor_tensor(dst, dst, ec(ebase), ALU.add))
            for oh, sl in ((oh1, sl1), (oh2, sl2)):
                ch.link(dve.tensor_tensor(t1, oh, dst, ALU.mult))
                ch.link(dve.tensor_reduce(sl, t1, AX, ALU.add))
                ch.link(dve.tensor_copy(sl.bitcast(I32), sl))
            ch.link(dve.tensor_copy(n_pad[:, :].bitcast(I32), n_e))
            ch.link(dve.tensor_scalar(te.bitcast(I32), n_e, float(P - 1), None, ALU.add))
            ch.link(dve.tensor_scalar(te.bitcast(I32), te.bitcast(I32), 7, None, ALU.logical_shift_right))
            ch.link(dve.tensor_copy(nt, te.bitcast(I32)))
            ch.link(dve.tensor_copy(te, nt))
            src, dst, sh = te, tb, 1
            while sh < E:
                ch.step(dve.tensor_copy(dst[:, 0:sh], src[:, 0:sh]))
                ch.link(dve.tensor_tensor(dst[:, sh:], src[:, sh:], src[:, 0:E - sh], ALU.add))
                src, dst, sh = dst, src, 2 * sh
            ends = src
            ch.link(dve.tensor_tensor(tc, ends, nt, ALU.subtract))
            ch.link(dve.scalar_tensor_tensor(out=tc, in0=tc, scalar=-float(P), in1=ebase, op0=ALU.mult, op1=ALU.add))
            big = ex[:, 0, 0:NTILE * E].rearrange("p (t e) -> p t e", t=NTILE)
            tbc = lambda a: a.unsqueeze(2).to_broadcast([P, NTILE, E])
            tec = lambda a: a.unsqueeze(1).to_broadcast([P, NTILE, E])
            ch.link(dve.tensor_tensor(big, tbc(t_tau[:, :]), tec(ends), ALU.is_ge))
            ch.link(dve.tensor_reduce(t_eid[:, :], big, AX, ALU.add))
            ch.link(dve.tensor_scalar(t_a[:, :], t_eid[:, :], -float(E), None, ALU.add))
            ch.link(dve.tensor_tensor(big, tbc(t_a[:, :]), tec(ecol), ALU.is_equal))
            ch.link(dve.tensor_tensor(big, big, tec(tc), ALU.mult))
            ch.link(dve.tensor_reduce(t_row[:, :], big, AX, ALU.add))
            ch.link(dve.scalar_tensor_tensor(out=t_row[:, :], in0=t_tau[:, :], scalar=float(P), in1=t_row[:, :],
                                             op0=ALU.mult, op1=ALU.add))
            ch.link(dve.tensor_scalar(t_a[:, :], t_a[:, :], 0.0, None, ALU.is_equal))
            ch.link(dve.tensor_scalar(t_tau[:, :], t_row[:, :], -1.0, float(ZROW), ALU.mult, ALU.add))
            ch.link(dve.tensor_tensor(t_tau[:, :], t_tau[:, :], t_a[:, :], ALU.mult))
            ch.link(dve.tensor_tensor(t_row[:, :].bitcast(I32), t_row[:, :], t_tau[:, :], ALU.add))
            ch.link(dve.tensor_scalar(t_eid[:, :].bitcast(I32), t_eid[:, :], float(E - 1), None, ALU.min))
            dve.memset(t_a[:, 0:1], 0.0).then_inc(s("d_tab"), 1)
            with dve.Fori(0, B) as b:
                ch.enter(b, CT * 5)
                for t in range(CT):
                    rows = TO if t < CT - 1 else LAST
                    q, v = CT * b + t, t % 3
                    dve.wait_ge(s(f"d_x_in{v}"), 32 * use3(b, t))
                    for c, (w, slt) in enumerate(((w1, sl1), (w2, sl2))):
                        ch.step(dve.tensor_copy(xd[0:rows, v, c, D:D + 1], w[0:rows, bass.ds(q, 1)]))
                        ch.step(dve.tensor_scalar(xd[0:rows, v, c, D + 1:D + 2].bitcast(I32),
                                                  tokid[0:rows, bass.ds(q, 1)].bitcast(I32), float(TOK * c), None, ALU.add))
                        ins = dve.tensor_copy(idx[0:rows, 2 * v + c:2 * v + c + 1].bitcast(I32),
                                              slt[0:rows, bass.ds(q, 1)].bitcast(I32))
                        if c == 0:
                            ch.link(ins)
                        else:
                            ch.sync()
                            ins.then_inc(s("d_meta"), 1)
                ch.leave(B)
            def expert_out(i, n, v, free):
                dve.wait_ge(s("m_down"), n + 1)
                if not free:
                    dve.wait_ge(s(f"m_sc{v}"), 16 * i)
                dve.tensor_scalar(ys[:, v], bank(5)[:, 0:D], xs[:, v, D:D + 1], None, ALU.mult).then_inc(s("m_y"), 1)

            def expert_tiles(i, first, second):
                for v in range(4):
                    n = 4 * i + v
                    dve.wait_ge(s("m_sil"), n + 1)
                    dve.wait_ge(s("m_up"), n + 1)
                    if not (first and v < 2):
                        dve.wait_ge(s("m_htp"), n - 1)
                    dve.tensor_tensor(hid[:, v % 2], sil[:, v % 2], bank(2 + v % 2), ALU.mult).then_inc(s("m_hid"), 1)
                    if v > 0:
                        expert_out(i, n - 1, v - 1, first)
                    elif not first:
                        expert_out(i - 1, n - 1, 3, second)

            expert_tiles(0, True, False)
            expert_tiles(1, False, True)
            with dve.Fori(2, NTILE // 4) as i:
                expert_tiles(i, False, False)
            expert_out(NTILE // 4 - 1, NTILE - 1, 3, False)
            for k in range(CH):
                dve.wait_ge(s(f"f_in{k % 2}"), 48 * (k // 2 + 1))
                dve.tensor_tensor(fin[:, k % 2, 1], fin[:, k % 2, 0], fin[:, k % 2, 1], ALU.add).then_inc(s("f_sum1"), 1)

        @block.tensor
        def _(pe):
            pe.wait_ge(s("consts"), 1)
            idt = ident[:, :]
            with pe.Fori(0, B) as b:
                pe.wait_ge(s("a_xnt"), 1 + 4 * b)
                for half in range(2):
                    for k in range(KD):
                        for t in range(4):
                            if k == 0:
                                pe.wait_ge(s("a_xn"), RT * b + 4 * half + t + 1)
                            mm = pe.transpose(bank(2 * k + half)[:, t * P:(t + 1) * P],
                                              xnb[:, 4 * half + t, k * P:(k + 1) * P], idt)
                        mm.then_inc(s("a_tp"), 1)
            pe.wait_ge(s("a_lm"), 1 + KD * B)
            pe.wait_ge(s("a_xnt"), 1 + 4 * B)
            pe.wait_ge(s("w_qk_in"), 16)
            for j in range(J):
                for c in range(2):
                    n = 2 * j + c
                    if n >= 8:
                        for e_ in ("act", "dve"):
                            pe.wait_ge(s(f"b_{'qk'[c]}_{e_}"), j - 3)
                    for k in range(KD):
                        mm = pe.matmul(bank(n % 8)[:, 0:B * M], wqk[:, k, c * INNER + j * P:c * INNER + (j + 1) * P],
                                       xm[:, k], start=(k == 0), stop=(k == KD - 1))
                    mm.then_inc(s("b_lm"), 1)
            for e_ in ("act", "dve"):
                pe.wait_ge(s(f"b_q_{e_}"), J)
            pe.wait_ge(s("b_kst"), 2)
            for g in range(B):
                for j in range(J):
                    mm = pe.matmul(bank(g)[:, j * M:(j + 1) * M], q_bd[:, j, g], k_st[:, j, g], start=True, stop=True)
                mm.then_inc(s("b_sim2"), 1)
            pe.wait_ge(s("b_a"), 2 * B)
            pe.wait_ge(s("b_sub"), B)
            for n in range(8):
                for q in range(4):
                    mm = pe.transpose(bank(n)[:, q * P:(q + 1) * P], zt[:, 4 * n + q], idt)
                mm.then_inc(s("b_at_tp"), 1)
            pe.wait_ge(s("w_in"), 16 * 5)
            pe.wait_ge(s("i_z0"), 2)

            def c1_sim(b, j):
                q, u = J * b + j, j % 2
                pe.wait_ge(s("c1_exp"), 1 + (q - 1 if j >= 1 else J * b))
                for half in range(2):
                    for k in range(KD):
                        mm = pe.matmul(bank(2 * u + half), g3[:, k, j * P:(j + 1) * P],
                                       xnt[:, k, HALO + 512 * half:HALO + 512 * half + 512],
                                       start=(k == 0), stop=(k == KD - 1))
                mm.then_inc(s("c1_sim"), 1)

            def c1_v3(b, j):
                q = J * b + j
                pe.wait_ge(s("c1_utb"), 1 + q + 1)
                pe.wait_ge(s("c1_v3"), 1 + 2 * q)
                for k in range(KD):
                    mm = pe.matmul(bank(7)[:, 0:P], utb[:, k], wv[:, k, j * P:(j + 1) * P],
                                   start=(k == 0), stop=(k == KD - 1))
                mm.then_inc(s("c1_v3mm"), 1)

            with pe.Fori(0, B) as b:
                pe.wait_ge(s("c1_exp"), 1 + J * b)
                for k in range(KD):
                    for j in range(J):
                        mm = pe.matmul(bank(2 * k, 2)[:, j * P:(j + 1) * P], wkt[:, j, k * P:(k + 1) * P],
                                       q_bd[:, j, b], start=True, stop=True)
                    mm.then_inc(s("c1_g3mm"), 1)
                pe.wait_ge(s("c1_g3"), KD * b + KD)
                pe.wait_ge(s("c1_xnt_in"), 16 * (b + 1))
                c1_sim(b, 0)
                for j in range(J):
                    u, q = j % 2, J * b + j
                    if j < J - 1:
                        c1_sim(b, j + 1)
                    pe.wait_ge(s("c1_exp"), 1 + q + 1)
                    pe.wait_ge(s("c1_e3a"), 1 + q)
                    pe.wait_ge(s("c1_e3b"), 1 + q)
                    for t in range(RT):
                        mm = pe.transpose(bank(4 + t // 4)[:, (t % 4) * P:(t % 4 + 1) * P],
                                          ex[:, u, t * P:(t + 1) * P], idt)
                    mm.then_inc(s("c1_tp"), 1)
                    if j >= 1:
                        c1_v3(b, j - 1)
                    else:
                        pe.wait_ge(s("c1_xn_in"), 16 * (b + 1))
                        pe.wait_ge(s("c1_utb"), 1 + q)
                    pe.wait_ge(s("c1_e3a"), 1 + q + 1)
                    pe.wait_ge(s("c1_e3b"), 1 + q + 1)
                    for k in range(KD):
                        for t in range(RT):
                            mm = pe.matmul(bank(6)[:, k * P:(k + 1) * P], xnb[:, t, k * P:(k + 1) * P], e3t[:, t],
                                           start=(t == 0), stop=(t == RT - 1))
                    mm.then_inc(s("c1_ut"), 1)
                c1_v3(b, J - 1)
            pe.wait_ge(s("c1_v3"), 1 + 2 * NQ)

            def products(lhs, rhs, waits, name):
                for g in range(4):
                    for w, n in waits:
                        pe.wait_ge(s(w), n + g)
                    for q in range(8 * g, 8 * g + 8):
                        o_ = ps[:, q * P:(q + 1) * P]
                        mm = pe.transpose(o_, lhs[:, q], idt) if rhs is None else \
                            pe.matmul(o_, lhs[:, q], rhs[:, q], start=True, stop=True)
                    mm.then_inc(s(name), 1)

            with pe.Fori(0, ITERS) as it:
                pe.wait_ge(s("i_zt"), 1 + 4 * it)
                products(att, z, (), "i_azmm")
                products(tt, None, (("i_t1", 4 * it + 1),), "i_t1tp")
                products(azt, tt, (("i_azt", 4 * it + 1),), "i_t1mm")
                products(azt, tt, (("i_t2", 4 * it + 1),), "i_t2mm")
                products(zt, tt, (("i_t3", 4 * it + 1),), "i_zmm")
                products(z, None, (("i_z", 4 * it + 1),), "i_ztp")
            pe.wait_ge(s("i_zt"), 1 + 4 * ITERS)
            for g in range(NQ // 4):
                if g >= 2:
                    pe.wait_ge(s("p_wt"), g - 1)
                for i in range(4):
                    q = 4 * g + i
                    mm = pe.matmul(bank(g % 2)[:, i * P:(i + 1) * P], v3[:, q // J, q % J], zt[:, q], start=True, stop=True)
                mm.then_inc(s("p_wt_mm"), 1)
                pe.wait_ge(s("p_wt"), g + 1)
                if g >= 2:
                    pe.wait_ge(s("p_pm"), g - 1)
                for i in range(4):
                    q = 4 * g + i
                    mm = pe.matmul(bank(2 + 2 * (g % 2), 2)[:, i * D:(i + 1) * D], wts[:, i], wfc[:, q % J],
                                   start=True, stop=True)
                mm.then_inc(s("p_mm"), 1)
            pe.wait_ge(s("p_pm"), NQ // 4)

            def c2_sim(b, t):
                q, u = CT * b + t, t % 2
                pe.wait_ge(s("c2_sub"), 1 + (q - 1 if t >= 1 else CT * b))
                for half in range(2):
                    for k in range(KD):
                        mm = pe.matmul(bank(2 * u + half), xnt[:, k, TO * t:TO * t + P], g1[:, k, 512 * half:512 * half + 512],
                                       start=(k == 0), stop=(k == KD - 1))
                mm.then_inc(s("c2_sim"), 1)

            def c2_tp(b, t):
                rows, u, q = (TO if t < CT - 1 else LAST), t % 2, CT * b + t
                pe.wait_ge(s("c2_x1n"), 1 + q + 1)
                pe.wait_ge(s("c2_lg"), 1 + q)
                for k in range(KD):
                    mm = pe.transpose(bank(7)[:, k * rows:(k + 1) * rows], x1n[0:rows, u, k * P:(k + 1) * P],
                                      ident[0:rows, 0:rows])
                mm.then_inc(s("c2_x1tp"), 1)

            def c2_lg(b, t):
                rows, q = (TO if t < CT - 1 else LAST), CT * b + t
                pe.wait_ge(s("c2_x1t"), q + 1)
                for k in range(KD):
                    mm = pe.matmul(bank(7)[0:rows, 256:256 + E], x1t[:, k, 0:rows], rw[:, k * E:(k + 1) * E],
                                   start=(k == 0), stop=(k == KD - 1))
                mm.then_inc(s("c2_lgmm"), 1)

            def c2_g1(b, t):
                pe.wait_ge(s("c2_sub"), 1 + CT * b)
                for k in range(KD):
                    for j in range(J):
                        mm = pe.matmul(bank(2 * k, 2)[:, j * P:(j + 1) * P], wqt[:, j, k * P:(k + 1) * P],
                                       k_bd[:, j, b], start=True, stop=True)
                    mm.then_inc(s("c2_g1mm"), 1)

            def c2_first_sim(b, t):
                pe.wait_ge(s("c2_g1"), KD * b + KD)
                pe.wait_ge(s("c2_xnt_in"), 16 * (b + 1))
                c2_sim(b, 0)

            def c2_conv(b, t):
                u, q = t % 2, CT * b + t
                pe.wait_ge(s("c2_a1"), 1 + q + 1)
                pe.wait_ge(s("c2_cvt"), 1 + q)
                for h in range(H):
                    c = 64 * (h % 2)
                    mm = pe.matmul(bank(4, 2)[c:c + 64, (h // 2) * P:(h // 2) * P + TO], a1[:, u, h], band[:, h],
                                   start=True, stop=True)
                mm.then_inc(s("c2_conv"), 1)

            def c2_y(b, t):
                rows, u, q = (TO if t < CT - 1 else LAST), t % 2, CT * b + t
                pe.wait_ge(s("c2_cvt"), 1 + q + 1)
                if t >= 1:
                    pe.wait_ge(s(f"c2_x1_{1 - u}"), 1 + use2(b, t - 1))
                else:
                    pe.wait_ge(s("c2_x1_0"), 1 + use2(b, 0) - 1)
                for j in range(J):
                    mm = pe.matmul(bank(6)[0:rows, 0:D], cvt[:, u, j, 0:rows], pm[:, b, j],
                                   start=(j == 0), stop=(j == J - 1))
                mm.then_inc(s("c2_y"), 1)

            def c2_pe(b, t, tile):
                if t > 0:
                    tile(c2_sim, 0)
                if t != 1:
                    tile(c2_conv, 1)
                tile(c2_tp, 5)
                if t == 0:
                    tile(c2_g1, 0)
                tile(c2_y, 2)
                tile(c2_lg, 5)
                if t == 0:
                    tile(c2_first_sim, 0)
                if t == 1:
                    tile(c2_conv, 1)

            pe.wait_ge(s("band_ok"), 1)
            c2_batches(pe, c2_pe, 5)
            pe.wait_ge(s("d_hot"), 1)
            hot = r_a[10].rearrange("p q e -> p (q e)")
            pe.matmul(bank(0)[:, 0:QT * E], tri[:, :], hot, start=True, stop=True)
            pe.matmul(bank(1)[:, 0:QT * E], ones[:, :], hot, start=True, stop=True).then_inc(s("d_cnt"), 1)
            pe.wait_ge(s("wgu_in"), 16 * KD)
            pe.wait_ge(s("wd_in"), 32)
            pe.wait_ge(s("d_tab"), 1)

            def expert(n):
                return pe.value_load(t_eid[0:1, bass.ds(n, 1)].bitcast(I32), min_val=0, max_val=E - 1)

            def x_columns(i, n, v, free):
                pe.wait_ge(s(f"m_xs_in{v}"), 16 * (i + 1))
                if not free:
                    pe.wait_ge(s("m_xst"), n)
                for k in range(KD):
                    mm = pe.transpose(bank(6)[:, k * P:(k + 1) * P], xs[:, v, k * P:(k + 1) * P], idt)
                mm.then_inc(s("m_xtp"), 1)

            def hidden(c, e, u):
                for k in range(KD):
                    mm = pe.matmul(bank(2 * c + u), xst[:, u, k], w_gu_s[:, e, k, c], start=(k == 0), stop=(k == KD - 1))
                mm.then_inc(s(("m_gate", "m_up")[c]), 1)

            def h_columns(n, u, free):
                pe.wait_ge(s("m_hid"), n + 1)
                if not free:
                    pe.wait_ge(s("m_ht"), n)
                for f in range(4):
                    mm = pe.transpose(bank(4)[:, f * P:(f + 1) * P], hid[:, u, f * P:(f + 1) * P], idt)
                mm.then_inc(s("m_htp"), 1)

            def down(e, n, u, free):
                pe.wait_ge(s("m_ht"), n + 1)
                if not free:
                    pe.wait_ge(s("m_y"), n)
                for f in range(4):
                    mm = pe.matmul(bank(5)[:, 0:D], hidt[:, u, f], w_d_s[:, e, f], start=(f == 0), stop=(f == 3))
                mm.then_inc(s("m_down"), 1)

            def expert_tiles(i, first, last):
                for v in range(4):
                    n, u = 4 * i + v, v % 2
                    e = expert(n)
                    pe.wait_ge(s("m_xst"), n + 1)
                    if not (first and v < 2):
                        pe.wait_ge(s("m_hid"), n - 1)
                    hidden(0, e, u)
                    if not (first and v == 0):
                        h_columns(n - 1, 1 - u, first and v == 1)
                    hidden(1, e, u)
                    if not (first and v == 0):
                        down(expert(n - 1), n - 1, 1 - u, first and v == 1)
                    if v < 3:
                        x_columns(i, n + 1, v + 1, False)
                    elif not last:
                        x_columns(i + 1, n + 1, 0, False)

            x_columns(0, 0, 0, True)
            expert_tiles(0, True, False)
            with pe.Fori(1, NTILE // 4 - 1) as i:
                expert_tiles(i, False, False)
            expert_tiles(NTILE // 4 - 1, False, True)
            h_columns(NTILE - 1, 1, False)
            down(expert(NTILE - 1), NTILE - 1, 1, False)


_OUT = (B, N, D)


def kernel(**inputs):
    import numpy as np
    import concourse.bacc as bacc
    from concourse.bass_utils import run_bass_kernel_spmd as run

    f = {k: np.asarray(v) for k, v in inputs.items()}
    wqkv = f["L0_attn_w_qkv"]
    taps = f["L0_attn_w_conv"].reshape(H, TAPS)
    band = np.zeros((H, P, TO), taps.dtype)
    for o in range(TO):
        band[:, o:o + TAPS, o] = taps
    gate_t = f["L0_ffn_w_gate"].transpose(0, 2, 1).reshape(E, KD, P, F)
    up_t = f["L0_ffn_w_up"].transpose(0, 2, 1).reshape(E, KD, P, F)
    arrays = {
        "x": f["L0_attn_x"],
        "w_qkv": wqkv,
        "wq_t": wqkv[:, 0:INNER].T,
        "wk_t": wqkv[:, INNER:2 * INNER].T,
        "conv_band": band,
        "w_fc": f["L0_attn_w_fc"],
        "b_fc": f["L0_attn_b_fc"],
        "router_t": f["L0_ffn_router_w"].T,
        "w_gu": np.stack([gate_t, up_t], axis=3),
        "w_down": f["L0_ffn_w_down"].transpose(0, 2, 1).reshape(E, 4, P, D).transpose(0, 2, 1, 3),
    }
    nc = bacc.Bacc("TRN2", target_bir_lowering=False, num_devices=1)
    args = []
    for name in list(arrays):
        arrays[name] = np.ascontiguousarray(arrays[name])
        args.append(nc.dram_tensor(name, arrays[name].shape, mybir.dt.from_np(arrays[name].dtype), kind="ExternalInput").ap())
    args.append(nc.dram_tensor("out", _OUT, F32, kind="ExternalOutput").ap())
    layer(nc, *args)
    r = run(nc, [arrays], core_ids=[0])
    return r.results[0]["out"]
```

```python
import math
from contextlib import ExitStack

import concourse.bass as bass
from concourse import mybir

F32 = mybir.dt.float32
I32 = mybir.dt.int32
U32 = mybir.dt.uint32
ALU = mybir.AluOpType
ACT = mybir.ActivationFunctionType
AX = mybir.AxisListType.X

P = 128
B, N, D = 4, 1024, 256
H, DH, M = 16, 64, 64
INNER = H * DH
J = H // 2
KD = D // P
RT = N // P
ITERS = 6
TAPS = 13
HALO = TAPS // 2
TO = P - 2 * HALO
CT = -(-N // TO)
LAST = N - (CT - 1) * TO
PADN = (CT - 1) * TO + P
NQ = B * J
EPS = 1e-5
E, F = 8, 512
JITTER2 = 0.02
TOK = B * N
REGION = TOK + P
ZROW = E * REGION
NTILE = (2 * TOK + E * (P - 1)) // P + 1
NTILE += -NTILE % 4
ROW = D + 4
QT = B * CT
RSQRT_MAGIC = float(0x5F3759DF)
BIG = 3.0e38
G = 3
STARTED = (
    "a_xnt", "a_lm", "a_xnt_out0", "a_xnt_out1",
    "c1_sim", "c1_exp", "c1_tp", "c1_e3a", "c1_e3b", "c1_ut", "c1_utb", "c1_v3mm", "c1_v3", "i_zt",
    "c2_sim", "c2_sub", "c2_a1", "c2_conv", "c2_cvt", "c2_y", "c2_x1_0", "c2_x1_1", "x1_out0", "x1_out1",
    "c2_x1n", "x1n_out0", "x1n_out1", "c2_x1tp", "c2_lgmm", "c2_lg", "d_free0", "d_free1",
)


class Chain:

    def __init__(self, eng, sem):
        self.eng, self.sem, self.base, self.n = eng, sem, 0, 0

    def step(self, ins):
        ins.then_inc(self.sem, 1)
        self.n += 1

    def sync(self):
        self.eng.wait_ge(self.sem, self.base + self.n)

    def link(self, ins):
        self.step(ins)
        self.sync()

    def enter(self, i, per_turn):
        self.start, self.per_turn, self.n0 = self.base + self.n, per_turn, self.n
        self.base, self.n = self.start + i * per_turn, 0

    def leave(self, turns):
        assert self.n == self.per_turn, (self.n, self.per_turn)
        self.base, self.n = self.start + turns * self.per_turn, 0


def layer(nc, x, w_qkv, wq_t, wk_t, conv_band, w_fc, b_fc, router_t, w_gu, w_down, out):
    with ExitStack() as ctx:
        def sb(name, words):
            return ctx.enter_context(nc.sbuf_tensor(name, [P, words], F32))

        def sem(name):
            return ctx.enter_context(nc.semaphore(name))

        def dram(name, shape):
            return nc.dram_tensor(name, shape, F32, kind="Internal").ap()

        xnt_d = dram("xnt_d", (B, P, KD * PADN))
        x1n_d = dram("x1n_d", (B, N, D))
        xs_d = dram("xs_d", (ZROW + P, ROW))

        mem = sb("mem", 50500)

        def at(start, words):
            return mem[:, start:start + words]

        SQ = NQ * P
        zt = at(0, SQ).rearrange("p (q c) -> p q c", q=NQ)
        z = at(SQ, SQ).rearrange("p (q c) -> p q c", q=NQ)
        azt = at(2 * SQ, SQ).rearrange("p (q c) -> p q c", q=NQ)
        tt = at(3 * SQ, SQ).rearrange("p (q c) -> p q c", q=NQ)
        att = at(4 * SQ, SQ).rearrange("p (q c) -> p q c", q=NQ)
        xna = at(2 * SQ, B * RT * D).rearrange("p (b t c) -> p b t c", b=B, t=RT)
        g3 = at(5 * SQ + RT * D, KD * INNER).rearrange("p (k c) -> p k c", k=KD)
        q_bd = at(6 * SQ, SQ).rearrange("p (j b c) -> p j b c", j=J, b=B)
        k_bd = at(7 * SQ, SQ).rearrange("p (j b c) -> p j b c", j=J, b=B)
        v3 = at(8 * SQ, SQ).rearrange("p (b j c) -> p b j c", b=B, j=J)
        o = 9 * SQ
        xnt = at(o, KD * PADN).rearrange("p (k n) -> p k n", k=KD); o += KD * PADN
        wqt = at(o, J * D).rearrange("p (j c) -> p j c", j=J); o += J * D
        wkt = at(o, J * D).rearrange("p (j c) -> p j c", j=J)
        xr = at(o, 2 * D).rearrange("p (u c) -> p u c", u=2)
        x1 = at(o + 2 * D, 2 * D).rearrange("p (u c) -> p u c", u=2)
        x1n = at(o + 4 * D, 2 * D).rearrange("p (u c) -> p u c", u=2)
        bfc = at(o + 6 * D, D)
        o += J * D
        wv = at(o, KD * INNER).rearrange("p (k c) -> p k c", k=KD)
        x1t = at(o, KD * P).rearrange("p (k c) -> p k c", k=KD)
        logits = at(o + KD * P, CT * E).rearrange("p (t e) -> p t e", t=CT)
        xd_second = o + KD * P + CT * E
        o += KD * INNER
        assert xd_second + G * 2 * ROW <= o
        wfc = at(o, J * D).rearrange("p (j c) -> p j c", j=J)
        xds = [at(at_, G * 2 * ROW).rearrange("p (v c w) -> p v c w", v=G, c=2) for at_ in (o, xd_second)]
        ro = o + G * 2 * ROW
        def routing(*dims):
            nonlocal ro
            words = math.prod(dims)
            ro += words
            names = "abc"[:len(dims)]
            return at(ro - words, words).rearrange(f"p ({' '.join(names)}) -> p {' '.join(names)}",
                                                   **dict(zip(names[1:], dims[1:])))
        ab, t1, t2, hot, pos = (routing(G, E) for _ in range(5))
        gap, gap_exp, one_hot, cnt = (routing(2, G, E) for _ in range(4))
        top = routing(2, G)
        first_e = routing(G)[:, :]
        weight, slot = routing(G, 2), routing(G, 2)
        assert ro <= o + J * D
        o += J * D
        ex = at(o, 2 * INNER).rearrange("p (u c) -> p u c", u=2); o += 2 * INNER
        e3t = at(o, RT * P).rearrange("p (t c) -> p t c", t=RT)
        wts = at(o, 8 * P).rearrange("p (u s c) -> p u s c", u=2, s=4)
        utb = at(o + RT * P, KD * P).rearrange("p (k c) -> p k c", k=KD)
        xnb = at(5 * SQ, RT * D).rearrange("p (t c) -> p t c", t=RT)
        xnts = (xnt, at(5 * SQ, KD * PADN).rearrange("p (k n) -> p k n", k=KD))
        xm = at(5 * SQ + KD * PADN, KD * B * M).rearrange("p (k c) -> p k c", k=KD)
        o += RT * P + KD * P
        assert o <= 50500
        xbs = at(0, 2 * RT * D).rearrange("p (u t c) -> p u t c", u=2, t=RT)
        wqk = at(SQ, KD * 2 * INNER).rearrange("p (k c) -> p k c", k=KD)
        k_st = at(8 * SQ, J * B * M).rearrange("p (j b c) -> p j b c", j=J, b=B)
        sm2 = at(8 * SQ + J * B * M, NQ * M).rearrange("p (q c) -> p q c", q=NQ)
        w_gu_s = at(0, E * KD * 2 * F).rearrange("p (e k g f) -> p e k g f", e=E, k=KD, g=2)
        pm = at(4 * SQ, NQ * D).rearrange("p (b j c) -> p b j c", b=B, j=J)
        a1 = at(6 * SQ, 2 * INNER).rearrange("p (u h c) -> p u h c", u=2, h=H)
        cvt = at(6 * SQ + 2 * INNER, 2 * J * TO).rearrange("p (u j c) -> p u j c", u=2, j=J)
        band = at(8 * SQ, H * TO).rearrange("p (h c) -> p h c", h=H)
        g1 = at(8 * SQ + KD * INNER, KD * INNER).rearrange("p (k c) -> p k c", k=KD)
        w_d_s = at(6 * SQ, E * 4 * D).rearrange("p (e f c) -> p e f c", e=E, f=4)
        o = 8 * SQ
        def take(words):
            nonlocal o
            o += words
            return at(o - words, words)
        xs = take(4 * ROW).rearrange("p (u c) -> p u c", u=4)
        xst = take(2 * D).rearrange("p (u k c) -> p u k c", u=2, k=KD)
        sil = take(2 * F).rearrange("p (u c) -> p u c", u=2)
        hid = take(2 * F).rearrange("p (u c) -> p u c", u=2)
        hidt = take(2 * F).rearrange("p (u f c) -> p u f c", u=2, f=4)
        ys = take(4 * D).rearrange("p (u c) -> p u c", u=4)

        ident = sb("ident", P)
        eyes = sb("eyes", 3 * P)
        eye7, eye15, eye13 = (eyes[:, i * P:(i + 1) * P] for i in range(3))
        tri = sb("tri", P)
        ones = sb("ones", P)
        shift = sb("shift", TO)
        sums16 = sb("sums16", RT)
        validf = sb("validf", 4)
        rw = sb("rw", KD * E)
        small = sb("small", 512)
        stats = small[:, 0:6 * RT].rearrange("p (t c) -> p t c", t=RT)
        mv = small[:, 48:48 + 2 * RT].rearrange("p (t c) -> p t c", t=RT)
        ve, rs, tmp = (small[:, 64 + 8 * i:72 + 8 * i] for i in range(3))
        mx = small[:, 96:128]
        sm = small[:, 128:160]
        ri = small[:, 160:192]
        zz = small[:, 192:200]
        mv2 = small[:, 200:204].rearrange("p (u c) -> p u c", u=2)
        st2 = small[:, 204:216].rearrange("p (u c) -> p u c", u=2)
        rs2 = small[:, 216:218]
        tm2 = small[:, 218:220]
        nmx = small[:, 220:222]
        s3 = small[:, 222:224]
        r3 = small[:, 224:226]
        idx = sb("idx", 2 * G * 2).rearrange("p (u v c) -> p u v c", u=2, v=G)
        ecol = small[:, 232:240]
        ebase = small[:, 240:248]
        n_e, nt, te, tb, tc = (small[:, 248 + 8 * i:256 + 8 * i] for i in range(5))
        mx2, sm2s, ri2 = (small[:, 288 + 32 * i:320 + 32 * i] for i in range(3))
        t_eid, t_row, t_a, t_tau = (sb(f"tab{i}", NTILE) for i in range(4))
        n_pad = sb("n_pad", E)
        tokid = sb("tokid", CT * 2).rearrange("p (t c) -> p t c", t=CT)
        run = sb("run", E)
        pad = sb("pad", ROW)

        ps = ctx.enter_context(nc.psum_tensor("ps", [P, 8 * 512], F32))

        def bank(i, n=1):
            return ps[:, i * 512:(i + n) * 512]

        S = {}

        def s(name):
            if name not in S:
                S[name] = sem(name)
            return S[name]

        def use2(b, t):
            return ((CT + 1 - t % 2) // 2) * b + t // 2 + 1

        def routed(b, t):
            g = t // G
            return g % 2, (2 * b + g // 2 if g % 2 == 0 else b)

        def group(b, t):
            return CT // G * b + t // G + 1

        def wait_alone(eng, name, count):
            eng.wait_ge(s(name), count)
            eng.sem_inc(s("passed"), 1)

        def x_loads(b, t):
            return {0: 6 * b + 2, 1: 2 * b + 2, 2: 6 * b + 6}[t // G]

        def pad_region(eng, e):
            n = eng.value_load(n_pad[0:1, e:e + 1].bitcast(I32), min_val=0, max_val=TOK)
            eng.dma_start(xs_d[bass.ds(n + e * REGION, P), :], pad[:, :]).then_inc(s("d_pad_out"), 16)

        def c2_batches(eng, step, steps, ch=None, links=0):
            def body(b, first, last):
                def tile(op, k, t):
                    if t >= k:
                        if not last:
                            op(b, t - k)
                    elif not first:
                        op(b - 1, CT + t - k)
                def route(op, stage, t):
                    for g in range(CT // G):
                        if not first and t == (G - last) * g + stage:
                            op(b - 1, G * g + stage)
                for t in range(steps if last else CT):
                    step(b, t, lambda op, k: tile(op, k, t), lambda op, stage: route(op, stage, t), first, last)

            body(0, True, False)
            with eng.Fori(1, B) as b:
                if ch:
                    ch.enter(b - 1, links)
                body(b, False, False)
                if ch:
                    ch.leave(B - 1)
            body(B, False, True)

        block = ctx.enter_context(nc.Block())
        x_t = x.rearrange("b (t p) c -> b p t c", p=P)

        @block.sync
        def _(sp):
            for name in STARTED:
                sp.sem_inc(s(name), 1)
            for b in range(B):
                if b >= 2:
                    sp.wait_ge(s("a_xn"), RT * (b - 1))
                for hf in range(2):
                    ts = slice(RT // 2 * hf, RT // 2 * (hf + 1))
                    sp.dma_start(xbs[:, b % 2, ts], x_t[b, :, ts]).then_inc(s(f"a_x_in{b % 2}{hf}"), 16)
            sp.dma_start(wqk, w_qkv[:, 0:2 * INNER].rearrange("(k p) c -> p k c", p=P)).then_inc(s("w_qk_in"), 16)
            sp.wait_ge(s("a_xnt"), 1 + 4 * B)
            sp.dma_start(wkt, wk_t.rearrange("(j p) c -> p j c", p=P)).then_inc(s("w_in"), 16)
            sp.dma_start(wv, w_qkv[:, 2 * INNER:].rearrange("(k p) c -> p k c", p=P)).then_inc(s("w_in"), 16)
            sp.dma_start(wqt, wq_t.rearrange("(j p) c -> p j c", p=P)).then_inc(s("w_in"), 16)
            sp.dma_start(wfc, w_fc.rearrange("(j p) c -> p j c", p=P)).then_inc(s("w_in"), 16)
            sp.dma_start(rw[:, :].rearrange("p (k e) -> p k e", k=KD),
                         router_t.rearrange("(k p) e -> p k e", p=P)).then_inc(s("w_in"), 16)
            sp.wait_ge(s("consts"), 1)
            sp.dma_start(xs_d[ZROW:ZROW + P, :], pad[:, :]).then_inc(s("d_pad_out"), 16)
            for u in range(2):
                sp.wait_ge(s(f"a_xnt_out{u}"), 1 + 16 * B // 2)
            with sp.Fori(0, B) as b:
                sp.wait_ge(s("c1_sim"), 1 + J * b)
                sp.dma_start(xnt, xnt_d[b].rearrange("p (k n) -> p k n", k=KD)).then_inc(s("c1_xnt_in"), 16)
                sp.wait_ge(s("c1_ut"), 1 + J * b)
                sp.dma_start(xnb, xna[:, b]).then_inc(s("c1_xn_in"), 16)
            sp.wait_ge(s("c1_sim"), 1 + J * B)
            sp.dma_start(xnt, xnt_d[0].rearrange("p (k n) -> p k n", k=KD)).then_inc(s("c2_xnt_in"), 16)
            sp.wait_ge(s("p_wt_mm"), NQ // 8)
            sp.dma_start(band, conv_band.rearrange("h p c -> p h c")).then_inc(s("band_in"), 16)
            sp.dma_start(bfc, b_fc.rearrange("(o c) -> o c", o=1).to_broadcast([P, D])).then_inc(s("bfc_in"), 16)
            sp.wait_ge(s("p_wt_mm"), NQ // 4)
            for k in range(KD):
                sp.dma_start(w_gu_s[:, :, k], w_gu[:, k].rearrange("e p g f -> p e g f")).then_inc(s("wgu_in"), 16)

            def down_weights(half):
                es = slice(4 * half, 4 * half + 4)
                sp.dma_start(w_d_s[:, es], w_down[es].rearrange("e p f c -> p e f c")).then_inc(s("wd_in"), 16)

            def dispatch_rows(b, t):
                u, n = routed(b, t)
                wait_alone(sp, f"d_free{u}", 1 + n)
                for i in (t + 1, t + 2):
                    wait_alone(sp, f"x1n_out{i % 2}", 1 + 16 * use2(b, i))
                full = G if t + G < CT else G - 1
                for c in range(2):
                    sp.dma_start(xds[u][0:TO, 0:full, c, 0:D],
                                 x1n_d[b, TO * t:TO * (t + full), :].rearrange("(v p) c -> p v c", v=full))\
                      .then_inc(s(f"d_x_in{u}"), 16)
                    if full < G:
                        sp.dma_start(xds[u][0:LAST, full, c, 0:D], x1n_d[b, TO * (t + full):N, :])\
                          .then_inc(s(f"d_x_in{u}"), 16)

            def batch_columns(b, t):
                sp.wait_ge(s("c2_sim"), 1 + CT * b)
                sp.dma_start(xnt, xnt_d[b].rearrange("p (k n) -> p k n", k=KD)).then_inc(s("c2_xnt_in"), 16)

            def residual_rows(b, t):
                rows, u = (TO if t < CT - 1 else LAST), t % 2
                sp.wait_ge(s(f"c2_x1_{u}"), 1 + use2(b, t) - 1)
                sp.dma_start(xr[0:rows, u], x[b, TO * t:TO * t + rows, :]).then_inc(s(f"c2_xr_in{u}"), 16)

            def c2_loads(b, t, tile, route, first, last):
                if t == 0 and not first:
                    tile(batch_columns, 0)
                if last and t == 0:
                    sp.wait_ge(s("c2_g1mm"), KD * B)
                    down_weights(1)
                tile(residual_rows, 2)
                route(dispatch_rows, 0)
                if last and t == 2:
                    sp.wait_ge(s("c2_y"), 1 + QT)
                    down_weights(0)

            c2_batches(sp, c2_loads, CT)
            sp.wait_ge(s("d_size"), 1)
            for e in range(E // 2):
                pad_region(sp, e)
            sp.wait_ge(s("d_tab"), 1)
            sp.wait_ge(s("d_pad_out"), 16 * (E + 1))
            sp.wait_ge(s("d_free0"), 1 + 2 * B)
            sp.wait_ge(s("d_free1"), 1 + B)
            def expert_rows(i, first):
                for v in range(4):
                    if not first:
                        sp.wait_ge(s(f"m_sc{v}"), 16 * i)
                    r = sp.value_load(t_row[0:1, bass.ds(4 * i + v, 1)].bitcast(I32), min_val=0, max_val=ZROW)
                    sp.dma_start(xs[:, v], xs_d[bass.ds(r, P), :]).then_inc(s(f"m_xs_in{v}"), 16)

            expert_rows(0, True)
            with sp.Fori(1, NTILE // 4) as i:
                expert_rows(i, False)
            for v in range(4):
                sp.wait_ge(s(f"m_sc{v}"), 16 * (NTILE // 4))

        @block.gpsimd
        def _(pool):
            ch = Chain(pool, s("pool_chain"))
            ch.link(pool.memset(ident[:, :], 0.0))
            ch.link(pool.affine_select(out=ident[:, :], in_=ident[:, :], compare_op=ALU.not_equal, fill=1.0,
                                       base=0, pattern=[[-1, P]], channel_multiplier=1))
            ch.link(pool.memset(sums16[:, :], 1.0))
            ch.link(pool.affine_select(out=sums16[:, :], in_=sums16[:, :], compare_op=ALU.is_ge, fill=0.0,
                                       base=0, pattern=[[-(N // M), RT]], channel_multiplier=1))
            ch.link(pool.affine_select(out=sums16[:, :], in_=sums16[:, :], compare_op=ALU.is_ge, fill=0.0,
                                       base=N // M - 1, pattern=[[N // M, RT]], channel_multiplier=-1))
            for halo in xnts:
                ch.link(pool.memset(halo[:, :, 0:HALO], 0.0))
                ch.link(pool.memset(halo[:, :, HALO + N:PADN], 0.0))
            ch.sync()
            pool.sem_inc(s("a_consts"), 1)
            for eye, c in ((eye7, 7.0), (eye15, 15.0), (eye13, 13.0 / 4)):
                ch.link(pool.tensor_scalar(eye, ident[:, :], c, 0.0, ALU.mult, ALU.add))
            ch.link(pool.memset(ones[:, :], 1.0))
            ch.link(pool.memset(validf[:, :], 1.0))
            ch.link(pool.affine_select(out=tri[:, :], in_=ones[:, :], compare_op=ALU.is_gt, fill=0.0,
                                       base=0, pattern=[[1, P]], channel_multiplier=-1))
            ch.link(pool.affine_select(out=validf[:, 0:1], in_=validf[:, 0:1], compare_op=ALU.is_ge, fill=0.0,
                                       base=-HALO, pattern=[[0, 1]], channel_multiplier=1))
            ch.link(pool.affine_select(out=validf[:, 1:2], in_=validf[:, 1:2], compare_op=ALU.is_ge, fill=0.0,
                                       base=LAST + HALO - 1, pattern=[[0, 1]], channel_multiplier=-1))
            ch.link(pool.affine_select(out=validf[:, 2:3], in_=validf[:, 2:3], compare_op=ALU.is_ge, fill=0.0,
                                       base=TO - 1, pattern=[[0, 1]], channel_multiplier=-1))
            ch.link(pool.affine_select(out=validf[:, 3:4], in_=validf[:, 3:4], compare_op=ALU.is_ge, fill=0.0,
                                       base=LAST - 1, pattern=[[0, 1]], channel_multiplier=-1))
            ch.link(pool.memset(shift[:, :], 0.0))
            ch.link(pool.affine_select(out=shift[:, :], in_=shift[:, :], compare_op=ALU.not_equal, fill=1.0,
                                       base=-HALO, pattern=[[-1, TO]], channel_multiplier=1))
            ch.link(pool.iota(ecol.bitcast(I32), pattern=[[1, E]], base=-E, channel_multiplier=0))
            ch.link(pool.iota(ebase.bitcast(I32), pattern=[[REGION, E]], base=0, channel_multiplier=0))
            ch.link(pool.iota(t_tau[:, :].bitcast(I32), pattern=[[1, NTILE]], base=0, channel_multiplier=0))
            ch.link(pool.iota(tokid.bitcast(I32), pattern=[[TO, CT], [0, 2]], base=0, channel_multiplier=1))
            ch.link(pool.memset(pad[:, :], 0.0))
            ch.link(pool.iota(pad[:, D + 1:D + 2].bitcast(I32), pattern=[[0, 1]], base=2 * TOK, channel_multiplier=1))
            ch.link(pool.memset(q_bd[0:64, :, :, 64:128], 0.0))
            ch.link(pool.memset(q_bd[64:128, :, :, 0:64], 0.0))
            ch.link(pool.memset(k_bd[0:64, :, :, 64:128], 0.0))
            ch.link(pool.memset(k_bd[64:128, :, :, 0:64], 0.0))
            pool.sem_inc(s("consts"), 1)
            pool.wait_ge(s("a_xn"), RT * B)
            ch.link(pool.memset(zt[0:64, :, 64:128], 0.0))
            ch.link(pool.memset(zt[64:128, :, 0:64], 0.0))
            pool.sem_inc(s("zt_zero"), 1)
            pool.wait_ge(s("b_a"), 2 * B)
            ch.link(pool.memset(v3[0:64, :, :, 64:128], 0.0))
            ch.link(pool.memset(v3[64:128, :, :, 0:64], 0.0))
            pool.sem_inc(s("v3_zero"), 1)
            pool.wait_ge(s("b_sums"), 2)
            pool.partition_all_reduce(zz[:, 2:4], zz[:, 0:2], P, bass.bass_isa.ReduceOp.max).then_inc(s("b_gmax"), 1)
            pool.wait_ge(s("b_scale"), 1)
            pool.tensor_scalar(z, att, zz[:, 1:2], 0.0, ALU.mult, ALU.add).then_inc(s("i_z0"), 1)
            pool.tensor_scalar(zt, zt, zz[:, 1:2], 0.0, ALU.mult, ALU.add).then_inc(s("i_z0"), 1)
            pool.wait_ge(s("band_in"), 16)
            pool.tensor_tensor(band, band, shift[:, :].unsqueeze(1).to_broadcast([P, H, TO]), ALU.add)\
                .then_inc(s("band_ok"), 1)
            pool.wait_ge(s("bfc_in"), 16)

            def inverse_deviation(b, t):
                u, q = t % 2, CT * b + t
                pool.wait_ge(s("c2_guess"), q + 1)
                v, r, w = zz[:, 4 + u:5 + u], rs2[:, u:u + 1], tm2[:, u:u + 1]
                for n in range(3):
                    ch.link(pool.tensor_tensor(w, r, r, ALU.mult))
                    ch.step(pool.tensor_tensor(w, w, v, ALU.mult))
                    wait_alone(pool, "pool_chain", ch.base + ch.n)
                    ch.link(pool.tensor_scalar(w, w, -0.5, 1.5, ALU.mult, ALU.add))
                    if n < 2:
                        ch.link(pool.tensor_tensor(r, r, w, ALU.mult))
                    else:
                        pool.tensor_tensor(r, r, w, ALU.mult).then_inc(s("c2_rs"), 1)

            def add_bias(b, t):
                rows, u = (TO if t < CT - 1 else LAST), t % 2
                pool.wait_ge(s(f"c2_xr_in{u}"), 16 * use2(b, t))
                pool.tensor_tensor(xr[0:rows, u], xr[0:rows, u], bfc[0:rows], ALU.add).then_inc(s("c2_xrb"), 1)

            def weigh(b, t):
                u, q = t % 2, CT * b + t
                pool.wait_ge(s("c2_rinv"), q + 1)
                pool.wait_ge(s("c2_conv"), 1 + (q - 1 if t >= 1 else CT * b))
                pool.tensor_tensor(a1[:, u], ex[:, u].rearrange("p (h c) -> p h c", h=H),
                                   ri[:, 16 * u:16 * u + 16].unsqueeze(2).to_broadcast([P, H, M]),
                                   ALU.mult).then_inc(s("c2_a1"), 1)

            def scatter(b, t):
                rows, u = (TO if t < CT - 1 else LAST), routed(b, t)[0]
                for c in range(2):
                    pool.indirect_dma_start(
                        out=xs_d, out_offset=bass.IndirectOffsetOnAxis(ap=idx[0:rows, u, t % G, c:c + 1].bitcast(U32), axis=0),
                        in_=xds[u][0:rows, t % G, c], in_offset=None).then_inc(s(f"d_sc{u}"), 16)

            def scatter_two(b, t):
                pool.wait_ge(s(f"d_x_in{routed(b, t)[0]}"), 16 * x_loads(b, t))
                wait_alone(pool, "d_meta", group(b, t))
                scatter(b, t - 1)
                scatter(b, t)

            def group_sent(b, t):
                u, n = routed(b, t)
                pool.wait_ge(s(f"d_sc{u}"), 32 * G * (n + 1))
                pool.sem_inc(s(f"d_free{u}"), 1)

            def c2_pool(b, t, tile, route, first, last):
                tile(add_bias, 2)
                tile(weigh, 0)
                route(lambda b, t: group_sent(b, t - 1), 3)
                tile(inverse_deviation, 3)
                route(scatter, 2)
                route(scatter_two, 1)
                if t == CT - 1 and not last:
                    route(group_sent, 2)

            c2_batches(pool, c2_pool, CT, ch, 11 * CT)
            for u in range(2):
                pool.wait_ge(s(f"x1_out{u}"), 1 + 16 * use2(B - 1, CT - 2 + (CT - u) % 2))

            def add_rows(i, first):
                for v in range(4):
                    if v > 0:
                        pool.wait_ge(s(f"m_sc{v - 1}"), 16 * (i + 1))
                    elif not first:
                        pool.wait_ge(s("m_sc3"), 16 * i)
                    wait_alone(pool, "m_y", 4 * i + v + 1)
                    pool.indirect_dma_start(
                        out=out_rows, out_offset=bass.IndirectOffsetOnAxis(ap=xs[:, v, D + 1:D + 2].bitcast(U32), axis=0),
                        in_=ys[:, v], in_offset=None, bounds_check=TOK - 1, oob_is_err=False,
                        compute_op=ALU.add).then_inc(s(f"m_sc{v}"), 16)

            out_rows = out.rearrange("b n c -> (b n) c")
            add_rows(0, True)
            with pool.Fori(1, NTILE // 4) as i:
                add_rows(i, False)

        @block.scalar
        def _(act):
            act.wait_ge(s("a_consts"), 1)
            with act.Fori(0, B // 2) as i:
                for u in range(2):
                    b = 2 * i + u
                    act.wait_ge(s(f"a_xnt_out{u}"), 1 + 16 * i)
                    for half in range(2):
                        act.wait_ge(s("a_tp"), 2 * b + half + 1)
                        for k in range(KD):
                            act.activation(xnts[u][:, k, HALO + 512 * half:HALO + 512 * half + 512],
                                           bank(2 * half + k), ACT.Copy).then_inc(s("a_xnt"), 1)
                    act.wait_ge(s("a_lmmm"), b + 1)
                    act.activation(xm[:, :, bass.ds(M * b, M)], bank(4)[:, 0:KD * M].rearrange("p (k m) -> p k m", k=KD),
                                   ACT.Copy).then_inc(s("a_lm"), 1)
                    act.wait_ge(s("a_xnt"), 1 + 4 * b + 4)
                    act.dma_start(xnt_d[b].rearrange("p (k n) -> p k n", k=KD), xnts[u]).then_inc(s(f"a_xnt_out{u}"), 16)
            act.wait_ge(s("consts"), 1)
            for j in range(J):
                act.wait_ge(s("b_lm"), 2 * j + 1)
                act.activation(q_bd[0:64, j, :, 0:64], bank(2 * j % 8)[0:64, 0:B * M].rearrange("p (b m) -> p b m", b=B),
                               ACT.Copy, scale=DH ** -0.5 / (N // M)).then_inc(s("b_q_act"), 1)
                act.wait_ge(s("b_lm"), 2 * j + 2)
                act.activation(k_bd[0:64, j, :, 0:64], bank((2 * j + 1) % 8)[0:64, 0:B * M].rearrange("p (b m) -> p b m", b=B),
                               ACT.Copy, scale=1.0 / (N // M)).then_inc(s("b_k_act"), 1)
                act.activation(k_st[0:64, j], bank((2 * j + 1) % 8)[0:64, 0:B * M].rearrange("p (b m) -> p b m", b=B),
                               ACT.Copy, scale=1.0 / (N // M)).then_inc(s("b_k_act"), 1)
            for g in range(B):
                act.wait_ge(s("b_sub"), g + 1)
                act.activation(sm2[:, J * g:J * g + J], sm2[:, J * g:J * g + J], ACT.Exp).then_inc(s("b_exp"), 1)
            for g in range(4):
                act.wait_ge(s("b_at_tp"), 2 * g + 1)
                act.activation(att[:, 8 * g:8 * g + 4], bank(2 * g).rearrange("p (q c) -> p q c", q=4),
                               ACT.Copy).then_inc(s("b_at_act"), 1)
            act.wait_ge(s("a_xnt_out1"), 1 + 16 * B // 2)
            def c1_tail(b, j):
                q = J * b + j
                act.wait_ge(s("c1_ut"), 1 + q + 1)
                act.wait_ge(s("c1_v3mm"), 1 + q)
                act.activation(utb, bank(6)[:, 0:KD * P].rearrange("p (k c) -> p k c", k=KD), ACT.Copy)\
                   .then_inc(s("c1_utb"), 1)

            with act.Fori(0, B) as b:
                for k in range(KD):
                    act.wait_ge(s("c1_g3mm"), 2 * b + k + 1)
                    act.activation(g3[:, k], bank(2 * k, 2), ACT.Copy).then_inc(s("c1_g3"), 1)
                for j in range(J):
                    u, q = j % 2, J * b + j
                    act.wait_ge(s("c1_nmx"), q + 1)
                    act.wait_ge(s("c1_tp"), 1 + (q - 1 if j >= 1 else J * b))
                    act.activation(ex[:, u], bank(2 * u, 2), ACT.Exp, bias=nmx[:, u:u + 1],
                                   accum_out=s3[:, u:u + 1]).then_inc(s("c1_exp"), 1)
                    if j >= 1:
                        c1_tail(b, j - 1)
                    act.wait_ge(s("c1_tp"), 1 + q + 1)
                    act.wait_ge(s("c1_ut"), 1 + q)
                    act.activation(e3t[:, 0:4], bank(4).rearrange("p (t c) -> p t c", t=4), ACT.Copy)\
                       .then_inc(s("c1_e3a"), 1)
                c1_tail(b, J - 1)
            with act.Fori(0, ITERS) as it:
                for g in range(4):
                    act.wait_ge(s("i_zmm"), 4 * it + g + 1)
                    act.activation(z[:, 8 * g:8 * g + 8], bank(2 * g, 2).rearrange("p (q c) -> p q c", q=8),
                                   ACT.Copy).then_inc(s("i_z"), 1)
                for g in range(4):
                    act.wait_ge(s("i_ztp"), g + 1 + 4 * it)
                    act.activation(zt[:, 8 * g:8 * g + 8], bank(2 * g, 2).rearrange("p (q c) -> p q c", q=8),
                                   ACT.Copy).then_inc(s("i_zt"), 1)
            for g in range(NQ // 4):
                act.wait_ge(s("p_wt_mm"), g + 1)
                if g >= 2:
                    act.wait_ge(s("p_mm"), g - 1)
                act.activation(wts[:, g % 2], bank(g % 2).rearrange("p (s c) -> p s c", s=4), ACT.Copy)\
                   .then_inc(s("p_wt"), 1)
            def store_rows(b, t):
                rows, u, q = (TO if t < CT - 1 else LAST), t % 2, CT * b + t
                act.wait_ge(s(f"c2_x1_{u}"), 1 + use2(b, t))
                act.dma_start(out[b, TO * t:TO * t + rows, :], x1[0:rows, u]).then_inc(s(f"x1_out{u}"), 16)

            def store_norm(b, t):
                rows, u, q = (TO if t < CT - 1 else LAST), t % 2, CT * b + t
                act.wait_ge(s("c2_x1n"), 1 + q + 1)
                act.dma_start(x1n_d[b, TO * t:TO * t + rows, :], x1n[0:rows, u]).then_inc(s(f"x1n_out{u}"), 16)

            def norm_columns(b, t):
                rows, q = (TO if t < CT - 1 else LAST), CT * b + t
                act.wait_ge(s("c2_x1tp"), 1 + q + 1)
                act.wait_ge(s("c2_lgmm"), 1 + q)
                act.activation(x1t[:, :, 0:rows], bank(7)[:, 0:KD * rows].rearrange("p (k c) -> p k c", k=KD),
                               ACT.Copy).then_inc(s("c2_x1t"), 1)

            def g1_out(b, t):
                for k in range(KD):
                    act.wait_ge(s("c2_g1mm"), 2 * b + k + 1)
                    act.activation(g1[:, k], bank(2 * k, 2), ACT.Copy, scale=DH ** -0.5).then_inc(s("c2_g1"), 1)

            def exponentials(b, t):
                act.wait_ge(s("c2_sub"), 1 + CT * b + t + 1)
                act.activation(ex[:, t % 2], ex[:, t % 2], ACT.Exp).then_inc(s("c2_exp"), 1)

            def conv_out(b, t):
                u, q = t % 2, CT * b + t
                act.wait_ge(s("c2_conv"), 1 + q + 1)
                act.wait_ge(s("c2_y"), 1 + (q - 1 if t >= 1 else CT * b))
                act.activation(cvt[:, u], bank(4, 2).rearrange("p (j c) -> p j c", j=J)[:, :, 0:TO],
                               ACT.Copy).then_inc(s("c2_cvt"), 1)

            def gap_exponentials(b, t):
                act.wait_ge(s("d_hot"), group(b, t))
                act.activation(gap_exp, gap, ACT.Exp, scale=-1.0).then_inc(s("d_exp"), 1)

            def c2_act(b, t, tile, route, first, last):
                if t > 0:
                    tile(exponentials, 0)
                tile(conv_out, 1)
                if t == 0:
                    tile(g1_out, 0)
                    tile(norm_columns, 4)
                    tile(exponentials, 0)
                tile(store_rows, 3)
                tile(store_norm, 4)
                if t > 0:
                    tile(norm_columns, 4)
                route(gap_exponentials, 0)

            c2_batches(act, c2_act, CT)
            act.wait_ge(s("d_size"), 1)
            for e in range(E // 2, E):
                pad_region(act, e)
            def xs_columns(n, v, free):
                act.wait_ge(s("m_xtp"), n + 1)
                if not free:
                    act.wait_ge(s("m_up"), n - 1)
                act.activation(xst[:, v % 2], bank(6)[:, 0:D].rearrange("p (k c) -> p k c", k=KD), ACT.Copy)\
                   .then_inc(s("m_xst"), 1)

            def hidden_columns(n, v, free):
                act.wait_ge(s("m_htp"), n + 1)
                if not free:
                    act.wait_ge(s("m_down"), n - 1)
                act.activation(hidt[:, v % 2], bank(4).rearrange("p (f c) -> p f c", f=4), ACT.Copy)\
                   .then_inc(s("m_ht"), 1)

            def expert_tiles(i, first, last):
                for v in range(4):
                    n = 4 * i + v
                    act.wait_ge(s("m_gate"), n + 1)
                    if not (first and v < 2):
                        act.wait_ge(s("m_hid"), n - 1)
                    act.activation(sil[:, v % 2], bank(v % 2), ACT.Silu).then_inc(s("m_sil"), 1)
                    if not (first and v == 0):
                        hidden_columns(n - 1, v + 3, first and v < 3)
                    if not (last and v == 3):
                        xs_columns(n + 1, v + 1, first and v == 0)

            xs_columns(0, 0, True)
            expert_tiles(0, True, False)
            with act.Fori(1, NTILE // 4 - 1) as i:
                expert_tiles(i, False, False)
            expert_tiles(NTILE // 4 - 1, False, True)
            hidden_columns(NTILE - 1, 3, False)
        @block.vector
        def _(dve):
            ch = Chain(dve, s("dve_chain"))
            def normalise(i, u):
                b = 2 * i + u
                for t in range(RT):
                    if t % (RT // 2) == 0:
                        dve.wait_ge(s(f"a_x_in{u}{t // (RT // 2)}"), 16 * (i + 1))
                    ch.step(dve.bn_stats(stats[:, t], xbs[:, u, t]))
                wait_alone(dve, "dve_chain", ch.base + ch.n)
                for t in range(RT):
                    ch.step(dve.bn_aggr(mv[:, t], stats[:, t]))
                ch.sync()
                ch.link(dve.tensor_scalar(ve, mv[:, :, 1], EPS, None, ALU.add))
                ch.link(dve.tensor_scalar(rs.bitcast(I32), ve.bitcast(I32), -0.5, RSQRT_MAGIC, ALU.mult, ALU.add))
                for _ in range(3):
                    ch.link(dve.tensor_tensor(tmp, rs, rs, ALU.mult))
                    ch.link(dve.scalar_tensor_tensor(out=tmp, in0=tmp, scalar=-0.5, in1=ve, op0=ALU.mult, op1=ALU.mult))
                    ch.link(dve.scalar_tensor_tensor(out=rs, in0=tmp, scalar=1.5, in1=rs, op0=ALU.add, op1=ALU.mult))
                for t in range(RT):
                    dve.tensor_scalar(xna[:, b, t], xbs[:, u, t], mv[:, t, 0:1], rs[:, t:t + 1],
                                      ALU.subtract, ALU.mult).then_inc(s("a_xn"), 1)

            with dve.Fori(0, B // 2) as i:
                ch.enter(i, 2 * (2 * RT + 11))
                for u in range(2):
                    normalise(i, u)
                ch.leave(B // 2)
            dve.wait_ge(s("consts"), 1)
            for j in range(J):
                dve.wait_ge(s("b_lm"), 2 * j + 1)
                dve.tensor_scalar(q_bd[64:128, j, :, 64:128], bank(2 * j % 8)[64:128, 0:B * M].rearrange("p (b m) -> p b m", b=B),
                                  DH ** -0.5 / (N // M), None, ALU.mult).then_inc(s("b_q_dve"), 1)
                dve.wait_ge(s("b_lm"), 2 * j + 2)
                dve.tensor_scalar(k_bd[64:128, j, :, 64:128],
                                  bank((2 * j + 1) % 8)[64:128, 0:B * M].rearrange("p (b m) -> p b m", b=B),
                                  1.0 / (N // M), None, ALU.mult).then_inc(s("b_k_dve"), 1)
                dve.tensor_scalar(k_st[64:128, j], bank((2 * j + 1) % 8)[64:128, 0:B * M].rearrange("p (b m) -> p b m", b=B),
                                  1.0 / (N // M), None, ALU.mult).then_inc(s("b_k_dve"), 1)
            def sim2_less_max(g):
                sl = slice(J * g, J * g + J)
                dve.wait_ge(s("b_sim2"), g + 1)
                pg = bank(g).rearrange("p (q c) -> p q c", q=J)
                ch.link(dve.tensor_reduce(mx2[:, sl], pg, AX, ALU.max))
                dve.tensor_tensor(sm2[:, sl], pg, mx2[:, sl].unsqueeze(2).to_broadcast([P, J, M]), ALU.subtract)\
                   .then_inc(s("b_sub"), 1)

            def sim2_weigh(g):
                sl = slice(J * g, J * g + J)
                dve.wait_ge(s("b_exp"), g + 1)
                ch.link(dve.tensor_reduce(sm2s[:, sl], sm2[:, sl], AX, ALU.add))
                ch.link(dve.reciprocal(ri2[:, sl], sm2s[:, sl]))
                for hf in range(2):
                    r = slice(64 * hf, 64 * hf + 64)
                    dve.tensor_tensor(zt[r, sl, 64 * hf:64 * hf + 64], sm2[r, sl],
                                      ri2[r, sl].unsqueeze(2).to_broadcast([64, J, M]), ALU.mult).then_inc(s("b_a"), 1)

            dve.wait_ge(s("zt_zero"), 1)
            for g in range(B):
                sim2_less_max(g)
                if g >= 1:
                    sim2_weigh(g - 1)
            sim2_weigh(B - 1)
            dve.wait_ge(s("b_a"), 2 * B)
            for g in range(4):
                dve.wait_ge(s("b_at_tp"), 2 * g + 2)
                dve.tensor_copy(att[:, 8 * g + 4:8 * g + 8], bank(2 * g + 1).rearrange("p (q c) -> p q c", q=4))\
                   .then_inc(s("b_at_dve"), 1)
            ch.link(dve.tensor_reduce(mx2, zt, AX, ALU.add))
            dve.tensor_reduce(zz[:, 0:1], mx2, AX, ALU.max).then_inc(s("b_sums"), 1)
            dve.wait_ge(s("b_at_dve"), 4)
            dve.wait_ge(s("b_at_act"), 4)
            ch.link(dve.tensor_reduce(sm2s, att, AX, ALU.add))
            dve.tensor_reduce(zz[:, 1:2], sm2s, AX, ALU.max).then_inc(s("b_sums"), 1)
            dve.wait_ge(s("b_gmax"), 1)
            ch.link(dve.tensor_tensor(zz[:, 0:1], zz[:, 2:3], zz[:, 3:4], ALU.mult))
            dve.reciprocal(zz[:, 1:2], zz[:, 0:1]).then_inc(s("b_scale"), 1)

            def c1_tail(b, j):
                q, u = J * b + j, j % 2
                dve.wait_ge(s("c1_v3mm"), 1 + q + 1)
                for hf in range(2):
                    r = slice(64 * hf, 64 * hf + 64)
                    dve.tensor_scalar(v3[r, b, j, 64 * hf:64 * hf + 64], bank(7)[r, 64 * hf:64 * hf + 64],
                                      r3[r, u:u + 1], None, ALU.mult).then_inc(s("c1_v3"), 1)

            with dve.Fori(0, B) as b:
                ch.enter(b, 2 * J)
                for j in range(J):
                    u, q = j % 2, J * b + j
                    dve.wait_ge(s("c1_sim"), 1 + q + 1)
                    ch.link(dve.tensor_reduce(mx[:, u:u + 1], bank(2 * u, 2), AX, ALU.max))
                    dve.wait_ge(s("c1_exp"), 1 + (q - 1 if j >= 1 else J * b))
                    dve.tensor_scalar(nmx[:, u:u + 1], mx[:, u:u + 1], -1.0, None, ALU.mult).then_inc(s("c1_nmx"), 1)
                    if j >= 2:
                        c1_tail(b, j - 2)
                    dve.wait_ge(s("c1_tp"), 1 + q + 1)
                    dve.wait_ge(s("c1_ut"), 1 + q)
                    dve.tensor_copy(e3t[:, 4:8], bank(5).rearrange("p (t c) -> p t c", t=4)).then_inc(s("c1_e3b"), 1)
                    dve.wait_ge(s("c1_v3"), 1 + 2 * (q - 1 if j >= 1 else q))
                    dve.wait_ge(s("c1_exp"), 1 + q + 1)
                    ch.link(dve.reciprocal(r3[:, u:u + 1], s3[:, u:u + 1]))
                c1_tail(b, J - 2)
                c1_tail(b, J - 1)
                ch.leave(B)
            def bracket(name_in, count, g, c, eye, dst, name_out):
                dve.wait_ge(s(name_in), count)
                dve.scalar_tensor_tensor(out=dst[:, 8 * g:8 * g + 8], in0=bank(2 * g, 2).rearrange("p (q c) -> p q c", q=8),
                                         scalar=c, in1=eye.unsqueeze(1).to_broadcast([P, 8, P]),
                                         op0=ALU.mult, op1=ALU.add).then_inc(s(name_out), 1)

            with dve.Fori(0, ITERS) as it:
                for g in range(4):
                    bracket("i_azmm", 4 * it + g + 1, g, -1.0, eye7, tt, "i_t1")
                for g in range(4):
                    bracket("i_t1tp", 4 * it + g + 1, g, -1.0, eye7, azt, "i_azt")
                for g in range(4):
                    bracket("i_t1mm", 4 * it + g + 1, g, -1.0, eye15, tt, "i_t2")
                for g in range(4):
                    bracket("i_t2mm", 4 * it + g + 1, g, -0.25, eye13, tt, "i_t3")

            def rows_out(b, t):
                rows, u, q = (TO if t < CT - 1 else LAST), t % 2, CT * b + t
                dve.wait_ge(s("c2_y"), 1 + q + 1)
                dve.wait_ge(s("c2_xrb"), q + 1)
                dve.wait_ge(s(f"x1_out{u}"), 1 + 16 * (use2(b, t) - 1))
                dve.wait_ge(s("c2_x1n"), 1 + (q - 1 if t >= 1 else CT * b))
                dve.tensor_tensor(x1[0:rows, u], bank(6)[0:rows, 0:D], xr[0:rows, u], ALU.add)\
                   .then_inc(s(f"c2_x1_{u}"), 1)

            def statistics(b, t):
                rows, u = (TO if t < CT - 1 else LAST), t % 2
                dve.wait_ge(s(f"c2_x1_{u}"), 1 + use2(b, t))
                ch.step(dve.bn_stats(st2[0:rows, u], x1[0:rows, u]))
                wait_alone(dve, "dve_chain", ch.base + ch.n)
                ch.link(dve.bn_aggr(mv2[0:rows, u], st2[0:rows, u]))
                ch.link(dve.tensor_scalar(zz[:, 4 + u:5 + u], mv2[:, u, 1:2], EPS, None, ALU.add))
                dve.tensor_scalar(rs2[:, u:u + 1].bitcast(I32), zz[:, 4 + u:5 + u].bitcast(I32), -0.5, RSQRT_MAGIC,
                                  ALU.mult, ALU.add).then_inc(s("c2_guess"), 1)

            def norm_rows(b, t):
                rows, u, q = (TO if t < CT - 1 else LAST), t % 2, CT * b + t
                dve.wait_ge(s("c2_rs"), q + 1)
                dve.wait_ge(s(f"x1n_out{u}"), 1 + 16 * (use2(b, t) - 1))
                dve.wait_ge(s("c2_x1tp"), 1 + (q - 1 if t >= 1 else CT * b))
                dve.tensor_scalar(x1n[0:rows, u], x1[0:rows, u], mv2[0:rows, u, 0:1], rs2[0:rows, u:u + 1],
                                  ALU.subtract, ALU.mult).then_inc(s("c2_x1n"), 1)

            def logits_out(b, t):
                rows, q = (TO if t < CT - 1 else LAST), CT * b + t
                dve.wait_ge(s("c2_lgmm"), 1 + q + 1)
                dve.tensor_copy(logits[0:rows, t], bank(7)[0:rows, 256:256 + E]).then_inc(s("c2_lg"), 1)

            for g in range(NQ // 4):
                dve.wait_ge(s("p_mm"), g + 1)
                dve.tensor_copy(pm[:, g // 2, 4 * (g % 2):4 * (g % 2) + 4],
                                bank(2 + 2 * (g % 2), 2).rearrange("p (s c) -> p s c", s=4)).then_inc(s("p_pm"), 1)
            ch.step(dve.memset(mv2, 1.0))
            ch.step(dve.memset(logits, 0.0))
            for v in (ecol, ebase, t_tau[:, :]):
                ch.step(dve.tensor_copy(v, v.bitcast(I32)))
            ch.sync()
            ch.link(dve.tensor_copy(run[:, :], ebase))
            ec = lambda a: a.unsqueeze(1).to_broadcast([P, G, E])
            bc = lambda a: a.unsqueeze(2).to_broadcast([P, G, E])

            def choices(b, t):
                dve.wait_ge(s("c2_lg"), 1 + CT * b + t + G)
                lg = logits[:, t:t + G]
                ch.link(dve.scalar_tensor_tensor(out=ab, in0=lg, scalar=-1.0, in1=lg, op0=ALU.mult, op1=ALU.max))
                for c in range(2):
                    if c == 1:
                        ch.link(dve.scalar_tensor_tensor(out=t2, in0=one_hot[:, 0], scalar=-BIG, in1=lg,
                                                         op0=ALU.mult, op1=ALU.add))
                        lg = t2
                    ch.link(dve.tensor_reduce(top[:, c], lg, AX, ALU.max))
                    ch.link(dve.tensor_tensor(gap[:, c], bc(top[:, c]), lg, ALU.subtract))
                    ch.link(dve.scalar_tensor_tensor(out=t1, in0=gap[:, c], scalar=0.0, in1=ec(ecol),
                                                     op0=ALU.is_equal, op1=ALU.mult))
                    ch.link(dve.tensor_reduce(first_e, t1, AX, ALU.min))
                    ch.link(dve.tensor_tensor(one_hot[:, c], bc(first_e), ec(ecol), ALU.is_equal))
                ch.link(dve.tensor_tensor(t1, one_hot[:, 0], one_hot[:, 1], ALU.add))
                full = G if t + G < CT else G - 1
                if full < G:
                    ch.link(dve.tensor_scalar(hot[:, full], t1[:, full], validf[:, 3:4], None, ALU.mult))
                dve.tensor_scalar(hot[:, 0:full], t1[:, 0:full], validf[:, 2:3], None, ALU.mult).then_inc(s("d_hot"), 1)

            def take_counts(b, t):
                dve.wait_ge(s("d_cnt"), group(b, t))
                dve.tensor_copy(cnt, bank(7)[:, 272:272 + 2 * G * E].rearrange("p (r v e) -> p r v e", r=2, v=G))\
                   .then_inc(s("d_taken"), 1)

            def slots(b, t):
                t -= 1
                dve.wait_ge(s("d_exp"), group(b, t))
                for c in range(2):
                    ch.link(dve.tensor_tensor(t1, ab, bc(top[:, c]), ALU.max))
                    ch.link(dve.scalar_tensor_tensor(out=t1, in0=t1, scalar=JITTER2, in1=gap[:, c],
                                                     op0=ALU.mult, op1=ALU.is_ge))
                    ch.link(dve.tensor_tensor(t1, t1, gap_exp[:, c], ALU.mult))
                    ch.link(dve.tensor_reduce(weight[:, :, c], t1, AX, ALU.add))
                ch.link(dve.reciprocal(weight, weight))
                dve.wait_ge(s("d_taken"), group(b, t))
                for v in range(G):
                    ch.step(dve.tensor_tensor(pos[:, v], cnt[:, 0, v], run[:, :], ALU.add))
                    ch.link(dve.tensor_tensor(run[:, :], cnt[:, 1, v], run[:, :], ALU.add))
                for c in range(2):
                    ch.link(dve.tensor_tensor(t1, one_hot[:, c], pos, ALU.mult))
                    ch.link(dve.tensor_reduce(slot[:, :, c], t1, AX, ALU.add))
                u, n = routed(b, t)
                dve.wait_ge(s(f"d_free{u}"), 1 + n)
                ch.step(dve.tensor_copy(xds[u][:, :, :, D], weight))
                ch.step(dve.tensor_copy(xds[u][:, :, :, D + 1].bitcast(I32), tokid[:, t:t + G].bitcast(I32)))
                ch.step(dve.tensor_copy(idx[:, u].bitcast(I32), slot))
                ch.sync()
                dve.tensor_scalar(tokid[:, t:t + G].bitcast(I32), tokid[:, t:t + G].bitcast(I32), float(N), None,
                                  ALU.add).then_inc(s("d_meta"), 1)


            def less_max(b, t):
                u, q = t % 2, CT * b + t
                m, sc = mx[:, 16 * u:16 * u + 16], bank(2 * u, 2).rearrange("p (h c) -> p h c", h=H)
                dve.wait_ge(s("c2_sim"), 1 + q + 1)
                ch.link(dve.tensor_reduce(m, sc, AX, ALU.max))
                dve.wait_ge(s("c2_a1"), 1 + (q - 1 if t >= 1 else CT * b))
                dve.tensor_tensor(ex[:, u].rearrange("p (h c) -> p h c", h=H), sc,
                                  m.unsqueeze(2).to_broadcast([P, H, M]), ALU.subtract).then_inc(s("c2_sub"), 1)

            def inverse_sums(b, t):
                u, q = t % 2, CT * b + t
                sums, inv = sm[:, 16 * u:16 * u + 16], ri[:, 16 * u:16 * u + 16]
                dve.wait_ge(s("c2_exp"), q + 1)
                ch.link(dve.tensor_reduce(sums, ex[:, u].rearrange("p (h c) -> p h c", h=H), AX, ALU.add))
                if t in (0, CT - 1):
                    ch.link(dve.reciprocal(inv, sums))
                    dve.tensor_scalar(inv, inv, validf[:, t // (CT - 1):t // (CT - 1) + 1], None, ALU.mult)\
                       .then_inc(s("c2_rinv"), 1)
                else:
                    dve.reciprocal(inv, sums).then_inc(s("c2_rinv"), 1)

            def c2_dve(b, t, tile, route, first, last):
                if t == 3:
                    tile(less_max, 0)
                    tile(norm_rows, 4)
                tile(rows_out, 3)
                if t not in (0, 3):
                    tile(less_max, 0)
                route(take_counts, 1)
                tile(logits_out, 5)
                if t != 3:
                    tile(norm_rows, 4)
                tile(statistics, 3)
                if t == 0:
                    route(choices, 0)
                    tile(less_max, 0)
                tile(inverse_sums, 0)
                if t > 0:
                    route(choices, 0)
                route(slots, 1)

            c2_batches(dve, c2_dve, CT, ch, CT * 5 + 2 + CT // G * (13 + 22) + 1)
            dve.wait_ge(s("c2_conv"), 1 + QT)
            dve.wait_ge(s("c2_sim"), 1 + QT)
            dve.wait_ge(s("d_meta"), group(B - 1, CT - 1))
            ch.link(dve.tensor_tensor(n_e, run[:, :], ebase, ALU.subtract))
            dve.tensor_copy(n_pad[:, :].bitcast(I32), n_e).then_inc(s("d_size"), 1)
            ch.link(dve.tensor_scalar(te.bitcast(I32), n_e, float(P - 1), None, ALU.add))
            ch.link(dve.tensor_scalar(te.bitcast(I32), te.bitcast(I32), 7, None, ALU.logical_shift_right))
            ch.link(dve.tensor_copy(nt, te.bitcast(I32)))
            ch.link(dve.tensor_copy(te, nt))
            src, dst, sh = te, tb, 1
            while sh < E:
                ch.step(dve.tensor_copy(dst[:, 0:sh], src[:, 0:sh]))
                ch.link(dve.tensor_tensor(dst[:, sh:], src[:, sh:], src[:, 0:E - sh], ALU.add))
                src, dst, sh = dst, src, 2 * sh
            ends = src
            ch.link(dve.tensor_tensor(tc, ends, nt, ALU.subtract))
            ch.link(dve.scalar_tensor_tensor(out=tc, in0=tc, scalar=-float(P), in1=ebase, op0=ALU.mult, op1=ALU.add))
            big = ex[:, 0, 0:NTILE * E].rearrange("p (t e) -> p t e", t=NTILE)
            tbc = lambda a: a.unsqueeze(2).to_broadcast([P, NTILE, E])
            tec = lambda a: a.unsqueeze(1).to_broadcast([P, NTILE, E])
            ch.link(dve.tensor_tensor(big, tbc(t_tau[:, :]), tec(ends), ALU.is_ge))
            ch.link(dve.tensor_reduce(t_eid[:, :], big, AX, ALU.add))
            ch.link(dve.tensor_scalar(t_a[:, :], t_eid[:, :], -float(E), None, ALU.add))
            ch.link(dve.tensor_tensor(big, tbc(t_a[:, :]), tec(ecol), ALU.is_equal))
            ch.link(dve.tensor_tensor(big, big, tec(tc), ALU.mult))
            ch.link(dve.tensor_reduce(t_row[:, :], big, AX, ALU.add))
            ch.link(dve.scalar_tensor_tensor(out=t_row[:, :], in0=t_tau[:, :], scalar=float(P), in1=t_row[:, :],
                                             op0=ALU.mult, op1=ALU.add))
            ch.link(dve.tensor_scalar(t_a[:, :], t_a[:, :], 0.0, None, ALU.is_equal))
            ch.link(dve.tensor_scalar(t_tau[:, :], t_row[:, :], -1.0, float(ZROW), ALU.mult, ALU.add))
            ch.link(dve.tensor_tensor(t_tau[:, :], t_tau[:, :], t_a[:, :], ALU.mult))
            ch.link(dve.tensor_tensor(t_row[:, :].bitcast(I32), t_row[:, :], t_tau[:, :], ALU.add))
            ch.link(dve.tensor_scalar(t_eid[:, :].bitcast(I32), t_eid[:, :], float(E - 1), None, ALU.min))
            dve.memset(t_a[:, 0:1], 0.0).then_inc(s("d_tab"), 1)
            def expert_out(i, n, v, free):
                dve.wait_ge(s("m_down"), n + 1)
                if not free:
                    dve.wait_ge(s(f"m_sc{v}"), 16 * i)
                dve.tensor_scalar(ys[:, v], bank(5)[:, 0:D], xs[:, v, D:D + 1], None, ALU.mult).then_inc(s("m_y"), 1)

            def expert_tiles(i, first, second):
                for v in range(4):
                    n = 4 * i + v
                    dve.wait_ge(s("m_sil"), n + 1)
                    dve.wait_ge(s("m_up"), n + 1)
                    if not (first and v < 2):
                        dve.wait_ge(s("m_htp"), n - 1)
                    dve.tensor_tensor(hid[:, v % 2], sil[:, v % 2], bank(2 + v % 2), ALU.mult).then_inc(s("m_hid"), 1)
                    if v > 0:
                        expert_out(i, n - 1, v - 1, first)
                    elif not first:
                        expert_out(i - 1, n - 1, 3, second)

            expert_tiles(0, True, False)
            expert_tiles(1, False, True)
            with dve.Fori(2, NTILE // 4) as i:
                expert_tiles(i, False, False)
            expert_out(NTILE // 4 - 1, NTILE - 1, 3, False)
        @block.tensor
        def _(pe):
            pe.wait_ge(s("a_consts"), 1)
            idt = ident[:, :]
            for b in range(B):
                for half in range(2):
                    pe.wait_ge(s("a_xnt"), 1 + 4 * b)
                    pe.wait_ge(s("a_lm"), 1 + b)
                    for t in range(4):
                        pe.wait_ge(s("a_xn"), RT * b + 4 * half + t + 1)
                        for k in range(KD):
                            mm = pe.transpose(bank(2 * half + k)[:, t * P:(t + 1) * P],
                                              xna[:, b, 4 * half + t, k * P:(k + 1) * P], idt)
                    mm.then_inc(s("a_tp"), 1)
                for t in range(RT):
                    for k in range(KD):
                        mm = pe.matmul(bank(4)[:, k * M + RT * t:k * M + RT * (t + 1)], xna[:, b, t, k * P:(k + 1) * P],
                                       sums16[:, :], start=True, stop=True)
                mm.then_inc(s("a_lmmm"), 1)
            pe.wait_ge(s("consts"), 1)
            pe.wait_ge(s("a_lm"), 1 + B)
            pe.wait_ge(s("a_xnt"), 1 + 4 * B)
            pe.wait_ge(s("w_qk_in"), 16)
            for j in range(J):
                for c in range(2):
                    n = 2 * j + c
                    if n >= 8:
                        for e_ in ("act", "dve"):
                            pe.wait_ge(s(f"b_{'qk'[c]}_{e_}"), (1 + c) * (j - 3))
                    for k in range(KD):
                        mm = pe.matmul(bank(n % 8)[:, 0:B * M], wqk[:, k, c * INNER + j * P:c * INNER + (j + 1) * P],
                                       xm[:, k], start=(k == 0), stop=(k == KD - 1))
                    mm.then_inc(s("b_lm"), 1)
            for e_ in ("act", "dve"):
                pe.wait_ge(s(f"b_q_{e_}"), J)
                pe.wait_ge(s(f"b_k_{e_}"), 2 * J)
            for g in range(B):
                for j in range(J):
                    mm = pe.matmul(bank(g)[:, j * M:(j + 1) * M], q_bd[:, j, g], k_st[:, j, g], start=True, stop=True)
                mm.then_inc(s("b_sim2"), 1)
            pe.wait_ge(s("b_sub"), B)
            for n in range(8):
                pe.wait_ge(s("b_a"), 2 * (n // 2 + 1))
                for q in range(4):
                    mm = pe.transpose(bank(n)[:, q * P:(q + 1) * P], zt[:, 4 * n + q], idt)
                mm.then_inc(s("b_at_tp"), 1)
            pe.wait_ge(s("w_in"), 16 * 5)
            pe.wait_ge(s("b_at_dve"), 4)
            pe.wait_ge(s("b_at_act"), 4)

            def c1_sim(b, j):
                q, u = J * b + j, j % 2
                pe.wait_ge(s("c1_exp"), 1 + (q - 1 if j >= 1 else J * b))
                for half in range(2):
                    for k in range(KD):
                        mm = pe.matmul(bank(2 * u + half), g3[:, k, j * P:(j + 1) * P],
                                       xnt[:, k, HALO + 512 * half:HALO + 512 * half + 512],
                                       start=(k == 0), stop=(k == KD - 1))
                mm.then_inc(s("c1_sim"), 1)

            def c1_v3(b, j):
                q = J * b + j
                pe.wait_ge(s("c1_utb"), 1 + q + 1)
                pe.wait_ge(s("c1_v3"), 1 + 2 * q)
                for k in range(KD):
                    mm = pe.matmul(bank(7)[:, 0:P], utb[:, k], wv[:, k, j * P:(j + 1) * P],
                                   start=(k == 0), stop=(k == KD - 1))
                mm.then_inc(s("c1_v3mm"), 1)

            with pe.Fori(0, B) as b:
                pe.wait_ge(s("c1_exp"), 1 + J * b)
                for k in range(KD):
                    for j in range(J):
                        mm = pe.matmul(bank(2 * k, 2)[:, j * P:(j + 1) * P], wkt[:, j, k * P:(k + 1) * P],
                                       q_bd[:, j, b], start=True, stop=True)
                    mm.then_inc(s("c1_g3mm"), 1)
                pe.wait_ge(s("c1_g3"), KD * b + KD)
                pe.wait_ge(s("c1_xnt_in"), 16 * (b + 1))
                c1_sim(b, 0)
                for j in range(J):
                    u, q = j % 2, J * b + j
                    if j == 0:
                        c1_sim(b, 1)
                    pe.wait_ge(s("c1_exp"), 1 + q + 1)
                    pe.wait_ge(s("c1_e3a"), 1 + q)
                    pe.wait_ge(s("c1_e3b"), 1 + q)
                    for t in range(RT):
                        mm = pe.transpose(bank(4 + t // 4)[:, (t % 4) * P:(t % 4 + 1) * P],
                                          ex[:, u, t * P:(t + 1) * P], idt)
                    mm.then_inc(s("c1_tp"), 1)
                    if 0 < j < J - 1:
                        c1_sim(b, j + 1)
                    if j >= 1:
                        c1_v3(b, j - 1)
                    else:
                        pe.wait_ge(s("c1_xn_in"), 16 * (b + 1))
                        pe.wait_ge(s("c1_utb"), 1 + q)
                    pe.wait_ge(s("c1_e3a"), 1 + q + 1)
                    pe.wait_ge(s("c1_e3b"), 1 + q + 1)
                    for k in range(KD):
                        for t in range(RT):
                            mm = pe.matmul(bank(6)[:, k * P:(k + 1) * P], xnb[:, t, k * P:(k + 1) * P], e3t[:, t],
                                           start=(t == 0), stop=(t == RT - 1))
                    mm.then_inc(s("c1_ut"), 1)
                c1_v3(b, J - 1)
            pe.wait_ge(s("c1_v3"), 1 + 2 * NQ)
            pe.wait_ge(s("v3_zero"), 1)
            pe.wait_ge(s("i_z0"), 2)

            def products(lhs, rhs, waits, name):
                for g in range(4):
                    for w, n in waits:
                        pe.wait_ge(s(w), n + g)
                    for q in range(8 * g, 8 * g + 8):
                        o_ = ps[:, q * P:(q + 1) * P]
                        mm = pe.transpose(o_, lhs[:, q], idt) if rhs is None else \
                            pe.matmul(o_, lhs[:, q], rhs[:, q], start=True, stop=True)
                    mm.then_inc(s(name), 1)

            with pe.Fori(0, ITERS) as it:
                pe.wait_ge(s("i_zt"), 1 + 4 * it)
                products(att, z, (), "i_azmm")
                products(tt, None, (("i_t1", 4 * it + 1),), "i_t1tp")
                products(azt, tt, (("i_azt", 4 * it + 1),), "i_t1mm")
                products(azt, tt, (("i_t2", 4 * it + 1),), "i_t2mm")
                products(zt, tt, (("i_t3", 4 * it + 1),), "i_zmm")
                products(z, None, (("i_z", 4 * it + 1),), "i_ztp")
            def landmark_values(g):
                pe.wait_ge(s("i_zt"), 1 + 4 * (ITERS - 1) + g // 2 + 1)
                if g >= 2:
                    pe.wait_ge(s("p_wt"), g - 1)
                for i in range(4):
                    q = 4 * g + i
                    mm = pe.matmul(bank(g % 2)[:, i * P:(i + 1) * P], v3[:, q // J, q % J], zt[:, q], start=True, stop=True)
                mm.then_inc(s("p_wt_mm"), 1)

            landmark_values(0)
            for g in range(NQ // 4):
                if g < NQ // 4 - 1:
                    landmark_values(g + 1)
                pe.wait_ge(s("p_wt"), g + 1)
                if g < 2:
                    pe.wait_ge(s("i_zt"), 1 + 4 * (ITERS - 1) + g + 2)
                else:
                    pe.wait_ge(s("p_pm"), g - 1)
                for i in range(4):
                    q = 4 * g + i
                    mm = pe.matmul(bank(2 + 2 * (g % 2), 2)[:, i * D:(i + 1) * D], wts[:, g % 2, i], wfc[:, q % J],
                                   start=True, stop=True)
                mm.then_inc(s("p_mm"), 1)
            pe.wait_ge(s("p_pm"), NQ // 4)

            def c2_sim(b, t):
                q, u = CT * b + t, t % 2
                pe.wait_ge(s("c2_sub"), 1 + (q - 1 if t >= 1 else CT * b))
                for half in range(2):
                    for k in range(KD):
                        mm = pe.matmul(bank(2 * u + half), xnt[:, k, TO * t:TO * t + P], g1[:, k, 512 * half:512 * half + 512],
                                       start=(k == 0), stop=(k == KD - 1))
                mm.then_inc(s("c2_sim"), 1)

            def c2_tp(b, t):
                rows, u, q = (TO if t < CT - 1 else LAST), t % 2, CT * b + t
                pe.wait_ge(s("c2_x1n"), 1 + q + 1)
                pe.wait_ge(s("c2_lg"), 1 + q)
                for k in range(KD):
                    mm = pe.transpose(bank(7)[:, k * rows:(k + 1) * rows], x1n[0:rows, u, k * P:(k + 1) * P],
                                      ident[0:rows, 0:rows])
                mm.then_inc(s("c2_x1tp"), 1)

            def c2_lg(b, t):
                rows, q = (TO if t < CT - 1 else LAST), CT * b + t
                pe.wait_ge(s("c2_x1t"), q + 1)
                for k in range(KD):
                    mm = pe.matmul(bank(7)[0:rows, 256:256 + E], x1t[:, k, 0:rows], rw[:, k * E:(k + 1) * E],
                                   start=(k == 0), stop=(k == KD - 1))
                mm.then_inc(s("c2_lgmm"), 1)

            def c2_g1(b, t):
                pe.wait_ge(s("c2_sub"), 1 + CT * b)
                for k in range(KD):
                    for j in range(J):
                        mm = pe.matmul(bank(2 * k, 2)[:, j * P:(j + 1) * P], wqt[:, j, k * P:(k + 1) * P],
                                       k_bd[:, j, b], start=True, stop=True)
                    mm.then_inc(s("c2_g1mm"), 1)

            def c2_first_sim(b, t):
                pe.wait_ge(s("c2_g1"), KD * b + KD)
                pe.wait_ge(s("c2_xnt_in"), 16 * (b + 1))
                c2_sim(b, 0)

            def c2_conv(b, t):
                u, q = t % 2, CT * b + t
                if t == 0:
                    pe.wait_ge(s("band_ok"), 1)
                pe.wait_ge(s("c2_a1"), 1 + q + 1)
                pe.wait_ge(s("c2_cvt"), 1 + q)
                for h in range(H):
                    c = 64 * (h % 2)
                    mm = pe.matmul(bank(4, 2)[c:c + 64, (h // 2) * P:(h // 2) * P + TO], a1[:, u, h], band[:, h],
                                   start=True, stop=True)
                mm.then_inc(s("c2_conv"), 1)

            def c2_y(b, t):
                rows, u, q = (TO if t < CT - 1 else LAST), t % 2, CT * b + t
                pe.wait_ge(s("c2_cvt"), 1 + q + 1)
                if t >= 1:
                    pe.wait_ge(s(f"c2_x1_{1 - u}"), 1 + use2(b, t - 1))
                else:
                    pe.wait_ge(s("c2_x1_0"), 1 + use2(b, 0) - 1)
                for j in range(J):
                    mm = pe.matmul(bank(6)[0:rows, 0:D], cvt[:, u, j, 0:rows], pm[:, b, j],
                                   start=(j == 0), stop=(j == J - 1))
                mm.then_inc(s("c2_y"), 1)

            def c2_counts(b, t):
                pe.wait_ge(s("d_hot"), group(b, t))
                for r, rows_of in enumerate((tri, ones)):
                    mm = pe.matmul(bank(7)[:, 272 + r * G * E:272 + (r + 1) * G * E], rows_of[:, :],
                                   hot.rearrange("p v e -> p (v e)"), start=True, stop=True)
                mm.then_inc(s("d_cnt"), 1)

            def counts_taken(b, t):
                pe.wait_ge(s("d_taken"), group(b, t))

            def c2_pe(b, t, tile, route, first, last):
                if t > 0:
                    tile(c2_sim, 0)
                tile(c2_lg, 5)
                route(c2_counts, 1)
                if t == 1:
                    tile(c2_y, 2)
                    tile(c2_conv, 1)
                else:
                    tile(c2_conv, 1)
                    if t == 0:
                        tile(c2_g1, 0)
                    tile(c2_y, 2)
                route(counts_taken, 1)
                tile(c2_tp, 4)
                if t == 0:
                    tile(c2_first_sim, 0)

            c2_batches(pe, c2_pe, CT)
            pe.wait_ge(s("wgu_in"), 16 * KD)
            pe.wait_ge(s("wd_in"), 32)
            pe.wait_ge(s("d_tab"), 1)

            def expert(n):
                return pe.value_load(t_eid[0:1, bass.ds(n, 1)].bitcast(I32), min_val=0, max_val=E - 1)

            def x_columns(i, n, v, free):
                pe.wait_ge(s(f"m_xs_in{v}"), 16 * (i + 1))
                if not free:
                    pe.wait_ge(s("m_xst"), n)
                for k in range(KD):
                    mm = pe.transpose(bank(6)[:, k * P:(k + 1) * P], xs[:, v, k * P:(k + 1) * P], idt)
                mm.then_inc(s("m_xtp"), 1)

            def hidden(c, e, u):
                for k in range(KD):
                    mm = pe.matmul(bank(2 * c + u), xst[:, u, k], w_gu_s[:, e, k, c], start=(k == 0), stop=(k == KD - 1))
                mm.then_inc(s(("m_gate", "m_up")[c]), 1)

            def h_columns(n, u, free):
                pe.wait_ge(s("m_hid"), n + 1)
                if not free:
                    pe.wait_ge(s("m_ht"), n)
                for f in range(4):
                    mm = pe.transpose(bank(4)[:, f * P:(f + 1) * P], hid[:, u, f * P:(f + 1) * P], idt)
                mm.then_inc(s("m_htp"), 1)

            def down(e, n, u, free):
                pe.wait_ge(s("m_ht"), n + 1)
                if not free:
                    pe.wait_ge(s("m_y"), n)
                for f in range(4):
                    mm = pe.matmul(bank(5)[:, 0:D], hidt[:, u, f], w_d_s[:, e, f], start=(f == 0), stop=(f == 3))
                mm.then_inc(s("m_down"), 1)

            def expert_tiles(i, first, last):
                for v in range(4):
                    n, u = 4 * i + v, v % 2
                    e = expert(n)
                    pe.wait_ge(s("m_xst"), n + 1)
                    if not (first and v < 2):
                        pe.wait_ge(s("m_hid"), n - 1)
                    hidden(0, e, u)
                    if v < 3:
                        x_columns(i, n + 1, v + 1, False)
                    elif not last:
                        x_columns(i + 1, n + 1, 0, False)
                    if not (first and v == 0):
                        h_columns(n - 1, 1 - u, first and v == 1)
                    hidden(1, e, u)
                    if not (first and v == 0):
                        down(expert(n - 1), n - 1, 1 - u, first and v == 1)

            x_columns(0, 0, 0, True)
            expert_tiles(0, True, False)
            with pe.Fori(1, NTILE // 4 - 1) as i:
                expert_tiles(i, False, False)
            expert_tiles(NTILE // 4 - 1, False, True)
            h_columns(NTILE - 1, 1, False)
            down(expert(NTILE - 1), NTILE - 1, 1, False)


_OUT = (B, N, D)


def kernel(**inputs):
    import numpy as np
    import concourse.bacc as bacc
    from concourse.bass_utils import run_bass_kernel_spmd as run

    f = {k: np.asarray(v) for k, v in inputs.items()}
    wqkv = f["L0_attn_w_qkv"]
    taps = f["L0_attn_w_conv"].reshape(H, TAPS)
    band = np.zeros((H, P, TO), taps.dtype)
    for o in range(TO):
        band[:, o:o + TAPS, o] = taps
    gate_t = f["L0_ffn_w_gate"].transpose(0, 2, 1).reshape(E, KD, P, F)
    up_t = f["L0_ffn_w_up"].transpose(0, 2, 1).reshape(E, KD, P, F)
    arrays = {
        "x": f["L0_attn_x"],
        "w_qkv": wqkv,
        "wq_t": wqkv[:, 0:INNER].T,
        "wk_t": wqkv[:, INNER:2 * INNER].T,
        "conv_band": band,
        "w_fc": f["L0_attn_w_fc"],
        "b_fc": f["L0_attn_b_fc"],
        "router_t": f["L0_ffn_router_w"].T,
        "w_gu": np.stack([gate_t, up_t], axis=3),
        "w_down": f["L0_ffn_w_down"].transpose(0, 2, 1).reshape(E, 4, P, D).transpose(0, 2, 1, 3),
    }
    nc = bacc.Bacc("TRN2", target_bir_lowering=False, num_devices=1)
    args = []
    for name in list(arrays):
        arrays[name] = np.ascontiguousarray(arrays[name])
        args.append(nc.dram_tensor(name, arrays[name].shape, mybir.dt.from_np(arrays[name].dtype), kind="ExternalInput").ap())
    args.append(nc.dram_tensor("out", _OUT, F32, kind="ExternalOutput").ap())
    layer(nc, *args)
    r = run(nc, [arrays], core_ids=[0])
    return r.results[0]["out"]
```
